# Optimizing a Trainium2 kernel written in Bass

```python
import numpy as np
import jax
import jax.numpy as jnp

def _softmax(x, axis=-1):
    return jax.nn.softmax(x, axis=axis)

def _gelu(x):
    return jax.nn.gelu(x, approximate=True)

def _silu(x):
    return jax.nn.silu(x)

def _sigmoid(x):
    return jax.nn.sigmoid(x)

def _layernorm(x, axis=-1, eps=1e-05):
    m = jnp.mean(x, axis=axis, keepdims=True)
    v = jnp.var(x, axis=axis, keepdims=True)
    return (x - m) / jnp.sqrt(v + eps)

def _scatter_add(tgt, idx, src, axis=0):
    return tgt.at[idx].add(src)

def _segment_sum(src, seg, n):
    return jax.ops.segment_sum(src, seg, n)
kernel_name = 'mk_macaron_d2_jaxref_r8_aa4cba'

def setup_inputs(seed: int=0):
    np.random.seed(seed)
    _w = jnp.asarray

    def _L0_attn_setup():
        import jax, jax.numpy as jnp
        import numpy as np
        HIDDEN = 256
        NUM_HEAD = 32
        GROUP = 8
        HEAD_DIM = HIDDEN // NUM_HEAD
        REP = NUM_HEAD // GROUP
        key = jax.random.key(seed)
        ks = jax.random.split(key, 9)
        s = 0.02
        kv_dim = GROUP * HEAD_DIM
        return {'hidden_states': jax.random.normal(ks[0], (2, 256, HIDDEN), dtype=jnp.float32), 'Wq': jax.random.normal(ks[1], (HIDDEN, HIDDEN), dtype=jnp.float32) * s, 'bq': jnp.zeros((HIDDEN,), dtype=jnp.float32), 'Wk': jax.random.normal(ks[2], (HIDDEN, kv_dim), dtype=jnp.float32) * s, 'bk': jnp.zeros((kv_dim,), dtype=jnp.float32), 'Wv': jax.random.normal(ks[3], (HIDDEN, kv_dim), dtype=jnp.float32) * s, 'bv': jnp.zeros((kv_dim,), dtype=jnp.float32), 'Wo': jax.random.normal(ks[4], (HIDDEN, HIDDEN), dtype=jnp.float32) * s, 'bo': jnp.zeros((HIDDEN,), dtype=jnp.float32)}
    _L0_attn_in = _L0_attn_setup()

    def _L0_ffn_setup():
        import jax, jax.numpy as jnp
        import numpy as np
        EPS = 1e-05
        ROPE_BASE = 150000.0
        NHEADS = 32
        KVHEADS = 8
        HEAD_DIM = 64
        TOP_K = 4

        def _rms(x, w):
            return x * jax.lax.rsqrt(jnp.mean(x * x, -1, keepdims=True) + EPS) * w

        def _rope(q, k):
            S, hd = (q.shape[1], q.shape[-1])
            half = hd // 2
            inv = 1.0 / ROPE_BASE ** (jnp.arange(half, dtype=jnp.float32) / half)
            ang = jnp.arange(S, dtype=jnp.float32)[:, None] * inv
            cos = jnp.concatenate([jnp.cos(ang), jnp.cos(ang)], -1)[None, :, None, :]
            sin = jnp.concatenate([jnp.sin(ang), jnp.sin(ang)], -1)[None, :, None, :]

            def rot(t):
                t1, t2 = (t[..., :half], t[..., half:])
                return jnp.concatenate([-t2, t1], -1)
            return (q * cos + rot(q) * sin, k * cos + rot(k) * sin)
        key = jax.random.key(seed)
        ks = jax.random.split(key, 12)
        B, S, D, H, E = (1, 128, 256, 256, 16)
        s = 0.02
        return {'x': jax.random.normal(ks[0], (B, S, D), jnp.float32), 'ln_w': jnp.ones((D,), jnp.float32), 'ff_ln_w': jnp.ones((D,), jnp.float32), 'wq': jax.random.normal(ks[1], (D, NHEADS * HEAD_DIM), jnp.float32) * s, 'wk': jax.random.normal(ks[2], (D, KVHEADS * HEAD_DIM), jnp.float32) * s, 'wv': jax.random.normal(ks[3], (D, KVHEADS * HEAD_DIM), jnp.float32) * s, 'wo': jax.random.normal(ks[4], (NHEADS * HEAD_DIM, D), jnp.float32) * s, 'wg': jax.random.normal(ks[5], (D, E), jnp.float32) * s, 'w1': jax.random.normal(ks[6], (E, D, H), jnp.float32) * s, 'w3': jax.random.normal(ks[7], (E, D, H), jnp.float32) * s, 'w2': jax.random.normal(ks[8], (E, H, D), jnp.float32) * s}
    _L0_ffn_in = _L0_ffn_setup()

    def _L1_attn_setup():
        import jax, jax.numpy as jnp
        import numpy as np
        B, T, C = (1, 512, 256)
        H, HK, D = (16, 4, 128)
        W = 128
        THETA = 10000.0

        def sine_table(features, length, max_timescale):
            fraction = jnp.arange(0, features, 2, dtype=jnp.float32) / features
            timescale = max_timescale ** fraction
            ang = jnp.arange(length, dtype=jnp.float32)[:, None] / timescale[None, :]
            ang = jnp.concatenate([ang, ang], axis=-1)
            return (jnp.sin(ang), jnp.cos(ang))

        def rotate_half(x):
            x1, x2 = jnp.split(x, 2, axis=-1)
            return jnp.concatenate([-x2, x1], axis=-1)

        def apply_rope(u, sin, cos):
            return u * cos[None, :, None, :] + rotate_half(u) * sin[None, :, None, :]
        key = jax.random.key(seed)
        ks = jax.random.split(key, 5)
        std = 0.02
        return {'x': jax.random.normal(ks[0], (B, T, C), jnp.float32), 'q_kernel': jax.random.normal(ks[1], (C, H * D), jnp.float32) * std, 'k_kernel': jax.random.normal(ks[2], (C, HK * D), jnp.float32) * std, 'v_kernel': jax.random.normal(ks[3], (C, HK * D), jnp.float32) * std, 'out_kernel': jax.random.normal(ks[4], (H * D, C), jnp.float32) * std}
    _L1_attn_in = _L1_attn_setup()

    def _L1_ffn_setup():
        import jax, jax.numpy as jnp
        import numpy as np
        EPS = 1e-06
        K_STEPS = 4
        USE_GATING = True

        def layer_norm(x, gamma, beta):
            mu = jnp.mean(x, axis=-1, keepdims=True)
            var = jnp.mean(jnp.square(x - mu), axis=-1, keepdims=True)
            return (x - mu) * jax.lax.rsqrt(var + EPS) * gamma + beta
        key = jax.random.key(seed)
        B, L, D, H = (4, 512, 256, 1024)
        ks = jax.random.split(key, 16)
        s = 0.02
        return {'x': jax.random.normal(ks[0], (B, L, D), dtype=jnp.float32), 'in_gamma': jnp.ones((D,), jnp.float32), 'in_beta': jnp.zeros((D,), jnp.float32), 'agg_w': jax.random.normal(ks[1], (D, D), jnp.float32) * s, 'agg_b': jnp.zeros((D,), jnp.float32), 'pn_gamma': jnp.ones((D,), jnp.float32), 'pn_beta': jnp.zeros((D,), jnp.float32), 'd1_w': jax.random.normal(ks[2], (D, H), jnp.float32) * s, 'd1_b': jnp.zeros((H,), jnp.float32), 'd2_w': jax.random.normal(ks[3], (H, D), jnp.float32) * s, 'd2_b': jnp.zeros((D,), jnp.float32), 'bc_w': jax.random.normal(ks[4], (D, D), jnp.float32) * s, 'bc_b': jnp.zeros((D,), jnp.float32), 'gate_w': jax.random.normal(ks[5], (D, D), jnp.float32) * s, 'gate_b': jnp.zeros((D,), jnp.float32), 'out_gamma': jnp.ones((D,), jnp.float32), 'out_beta': jnp.zeros((D,), jnp.float32)}
    _L1_ffn_in = _L1_ffn_setup()
    _d = {'L0_attn_hidden_states': _L0_attn_in['hidden_states'], 'L0_attn_Wq': _L0_attn_in['Wq'], 'L0_attn_bq': _L0_attn_in['bq'], 'L0_attn_Wk': _L0_attn_in['Wk'], 'L0_attn_bk': _L0_attn_in['bk'], 'L0_attn_Wv': _L0_attn_in['Wv'], 'L0_attn_bv': _L0_attn_in['bv'], 'L0_attn_Wo': _L0_attn_in['Wo'], 'L0_attn_bo': _L0_attn_in['bo'], 'L0_ffn_ln_w': _L0_ffn_in['ln_w'], 'L0_ffn_ff_ln_w': _L0_ffn_in['ff_ln_w'], 'L0_ffn_wq': _L0_ffn_in['wq'], 'L0_ffn_wk': _L0_ffn_in['wk'], 'L0_ffn_wv': _L0_ffn_in['wv'], 'L0_ffn_wo': _L0_ffn_in['wo'], 'L0_ffn_wg': _L0_ffn_in['wg'], 'L0_ffn_w1': _L0_ffn_in['w1'], 'L0_ffn_w3': _L0_ffn_in['w3'], 'L0_ffn_w2': _L0_ffn_in['w2'], 'L1_attn_q_kernel': _L1_attn_in['q_kernel'], 'L1_attn_k_kernel': _L1_attn_in['k_kernel'], 'L1_attn_v_kernel': _L1_attn_in['v_kernel'], 'L1_attn_out_kernel': _L1_attn_in['out_kernel'], 'L1_ffn_in_gamma': _L1_ffn_in['in_gamma'], 'L1_ffn_in_beta': _L1_ffn_in['in_beta'], 'L1_ffn_agg_w': _L1_ffn_in['agg_w'], 'L1_ffn_agg_b': _L1_ffn_in['agg_b'], 'L1_ffn_pn_gamma': _L1_ffn_in['pn_gamma'], 'L1_ffn_pn_beta': _L1_ffn_in['pn_beta'], 'L1_ffn_d1_w': _L1_ffn_in['d1_w'], 'L1_ffn_d1_b': _L1_ffn_in['d1_b'], 'L1_ffn_d2_w': _L1_ffn_in['d2_w'], 'L1_ffn_d2_b': _L1_ffn_in['d2_b'], 'L1_ffn_bc_w': _L1_ffn_in['bc_w'], 'L1_ffn_bc_b': _L1_ffn_in['bc_b'], 'L1_ffn_gate_w': _L1_ffn_in['gate_w'], 'L1_ffn_gate_b': _L1_ffn_in['gate_b'], 'L1_ffn_out_gamma': _L1_ffn_in['out_gamma'], 'L1_ffn_out_beta': _L1_ffn_in['out_beta']}
    _x0 = _d['L0_attn_hidden_states']
    _d['L0_attn_hidden_states'] = jax.random.normal(jax.random.fold_in(jax.random.key(seed), 1), (4, 512, 256), dtype=_x0.dtype)
    del _x0
    return _d

def reference(L0_attn_hidden_states, L0_attn_Wq, L0_attn_bq, L0_attn_Wk, L0_attn_bk, L0_attn_Wv, L0_attn_bv, L0_attn_Wo, L0_attn_bo, L0_ffn_ln_w, L0_ffn_ff_ln_w, L0_ffn_wq, L0_ffn_wk, L0_ffn_wv, L0_ffn_wo, L0_ffn_wg, L0_ffn_w1, L0_ffn_w3, L0_ffn_w2, L1_attn_q_kernel, L1_attn_k_kernel, L1_attn_v_kernel, L1_attn_out_kernel, L1_ffn_in_gamma, L1_ffn_in_beta, L1_ffn_agg_w, L1_ffn_agg_b, L1_ffn_pn_gamma, L1_ffn_pn_beta, L1_ffn_d1_w, L1_ffn_d1_b, L1_ffn_d2_w, L1_ffn_d2_b, L1_ffn_bc_w, L1_ffn_bc_b, L1_ffn_gate_w, L1_ffn_gate_b, L1_ffn_out_gamma, L1_ffn_out_beta):

    def _L0_attn_ref(hidden_states, Wq, bq, Wk, bk, Wv, bv, Wo, bo):
        import jax, jax.numpy as jnp
        import numpy as np
        HIDDEN = 256
        NUM_HEAD = 32
        GROUP = 8
        HEAD_DIM = HIDDEN // NUM_HEAD
        REP = NUM_HEAD // GROUP
        B, S, H = hidden_states.shape
        q = hidden_states @ Wq + bq
        k = hidden_states @ Wk + bk
        v = hidden_states @ Wv + bv
        q = q.reshape(B, S, NUM_HEAD, HEAD_DIM).transpose(0, 2, 1, 3)
        k = k.reshape(B, S, GROUP, HEAD_DIM).transpose(0, 2, 1, 3)
        v = v.reshape(B, S, GROUP, HEAD_DIM).transpose(0, 2, 1, 3)
        k = jnp.repeat(k, REP, axis=1)
        v = jnp.repeat(v, REP, axis=1)
        scale = 1.0 / jnp.sqrt(jnp.float32(HEAD_DIM))
        scores = jnp.einsum('bhqd,bhkd->bhqk', q, k) * scale
        attn = jax.nn.softmax(scores, axis=-1)
        out = jnp.einsum('bhqk,bhkd->bhqd', attn, v)
        out = out.transpose(0, 2, 1, 3).reshape(B, S, NUM_HEAD * HEAD_DIM)
        return out @ Wo + bo

    def _L0_ffn_ref(x, ln_w, ff_ln_w, wq, wk, wv, wo, wg, w1, w3, w2):
        import jax, jax.numpy as jnp
        import numpy as np
        EPS = 1e-05
        ROPE_BASE = 150000.0
        NHEADS = 32
        KVHEADS = 8
        HEAD_DIM = 64
        TOP_K = 4

        def _rms(x, w):
            return x * jax.lax.rsqrt(jnp.mean(x * x, -1, keepdims=True) + EPS) * w

        def _rope(q, k):
            S, hd = (q.shape[1], q.shape[-1])
            half = hd // 2
            inv = 1.0 / ROPE_BASE ** (jnp.arange(half, dtype=jnp.float32) / half)
            ang = jnp.arange(S, dtype=jnp.float32)[:, None] * inv
            cos = jnp.concatenate([jnp.cos(ang), jnp.cos(ang)], -1)[None, :, None, :]
            sin = jnp.concatenate([jnp.sin(ang), jnp.sin(ang)], -1)[None, :, None, :]

            def rot(t):
                t1, t2 = (t[..., :half], t[..., half:])
                return jnp.concatenate([-t2, t1], -1)
            return (q * cos + rot(q) * sin, k * cos + rot(k) * sin)
        B, S, D = x.shape
        h = _rms(x, ln_w)
        q = (h @ wq).reshape(B, S, NHEADS, HEAD_DIM)
        k = (h @ wk).reshape(B, S, KVHEADS, HEAD_DIM)
        v = (h @ wv).reshape(B, S, KVHEADS, HEAD_DIM)
        q, k = _rope(q, k)
        g = NHEADS // KVHEADS
        k = jnp.repeat(k, g, axis=2)
        v = jnp.repeat(v, g, axis=2)
        scores = jnp.einsum('bqhd,bkhd->bhqk', q, k) / np.float32(np.sqrt(HEAD_DIM))
        causal = jnp.tril(jnp.ones((S, S), bool))
        scores = jnp.where(causal[None, None], scores, jnp.float32(-1e+30))
        attn = jax.nn.softmax(scores, -1)
        o = jnp.einsum('bhqk,bkhd->bqhd', attn, v).reshape(B, S, NHEADS * HEAD_DIM)
        x = x + o @ wo
        h = _rms(x, ff_ln_w)
        logits = h @ wg
        topv, topi = jax.lax.top_k(logits, TOP_K)
        gate = jax.nn.softmax(topv, -1)
        bidx = jnp.arange(B)[:, None, None]
        sidx = jnp.arange(S)[None, :, None]
        weights = jnp.zeros_like(logits).at[bidx, sidx, topi].set(gate)
        a = jax.nn.silu(jnp.einsum('bsd,edh->bseh', h, w1)) * jnp.einsum('bsd,edh->bseh', h, w3)
        y = jnp.einsum('bseh,ehd->bsed', a, w2)
        moe = jnp.einsum('bsed,bse->bsd', y, weights)
        return x + moe

    def _L1_attn_ref(x, q_kernel, k_kernel, v_kernel, out_kernel):
        import jax, jax.numpy as jnp
        import numpy as np
        B, T, C = (1, 512, 256)
        H, HK, D = (16, 4, 128)
        W = 128
        THETA = 10000.0

        def sine_table(features, length, max_timescale):
            fraction = jnp.arange(0, features, 2, dtype=jnp.float32) / features
            timescale = max_timescale ** fraction
            ang = jnp.arange(length, dtype=jnp.float32)[:, None] / timescale[None, :]
            ang = jnp.concatenate([ang, ang], axis=-1)
            return (jnp.sin(ang), jnp.cos(ang))

        def rotate_half(x):
            x1, x2 = jnp.split(x, 2, axis=-1)
            return jnp.concatenate([-x2, x1], axis=-1)

        def apply_rope(u, sin, cos):
            return u * cos[None, :, None, :] + rotate_half(u) * sin[None, :, None, :]
        b, t, c = x.shape
        q = jnp.dot(x, q_kernel).reshape(b, t, H, D)
        k = jnp.dot(x, k_kernel).reshape(b, t, HK, D)
        v = jnp.dot(x, v_kernel).reshape(b, t, HK, D)
        sin, cos = sine_table(D, t, THETA)
        q = apply_rope(q, sin, cos)
        k = apply_rope(k, sin, cos)
        rep = H // HK
        k = jnp.repeat(k, rep, axis=2)
        v = jnp.repeat(v, rep, axis=2)
        nb = t // W
        qb = q.reshape(b, nb, W, H, D)
        kb = k.reshape(b, nb, W, H, D)
        vb = v.reshape(b, nb, W, H, D)
        pad = ((0, 0), (1, 0), (0, 0), (0, 0), (0, 0))
        kp = jnp.pad(kb, pad)
        vp = jnp.pad(vb, pad)
        kw = jnp.concatenate([kp[:, :-1], kp[:, 1:]], axis=2)
        vw = jnp.concatenate([vp[:, :-1], vp[:, 1:]], axis=2)
        scale = 1.0 / np.sqrt(D)
        scores = jnp.einsum('bnqhd,bnkhd->bnhqk', qb, kw).astype(jnp.float32) * scale
        p = jnp.arange(W)[:, None]
        j = jnp.arange(2 * W)[None, :]
        base = (j >= p) & (j <= p + W)
        blk = jnp.arange(nb)[:, None, None]
        mask = base[None] & ((blk > 0) | (j[None] >= W))
        scores = jnp.where(mask[None, :, None], scores, jnp.float32(-1e+30))
        probs = jax.nn.softmax(scores, axis=-1).astype(v.dtype)
        ob = jnp.einsum('bnhqk,bnkhd->bnqhd', probs, vw)
        out = ob.reshape(b, t, H * D)
        return jnp.dot(out, out_kernel)

    def _L1_ffn_ref(x, in_gamma, in_beta, agg_w, agg_b, pn_gamma, pn_beta, d1_w, d1_b, d2_w, d2_b, bc_w, bc_b, gate_w, gate_b, out_gamma, out_beta):
        import jax, jax.numpy as jnp
        import numpy as np
        EPS = 1e-06
        K_STEPS = 4
        USE_GATING = True

        def layer_norm(x, gamma, beta):
            mu = jnp.mean(x, axis=-1, keepdims=True)
            var = jnp.mean(jnp.square(x - mu), axis=-1, keepdims=True)
            return (x - mu) * jax.lax.rsqrt(var + EPS) * gamma + beta
        x_norm = layer_norm(x, in_gamma, in_beta)
        thought = x_norm[:, -1, :] @ agg_w + agg_b
        for _ in range(K_STEPS):
            t = layer_norm(thought, pn_gamma, pn_beta)
            t = jax.nn.gelu(t @ d1_w + d1_b, approximate=False)
            thought = thought + (t @ d2_w + d2_b)
        broadcast = (thought @ bc_w + bc_b)[:, None, :]
        if USE_GATING:
            gate = jax.nn.sigmoid(x @ gate_w + gate_b)
            out = x + gate * broadcast
        else:
            out = x + broadcast
        return layer_norm(out, out_gamma, out_beta)
    x = L0_attn_hidden_states
    x = x + 0.5 * _L0_ffn_ref(_layernorm(x, axis=-1), L0_ffn_ln_w, L0_ffn_ff_ln_w, L0_ffn_wq, L0_ffn_wk, L0_ffn_wv, L0_ffn_wo, L0_ffn_wg, L0_ffn_w1, L0_ffn_w3, L0_ffn_w2)
    x = x + _L0_attn_ref(_layernorm(x, axis=-1), L0_attn_Wq, L0_attn_bq, L0_attn_Wk, L0_attn_bk, L0_attn_Wv, L0_attn_bv, L0_attn_Wo, L0_attn_bo)
    x = x + 0.5 * _L0_ffn_ref(_layernorm(x, axis=-1), L0_ffn_ln_w, L0_ffn_ff_ln_w, L0_ffn_wq, L0_ffn_wk, L0_ffn_wv, L0_ffn_wo, L0_ffn_wg, L0_ffn_w1, L0_ffn_w3, L0_ffn_w2)
    x = x + 0.5 * _L1_ffn_ref(_layernorm(x, axis=-1), L1_ffn_in_gamma, L1_ffn_in_beta, L1_ffn_agg_w, L1_ffn_agg_b, L1_ffn_pn_gamma, L1_ffn_pn_beta, L1_ffn_d1_w, L1_ffn_d1_b, L1_ffn_d2_w, L1_ffn_d2_b, L1_ffn_bc_w, L1_ffn_bc_b, L1_ffn_gate_w, L1_ffn_gate_b, L1_ffn_out_gamma, L1_ffn_out_beta)
    x = x + _L1_attn_ref(_layernorm(x, axis=-1), L1_attn_q_kernel, L1_attn_k_kernel, L1_attn_v_kernel, L1_attn_out_kernel)
    x = x + 0.5 * _L1_ffn_ref(_layernorm(x, axis=-1), L1_ffn_in_gamma, L1_ffn_in_beta, L1_ffn_agg_w, L1_ffn_agg_b, L1_ffn_pn_gamma, L1_ffn_pn_beta, L1_ffn_d1_w, L1_ffn_d1_b, L1_ffn_d2_w, L1_ffn_d2_b, L1_ffn_bc_w, L1_ffn_bc_b, L1_ffn_gate_w, L1_ffn_gate_b, L1_ffn_out_gamma, L1_ffn_out_beta)
    return x

_drawn_inputs = setup_inputs


def setup_inputs(seed=0):
    import zlib

    import numpy as np

    out = dict(_drawn_inputs(seed))
    spreads = {'L0_attn_bq': (0.0, 0.8),
     'L0_attn_bk': (0.0, 2.0),
     'L0_attn_bv': (0.0, 0.42),
     'L0_attn_bo': (0.0, 0.1),
     'L0_ffn_ln_w': (1.0, 0.6),
     'L0_ffn_ff_ln_w': (1.0, 0.6),
     'L1_ffn_in_gamma': (1.0, 0.6),
     'L1_ffn_in_beta': (0.0, 2.0),
     'L1_ffn_agg_b': (0.0, 2.0),
     'L1_ffn_pn_gamma': (1.0, 0.6),
     'L1_ffn_pn_beta': (0.0, 2.0),
     'L1_ffn_d1_b': (0.0, 2.0),
     'L1_ffn_d2_b': (0.0, 1.157),
     'L1_ffn_bc_b': (0.0, 1.64),
     'L1_ffn_gate_b': (0.0, 2.0),
     'L1_ffn_out_gamma': (1.0, 0.6),
     'L1_ffn_out_beta': (0.0, 0.8)}
    factors = {'L0_attn_Wq': 8.0,
     'L0_attn_Wk': 8.0,
     'L0_attn_Wv': 8.0,
     'L0_attn_Wo': 2.902,
     'L0_ffn_wq': 8.0,
     'L0_ffn_wk': 8.0,
     'L0_ffn_wv': 2.794,
     'L0_ffn_wo': 2.817,
     'L0_ffn_wg': 8.0,
     'L0_ffn_w1': 8.0,
     'L0_ffn_w3': 8.0,
     'L0_ffn_w2': 8.0,
     'L1_attn_q_kernel': 8.0,
     'L1_attn_k_kernel': 8.0,
     'L1_attn_v_kernel': 3.31,
     'L1_attn_out_kernel': 3.228,
     'L1_ffn_gate_w': 7.756,
     'L1_ffn_agg_w': 5.738,
     'L1_ffn_d1_w': 4.208}
    for name, (base, spread) in spreads.items():
        noise = np.random.default_rng([zlib.crc32(name.encode()), seed]).standard_normal(out[name].shape)
        drawn = base * np.exp(spread * noise) if base else spread * noise
        out[name] = jnp.asarray(drawn.astype(out[name].dtype))
    for name, factor in factors.items():
        out[name] = (out[name] * factor).astype(out[name].dtype)
    return out
```

```python
import numpy as np
import concourse.bass as bass
from concourse import mybir
from contextlib import ExitStack

P = 128
B, S, D = 4, 512, 256
T = S // P
NT = B * T
KC = D // P
E, TOPK, H = 16, 4, 256
HC = H // P
KV = 4
NEG = -1e30
LN_EPS, RMS_EPS, FFN_EPS = 1e-5, 1e-5, 1e-6
BANK = 512
NU = 4
QW = 512
KW = 128
SH, SKV, SD = 32, 8, 8
PARTS = 3
SENT = (-3.0e38, -3.1e38, -3.2e38, -3.3e38)


class Lane:

    def __init__(self, name, sem):
        self.name, self.sem, self.done, self.queue, self.seen = name, sem, 0, [], {}
        self.one_by_one = name == "pool"

    def waits(self, after):
        need = {}
        stack = list(after)
        while stack:
            t = stack.pop()
            if t is None:
                continue
            if isinstance(t, list):
                stack.extend(t)
            elif t[1] > max(need.get(t[0], (0, 0))[1], self.seen.get(t[0], 0)):
                need[t[0]] = t
        for k, t in need.items():
            self.seen[k] = t[1]
        return list(need.values())

    def do(self, emit, *after, signal=True):
        if self.one_by_one and self.done:
            after = (*after, self.last())
        self.queue.append((self.waits(after), emit, self.sem if signal else None, 1))
        if signal:
            self.done += 1
            return (self.sem, self.done)
        return None

    def fence(self, *after):
        self.queue.append((self.waits(after), None, None, 0))

    def last(self):
        return (self.sem, self.done)

    def play(self, eng):
        for waits, emit, sem, n in self.queue:
            for s, v in waits:
                eng.wait_ge(s, v)
            if emit is not None:
                ins = emit(eng)
                if sem is not None:
                    ins.then_inc(sem, n)


class Flag:

    def __init__(self, sem):
        self.sem, self.n = sem, 0

    def dma(self, lane, out, in_, *after, by_element=False):
        lane.queue.append((lane.waits(after), lambda e: e.dma_start(out, in_, allow_slow_non_contiguous=by_element),
                           self.sem, 16))
        self.n += 16
        return (self.sem, self.n)


class Slot:
    def __init__(self, ap, after, flag=None):
        self.ap, self.after, self.flag, self.users = ap, after, flag, None

    def free(self, *tokens):
        self.users = (self.users or []) + list(tokens)


class Ring:

    def __init__(self, aps, flags=None):
        self.slots, self.n = [Slot(a, [], f) for a, f in zip(aps, flags or [None] * len(aps))], 0
        for s in self.slots:
            s.users = []

    def take(self):
        i = self.n % len(self.slots)
        old = self.slots[i]
        assert old.users is not None, "a buffer is taken before its last use is queued"
        self.slots[i] = Slot(old.ap, old.users, old.flag)
        self.n += 1
        return self.slots[i]


def build(nc, io, out, phases=8):
    F32, F32R, BF16 = mybir.dt.float32, mybir.dt.float32r, mybir.dt.bfloat16
    ALU, ACT, AX = mybir.AluOpType, mybir.ActivationFunctionType, mybir.AxisListType
    ctx = ExitStack()

    def sem(name):
        return ctx.enter_context(nc.semaphore(name))

    pe, act, dve, pool, sp = (Lane(n, sem(n + "_done")) for n in ("pe", "act", "dve", "pool", "sp"))
    lanes = (pe, act, dve, pool)
    banks = [ctx.enter_context(nc.psum_tensor(f"bank{i}", [P, BANK], F32)) for i in range(8)]

    def allocator(stack, prefix):
        def sb(name, shape, dt=F32):
            return stack.enter_context(nc.sbuf_tensor(f"{prefix}_{name}", shape, dt))
        return sb

    top = allocator(ctx, "g")

    res = top("res", [P, NT, D])
    ident = top("ident", [P, P])
    identb = top("identb", [P, P], BF16)
    half = top("minus_half", [P, NT])
    STAGE_W = 1536
    stage_mem = [top(f"stage{i}", [P, STAGE_W]) for i in range(2)]
    stage = Ring([m[:, :] for m in stage_mem], [Flag(sem(f"stage{i}")) for i in range(2)])
    res_saved = nc.dram_tensor("res_saved", (NT, P, D), F32, kind="Internal").ap()
    parts_saved = nc.dram_tensor("parts_saved", (2, PARTS, D + SKV * SD, S), BF16, kind="Internal").ap()

    def make_ident(m):
        z = pool.do(lambda e: e.memset(m[:, :], 0.0))
        return pool.do(lambda e: e.affine_select(out=m[:, :], in_=m[:, :], compare_op=ALU.not_equal, fill=1.0,
                                                 base=0, pattern=[[-1, P]], channel_multiplier=1), z)
    ident_made = [make_ident(ident), make_ident(identb)]
    half_made = pool.do(lambda e: e.memset(half[:, :], -0.5))
    res_flag = Flag(sem("res_load"))
    loaded = None
    x_tiles = io["L0_attn_hidden_states"].rearrange("b (t p) d -> (b t) p d", p=P)
    for b in range(B):
        bt = slice(b * T, b * T + T)
        loaded = res_flag.dma(sp, res[:, bt, :], x_tiles[bt].rearrange("t p d -> p t d"))
    res_ready = [loaded for _ in range(NT)]
    res_read = [[] for _ in range(NT)]
    pe.fence(ident_made)

    def fetch(pieces):
        slot = stage.take()
        for rows, view, src in pieces:
            slot.token = slot.flag.dma(sp, view(slot.ap[rows, :]), src, slot.after)
        return slot

    def split(slot, width, hi, lo, *after):
        raw = slot.ap[:, 0:width]
        h = act.do(lambda e: e.activation(hi, raw, ACT.Copy), slot.token, *after)
        l = pool.do(lambda e: e.tensor_tensor(lo, raw, hi.bitcast(F32), ALU.subtract), h, *after)
        slot.free(h, l)
        return [h, l]

    def chunks(src):
        return src.rearrange("(c p) n -> p c n", p=P)

    def into(c0, cols, width):
        return lambda a: a[:, 0:KC * width].rearrange("p (c n) -> p c n", c=KC)[:, :, c0:c0 + cols]

    def product(out_ap, pairs, *after):
        tok = None
        for n, (l, r) in enumerate(pairs):
            last = n == len(pairs) - 1
            tok = pe.do(lambda e, l=l, r=r, n=n, last=last: e.matmul(out_ap, l, r, start=(n == 0), stop=last),
                        *(after if n == 0 else ()), signal=last)
        return tok

    def three(lh, ll, rh, rl):
        return [(lh, rh), (ll, rh), (lh, rl)]

    def transpose(out_ap, in_ap, n, *after, signal=True):
        return pe.do(lambda e: e.transpose(out_ap, in_ap, ident[0:n, 0:n]), *after, signal=signal)

    class Norm:

        def __init__(self, sb, name, parts=P, tiles=T):
            self.p, self.n = parts, tiles
            self.st = sb(name + "_st", [parts, tiles, 6])
            self.mv = sb(name + "_mv", [parts, tiles, 2])
            self.ve = sb(name + "_ve", [parts, tiles])
            self.rs = sb(name + "_rs", [parts, tiles])
            self.read = []

        def run(self, tiles, eps, ready):
            agg = []
            for i, x in enumerate(tiles):
                s = dve.do(lambda e, i=i, x=x: e.bn_stats(self.st[:, i, :], x), ready[i], *self.read)
                agg.append((i, s))
            done = [dve.do(lambda e, i=i: e.bn_aggr(self.mv[:, i, :], self.st[:, i, :]), s) for i, s in agg]
            v = dve.do(lambda e: e.tensor_scalar(self.ve[:, :], self.mv[:, :, 1], eps, None, ALU.add), done)
            r = pool.do(lambda e: e.tensor_tensor(self.rs[:, :], self.ve[:, :], half[0:self.p, 0:self.n], ALU.pow), v,
                        half_made)
            self.read = [v]
            return r

    def feature_major(src, ready, ring, hi, lo, scale, slots, *after):
        toks, reads = [], []
        for c in range(KC):
            bank = ring.take()
            for t in range(T):
                tt = transpose(bank.ap[:, t * P:(t + 1) * P], src(t)[:, c * P:(c + 1) * P], P,
                               ready[t], bank.after, signal=t == T - 1)
            reads.append(tt)
            sc = scale[:, c:c + 1] if scale is not None else 1.0
            h = act.do(lambda e, c=c, bank=bank, sc=sc: e.activation(hi[:, c, :], bank.ap, ACT.Copy, scale=sc), tt, *after)
            l = dve.do(lambda e, c=c, bank=bank, sc=sc: e.scalar_tensor_tensor(
                lo[:, c, :], bank.ap, sc, hi[:, c, :].bitcast(F32), ALU.mult, ALU.subtract), h, *after)
            bank.free(h, l)
            toks += [h, l]
        return toks, reads

    def attention_phase(ph, wide, pre):
        stack = ExitStack()
        sb = allocator(stack, f"p{ph}")
        hd = 128 if wide else 64
        nk = KW // hd
        nh = QW // hd
        n = "L1_attn_" if wide else "L0_ffn_"
        wq, wk, wv = (io[n + a] for a in (("q_kernel", "k_kernel", "v_kernel") if wide else ("wq", "wk", "wv")))
        wo = io["L1_attn_out_kernel"] if wide else io["L0_ffn_wo"]
        cs_dram, sn_dram = (io["rope1_cos"], io["rope1_sin"]) if wide else (io["rope0_cos"], io["rope0_sin"])
        scale = 1.0 / float(np.sqrt(hd))
        fence = [l.last() for l in lanes]

        aT_hi, aT_lo = (sb(f"aT_{s}", [P, B, KC, S], F32R) for s in ("hi", "lo"))
        w_hi, w_lo = (sb(f"w_{s}", [P, 2, KC * (QW + 2 * KW)], F32R) for s in ("hi", "lo"))
        o_hi, o_lo = (sb(f"o_{s}", [P, 2, KV * D], F32R) for s in ("hi", "lo"))
        cs = sb("cos", [P, T, hd])
        sn = sb("sin", [P, T, hd])
        lnw = sb("lnw", [P, KC])
        mask = sb("mask", [P, 2 * P], BF16)
        rope_a = Ring([sb(f"rope_a{i}", [P, QW + KW])[:, :] for i in range(2)])
        rope_b = Ring([sb(f"rope_b{i}", [P, QW + KW])[:, :] for i in range(1)])
        tm = Ring([sb(f"tm{i}", [P, QW + nk * P])[:, :] for i in range(2)])
        v_sb = Ring([sb(f"v{i}", [P, T, KW])[:, :, :] for i in range(2)])
        q_st = Ring([sb(f"q{i}", [P, 8, P], F32R)[:, :, :] for i in range(5)])
        k_st = Ring([sb(f"k{i}", [P, 2, 2, S], F32R)[:, :, :, :] for i in range(2)])
        prob = Ring([sb(f"prob{i}", [P, S])[:, :] for i in range(6)])
        prT = Ring([sb(f"prT{i}", [P, KV * P])[:, :] for i in range(10)])
        oT_hi, oT_lo = (Ring([sb(f"oT_{s}{i}", [P, KV * P], F32R)[:, :] for i in range(1)]) for s in ("hi", "lo"))
        small = Ring([sb(f"small{i}", [P, 3, KV])[:, :, :] for i in range(3)])
        norm = Norm(sb, "ln")
        r2 = sb("rms", [P, T])
        n_tile = Ring([sb(f"n_tile{i}", [P, D])[:, :] for i in range(4)])
        sring, tring, wring = Ring([b[:, :] for b in banks[0:3]]), Ring([b[:, :] for b in banks[3:5]]), \
            Ring([b[:, :] for b in banks[5:8]])

        cflag = Flag(sem(f"p{ph}_const"))
        ctok = cflag.dma(sp, cs[:, :, :], cs_dram.rearrange("(t p) d -> p t d", p=P), fence)
        ctok = cflag.dma(sp, sn[:, :, :], sn_dram.rearrange("(t p) d -> p t d", p=P), fence)
        if not wide:
            ctok = cflag.dma(sp, lnw[:, :], io["L0_ffn_ln_w"].rearrange("(c p) -> p c", p=P), fence,
                             by_element=True)
        for l in lanes:
            l.fence(fence)
        mz = pool.do(lambda e: e.memset(mask[:, :], 0.0))
        m1 = pool.do(lambda e: e.affine_select(out=mask[:, P:], in_=mask[:, P:], compare_op=ALU.is_ge, fill=NEG,
                                               base=0, pattern=[[-1, P]], channel_multiplier=1), mz)
        m2 = pool.do(lambda e: e.affine_select(out=mask[:, :P], in_=mask[:, :P], compare_op=ALU.is_ge, fill=NEG,
                                               base=0, pattern=[[1, P]], channel_multiplier=-1), mz)
        pe.fence(m1, m2)

        WQKV = QW + 2 * KW

        def fetch_qkv(c):
            return fetch([(slice(0, P), into(0, QW, WQKV), chunks(wq[:, c * QW:(c + 1) * QW])),
                          (slice(0, P), into(QW, KW, WQKV), chunks(wk[:, c * KW:(c + 1) * KW])),
                          (slice(0, P), into(QW + KW, KW, WQKV), chunks(wv[:, c * KW:(c + 1) * KW]))])

        def fetch_o(c):
            rows = KV * hd
            return fetch([(slice(i * hd, (i + 1) * hd),
                           lambda a: a[:, 0:KV * D].rearrange("p (j n) -> p j n", j=KV),
                           wo[c * QW + i * rows:c * QW + (i + 1) * rows, :].rearrange("(j d) n -> d j n", d=hd))
                          for i in range(nk)])

        w_ready, o_ready, w_used, o_used = {}, {}, {}, {}

        def split_qkv(c, slot):
            w_ready[c] = split(slot, KC * WQKV, w_hi[:, c % 2, :], w_lo[:, c % 2, :], w_used.get(c - 2))

        def split_o(c, slot):
            o_ready[c] = split(slot, KV * D, o_hi[:, c % 2, :], o_lo[:, c % 2, :], o_used.get(c - 2))

        slot_qkv, slot_o = pre or (fetch_qkv(0), fetch_o(0))
        split_qkv(0, slot_qkv)
        split_o(0, slot_o)

        aT_ready = {}
        saves = [Flag(sem(f"p{ph}_save{b}")) for b in range(0 if wide else B)]

        def norm_batch(b):
            tiles = [b * T + t for t in range(T)]
            ready = [[res_ready[i]] for i in tiles]
            rs = norm.run([res[:, i, :] for i in tiles], LN_EPS, ready)
            done = []
            if not wide:
                save = saves[b].dma(sp, res_saved[b * T:(b + 1) * T].rearrange("t p d -> p t d"),
                                 res[:, b * T:(b + 1) * T, :], ready)
                saved_tokens[b:b + 1] = [save]
                a1 = dve.do(lambda e: e.tensor_tensor(r2[:, :], norm.mv[:, :, 1], norm.rs[:, :], ALU.mult), rs, *norm_reads)
                a2 = dve.do(lambda e: e.tensor_tensor(norm.ve[:, :], r2[:, :], norm.rs[:, :], ALU.mult), a1)
                a3 = dve.do(lambda e: e.tensor_scalar(norm.ve[:, :], norm.ve[:, :], RMS_EPS, None, ALU.add), a2)
                rr = pool.do(lambda e: e.tensor_tensor(r2[:, :], norm.ve[:, :], half[:, 0:T], ALU.pow), a3)
                srcs = []
                for t, i in enumerate(tiles):
                    u = dve.do(lambda e, t=t, i=i: e.tensor_scalar(
                        res[:, i, :], res[:, i, :], norm.mv[:, t, 0:1], norm.rs[:, t:t + 1],
                        ALU.subtract, ALU.mult), rs, ready[t], save)
                    res_ready[i] = u
                    nt = n_tile.take()
                    h = act.do(lambda e, t=t, i=i, nt=nt: e.activation(nt.ap, res[:, i, :], ACT.Copy,
                                                                      scale=r2[:, t:t + 1]), u, rr, nt.after)
                    srcs.append((nt, h))
                norm_reads[:] = [srcs[-1][1]]
                norm.read = [srcs[-1][1], u]
            else:
                srcs = []
                for t, i in enumerate(tiles):
                    nt = n_tile.take()
                    h = dve.do(lambda e, t=t, i=i, nt=nt: e.tensor_scalar(
                        nt.ap, res[:, i, :], norm.mv[:, t, 0:1], norm.rs[:, t:t + 1],
                        ALU.subtract, ALU.mult), rs, ready[t], nt.after)
                    srcs.append((nt, h))
                norm.read = [srcs[-1][1]]
            toks, reads = feature_major(lambda t: srcs[t][0].ap, [s[1] for s in srcs], wring,
                                        aT_hi[:, b], aT_lo[:, b], None if wide else lnw, None, ctok)
            for nt, _ in srcs:
                nt.free(*reads)
            aT_ready[b] = toks

        norm_reads = []

        class Unit:
            pass

        def prepare(c, b, unit):
            if c == 0:
                norm_batch(b)
            unit.k, unit.v = k_st.take(), v_sb.take()
            unit.q, unit.q_tok, unit.k_tok, unit.v_tok = [], [], [], []
            whi = w_hi[:, c % 2, :].rearrange("p (k n) -> p k n", k=KC)
            wlo = w_lo[:, c % 2, :].rearrange("p (k n) -> p k n", k=KC)
            for t in range(T):
                tok = slice(t * P, (t + 1) * P)

                def project(bank, c0, cols):
                    pairs = []
                    for k in range(KC):
                        pairs += three(aT_hi[:, b, k, tok], aT_lo[:, b, k, tok],
                                       whi[:, k, c0:c0 + cols], wlo[:, k, c0:c0 + cols])
                    return product(bank.ap[:, 0:cols], pairs, aT_ready[b], w_ready[c], bank.after)
                qb, kb = wring.take(), wring.take()
                qp = project(qb, 0, QW)
                kp = project(kb, QW, 2 * KW)
                w_used[c] = kp
                ra, rb, tb = rope_a.take(), rope_b.take(), tm.take()
                hf = hd // 2

                def rotate(bank, ready, width, at):
                    heads = width // hd
                    x = bank.ap[:, 0:width].rearrange("p (h d) -> p h d", d=hd)
                    a = ra.ap[:, at:at + width].rearrange("p (h d) -> p h d", d=hd)
                    bb = rb.ap[:, at:at + width].rearrange("p (h d) -> p h d", d=hd)

                    def table(m, lo_, hi_):
                        return m[:, t, lo_:hi_].unsqueeze(1).to_broadcast([P, heads, hi_ - lo_])
                    c_all, s_left, s_right = table(cs, 0, hd), table(sn, 0, hf), table(sn, hf, hd)
                    r1 = dve.do(lambda e: e.tensor_tensor(a, x, c_all, ALU.mult), ready, ctok, ra.after)
                    r2_ = dve.do(lambda e: e.tensor_tensor(bb[:, :, 0:hf], x[:, :, hf:hd], s_left, ALU.mult),
                                 ready, rb.after)
                    r3 = dve.do(lambda e: e.tensor_tensor(bb[:, :, hf:hd], x[:, :, 0:hf], s_right, ALU.mult),
                                ready, rb.after)
                    return [r1, r2_, r3]
                qr = rotate(qb, qp, QW, 0)
                qb.free(*qr)
                vc = act.do(lambda e, t=t, kb=kb: e.activation(unit.v.ap[:, t, :], kb.ap[:, KW:2 * KW], ACT.Copy),
                            kp, unit.v.after)
                kr = rotate(kb, [kp, vc], KW, QW)
                kb.free(vc, *kr)
                unit.v_tok.append(vc)
                sums = [pool.do(lambda e, ra=ra, rb=rb, tb=tb: e.tensor_tensor(
                    tb.ap[:, 0:QW], ra.ap[:, 0:QW], rb.ap[:, 0:QW], ALU.add), qr, tb.after)]
                for g in range(nk):
                    for rep in range(nk):
                        dst = tb.ap[:, QW + g * P + rep * hd:QW + g * P + (rep + 1) * hd]
                        sums.append(pool.do(lambda e, dst=dst, ra=ra, rb=rb, g=g: e.tensor_tensor(
                            dst, ra.ap[:, QW + g * hd:QW + (g + 1) * hd],
                            rb.ap[:, QW + g * hd:QW + (g + 1) * hd], ALU.add), kr, tb.after))
                ra.free(sums[-1])
                rb.free(sums[-1])
                yield
                tq, tk, q = wring.take(), wring.take(), q_st.take()
                for j in range(QW // P):
                    qt = transpose(tq.ap[:, j * P:(j + 1) * P], tb.ap[:, j * P:(j + 1) * P], P, sums, tq.after,
                                   signal=j == QW // P - 1)
                for g in range(nk):
                    kt = transpose(tk.ap[:, g * P:(g + 1) * P], tb.ap[:, QW + g * P:QW + (g + 1) * P], P, sums,
                                   tk.after, signal=g == nk - 1)
                tb.free(kt)
                xq = tq.ap.rearrange("p (j n) -> p j n", j=QW // P)
                made = []
                if wide:
                    h = act.do(lambda e, xq=xq, q=q: e.activation(q.ap[:, 0:4, :], xq, ACT.Copy), qt, q.after)
                    l = dve.do(lambda e, xq=xq, q=q: e.tensor_tensor(q.ap[:, 4:8, :], xq, q.ap[:, 0:4, :].bitcast(F32),
                                                                     ALU.subtract), h, q.after)
                    made = [h, l]
                else:
                    qv = q.ap.rearrange("p (j s) n -> p j s n", s=2)
                    halves = [xq[0:hd], xq[hd:P]]
                    hs = [act.do(lambda e, s=s, qv=qv, src=halves[s]: e.activation(qv[0:hd, :, s, :], src, ACT.Copy),
                                 qt, q.after) for s in range(2)]
                    ls = [dve.do(lambda e, s=s, qv=qv, src=halves[s]: e.tensor_tensor(
                        qv[hd:P, :, s, :], src, qv[0:hd, :, s, :].bitcast(F32), ALU.subtract), hs, q.after)
                        for s in range(2)]
                    made = hs + ls
                tq.free(*made)
                xk = tk.ap[:, 0:nk * P].rearrange("p (g n) -> p g n", g=nk)
                h = act.do(lambda e, xk=xk, tok=tok: e.activation(unit.k.ap[:, 0, 0:nk, tok], xk, ACT.Copy, scale=scale),
                           kt, unit.k.after)
                l = dve.do(lambda e, xk=xk, tok=tok: e.scalar_tensor_tensor(
                    unit.k.ap[:, 1, 0:nk, tok], xk, scale, unit.k.ap[:, 0, 0:nk, tok].bitcast(F32),
                    ALU.mult, ALU.subtract), h, unit.k.after)
                tk.free(h, l)
                unit.q.append(q)
                unit.q_tok.append(made)
                unit.k_tok += [h, l]
                yield

        class Group:
            pass

        def group(c, b, unit, t, g):
            o = Group()
            o.c, o.b, o.u, o.t, o.g = c, b, unit, t, g
            o.k0 = max(0, t - 1) if wide else 0
            o.nkt = t + 1 - o.k0
            o.probs, o.exps = [], []
            o.sm = small.take()
            return o

        def scores(o, j):
            keys = slice(o.k0 * P, (o.t + 1) * P)
            w = o.nkt * P
            bank, pr = sring.take(), prob.take()
            q, k = o.u.q[o.t].ap, o.u.k.ap
            khi, klo = k[:, 0, o.g, keys], k[:, 1, o.g, keys]
            if wide:
                pairs = three(q[:, j, :], q[:, 4 + j, :], khi, klo)
            else:
                head = o.g * KV + j
                pairs = [(q[:, head, :], khi), (q[:, head, :], klo)]
            for n_, (l, r) in enumerate(pairs):
                pe.do(lambda e, l=l, r=r, n_=n_: e.matmul(bank.ap[:, 0:w], l, r, start=(n_ == 0), stop=False),
                      o.u.q_tok[o.t], o.u.k_tok[0:2 * (o.t + 1)], bank.after, signal=False)
            mw = min(w, 2 * P) if wide else P
            done = pe.do(lambda e: e.matmul(bank.ap[:, w - mw:w], identb[:, :], mask[:, 2 * P - mw:2 * P],
                                            start=False, stop=True))
            sm = o.sm.ap
            mx = dve.do(lambda e: e.tensor_reduce(sm[:, 0, j:j + 1], bank.ap[:, 0:w], axis=AX.X, op=ALU.max,
                                                  negate=True), done, o.sm.after)
            ex = act.do(lambda e: e.activation(pr.ap[:, 0:w], bank.ap[:, 0:w], ACT.Exp, bias=sm[:, 0, j:j + 1],
                                               accum_out=sm[:, 1, j:j + 1]), mx, pr.after, o.sm.after)
            bank.free(mx, ex)
            o.probs.append(pr)
            o.exps.append(ex)
            o.score_tok = done

        def normalise(o):
            w = o.nkt * P
            sm = o.sm.ap
            r = dve.do(lambda e: e.reciprocal(sm[:, 2, :], sm[:, 1, :]), o.exps)
            o.norms = [dve.do(lambda e, j=j: e.tensor_scalar(o.probs[j].ap[:, 0:w], o.probs[j].ap[:, 0:w],
                                                             sm[:, 2, j:j + 1], None, ALU.mult), r, o.exps[j])
                       for j in range(KV)]
            o.sm.free(*o.norms)
            o.prT, o.prT_tok = [], []

        evacs = [0]

        def turn(o, kt):
            bank, dst = tring.take(), prT.take()
            for j in range(KV):
                tt = transpose(bank.ap[:, j * P:(j + 1) * P], o.probs[j].ap[:, kt * P:(kt + 1) * P], P,
                               o.norms[j], bank.after, signal=j == KV - 1)
            if kt == o.nkt - 1:
                for pr in o.probs:
                    pr.free(tt)
            evacs[0] += 1
            if evacs[0] % 4 == 0:
                cp = dve.do(lambda e: e.tensor_copy(dst.ap, bank.ap), tt, dst.after)
            else:
                cp = act.do(lambda e: e.activation(dst.ap, bank.ap, ACT.Copy), tt, dst.after)
            bank.free(cp)
            o.prT.append(dst)
            o.prT_tok.append(cp)

        def weigh(os):
            bank = wring.take()
            first = os[0]
            for kt in range(first.nkt):
                for o in os:
                    rows = slice(o.g * hd, (o.g + 1) * hd)
                    last = kt == first.nkt - 1 and o is os[-1]
                    tok = pe.do(lambda e, o=o, rows=rows, kt=kt: e.matmul(
                        bank.ap[rows, :], o.u.v.ap[:, o.k0 + kt, o.g * hd:(o.g + 1) * hd], o.prT[kt].ap,
                        start=kt == 0, stop=kt == o.nkt - 1),
                        o.prT_tok[kt], o.u.v_tok[0:o.t + 1], bank.after, signal=last)
            for o in os:
                for s in o.prT:
                    s.free(tok)
            hi, lo = oT_hi.take(), oT_lo.take()
            h = act.do(lambda e: e.activation(hi.ap, bank.ap, ACT.Copy), tok, hi.after)
            l = dve.do(lambda e: e.tensor_tensor(lo.ap, bank.ap, hi.ap.bitcast(F32), ALU.subtract), h, lo.after)
            bank.free(h, l)
            return first, hi, lo, [h, l], tok

        def project_out(w):
            o, hi, lo, ready, _ = w
            bank = wring.take()
            ohi = o_hi[:, o.c % 2, :].rearrange("p (j n) -> p j n", j=KV)
            olo = o_lo[:, o.c % 2, :].rearrange("p (j n) -> p j n", j=KV)
            pairs = []
            for j in range(KV):
                cols = slice(j * P, (j + 1) * P)
                pairs += three(hi.ap[:, cols], lo.ap[:, cols], ohi[:, j, :], olo[:, j, :])
            tok = product(bank.ap[:, 0:D], pairs, ready, o_ready[o.c], bank.after)
            hi.free(tok)
            lo.free(tok)
            o_used[o.c] = tok
            i = o.b * T + o.t
            add = dve.do(lambda e: e.tensor_tensor(res[:, i, :], bank.ap[:, 0:D], res[:, i, :], ALU.add),
                         tok, res_ready[i])
            bank.free(add)
            res_ready[i] = add

        units = [(c, b) for c in range(NU) for b in range(B)]
        made = Unit()
        for _ in prepare(0, 0, made):
            pass
        prev = None
        pend = None
        wo_next = None
        for n_u, (c, b) in enumerate(units):
            unit = made
            made = Unit()
            nxt = units[n_u + 1] if n_u + 1 < len(units) else None
            if b == 1 and c + 1 < NU:
                slot_qkv, slot_o = fetch_qkv(c + 1), fetch_o(c + 1)
            if b == 2 and c + 1 < NU:
                split_qkv(c + 1, slot_qkv)
                split_o(c + 1, slot_o)
            back = prepare(*nxt, made) if nxt else iter(())
            steps = [(t, g) for t in range(T) for g in range(nk)]
            per_step = 2 * T // len(steps)
            for t, g in steps:
                cur = group(c, b, unit, t, g)
                nturn = prev.nkt if prev else 0
                for j in range(KV):
                    for kt in range(2 * j, min(2 * j + 2, nturn)):
                        turn(prev, kt)
                    scores(cur, j)
                if wo_next:
                    project_out(wo_next)
                    wo_next = None
                if prev:
                    pend = (pend or []) + [prev]
                    if prev.g == nk - 1:
                        wo_next = weigh(pend)
                        if prev.t == T - 1:
                            prev.u.v.free(wo_next[4])
                        pend = None
                for _ in range(per_step):
                    next(back, None)
                if g == nk - 1:
                    unit.q[t].free(cur.score_tok)
                normalise(cur)
                prev = cur
            unit.k.free(cur.score_tok)
            for _ in back:
                pass
        for kt in range(prev.nkt):
            turn(prev, kt)
        if wo_next:
            project_out(wo_next)
        project_out(weigh((pend or []) + [prev]))
        stack.close()

    def moe_phase(ph, pre):
        stack = ExitStack()
        sb = allocator(stack, f"p{ph}")
        fence = [l.last() for l in lanes]
        hT_hi, hT_lo = (sb(f"hT_{s}", [P, B, KC, S], F32R) for s in ("hi", "lo"))
        w_hi, w_lo = (sb(f"w_{s}", [P, 2, 3 * KC * H], F32R) for s in ("hi", "lo"))
        xin = sb("xin", [P, NT, D])
        wg_raw = sb("wg", [P, KC, E])
        wg_hi, wg_lo = (sb(f"wg_{s}", [P, KC, E], F32R) for s in ("hi", "lo"))
        lnw = sb("lnw", [P, KC])
        sq = sb("sq", [P, D])
        ms, rs = sb("ms", [P, T]), sb("rs", [P, T])
        n_tile = Ring([sb(f"n_tile{i}", [P, D])[:, :] for i in range(4)])
        silu = Ring([sb(f"silu{i}", [P, S])[:, :] for i in range(3)])
        full = Ring([sb(f"full{i}", [P, S])[:, :] for i in range(3)])
        a_hi, a_lo = (Ring([sb(f"a_{s}{i}", [P, HC, S], F32R)[:, :, :] for i in range(2)]) for s in ("hi", "lo"))
        ext = sb("ext", [P, T, E + 4])
        rep = sb("rep", [P, T, E + 4])
        top8 = sb("top8", [P, T, 8])
        ex, sel, gate = sb("ex", [P, T, E]), sb("sel", [P, T, E]), sb("gate", [P, NT, E])
        gs = sb("gs", [P, 2, T])
        aring, yring = Ring([b[:, :] for b in banks[0:5]]), Ring([b[:, :] for b in banks[5:8]])

        cflag = Flag(sem(f"p{ph}_const"))
        cflag.dma(sp, wg_raw[:, :, :], chunks(io["L0_ffn_wg"]), fence)
        ctok = cflag.dma(sp, lnw[:, :], io["L0_ffn_ff_ln_w"].rearrange("(c p) -> p c", p=P), fence,
                             by_element=True)
        xflag = Flag(sem(f"p{ph}_x"))
        xtok = xflag.dma(sp, xin[:, :, :], res_saved.rearrange("t p d -> p t d"), fence, saved_tokens)
        for l in lanes:
            l.fence(fence)
        wgh = act.do(lambda e: e.activation(wg_hi[:, :, :], wg_raw[:, :, :], ACT.Copy), ctok)
        wgl = dve.do(lambda e: e.tensor_tensor(wg_lo[:, :, :], wg_raw[:, :, :], wg_hi[:, :, :].bitcast(F32),
                                               ALU.subtract), wgh, ctok)
        sent = [dve.do(lambda e, k=k: e.memset(ext[:, :, E + k], SENT[k])) for k in range(4)]

        w1, w3, w2 = io["L0_ffn_w1"], io["L0_ffn_w3"], io["L0_ffn_w2"]

        def fetch_e(e_):
            def at(i):
                return lambda a: a[:, i * KC * H:(i + 1) * KC * H].rearrange("p (c n) -> p c n", c=KC)
            return fetch([(slice(0, P), at(i), chunks(w[e_])) for i, w in enumerate((w1, w3, w2))])

        w_ready, w_used = {}, {}

        def split_e(e_, slot):
            w_ready[e_] = split(slot, 3 * KC * H, w_hi[:, e_ % 2, :], w_lo[:, e_ % 2, :], w_used.get(e_ - 2))

        slots = {0: pre or fetch_e(0)}
        slots[1] = fetch_e(1)
        hT_ready, gate_ready = {}, {}
        prior = {"sq": None, "ms": [], "small": []}

        def norm_batch(b):
            tiles = [b * T + t for t in range(T)]
            s = []
            for t, i in enumerate(tiles):
                q_ = act.do(lambda e, t=t, i=i: e.activation(sq[:, :], res[:, i, :], ACT.Square,
                                                             accum_out=ms[:, t:t + 1]),
                            res_ready[i], prior["sq"], *prior["ms"])
                prior["sq"] = q_
                s.append(q_)
            m = dve.do(lambda e: e.tensor_scalar(ms[:, :], ms[:, :], 1.0 / D, RMS_EPS, ALU.mult, ALU.add), s)
            r = pool.do(lambda e: e.tensor_tensor(rs[:, :], ms[:, :], half[:, 0:T], ALU.pow), m, *prior["ms"])
            srcs = []
            for t, i in enumerate(tiles):
                nt = n_tile.take()
                h = dve.do(lambda e, t=t, i=i, nt=nt: e.tensor_scalar(nt.ap, res[:, i, :], rs[:, t:t + 1], None,
                                                                     ALU.mult), r, nt.after)
                srcs.append((nt, h))
            prior["ms"] = [r, srcs[-1][1]]
            toks, reads = feature_major(lambda t: srcs[t][0].ap, [s_[1] for s_ in srcs], aring,
                                        hT_hi[:, b], hT_lo[:, b], lnw, None, ctok)
            for nt, _ in srcs:
                nt.free(*reads)
            hT_ready[b] = toks

        def route_batch(b):
            bank = aring.take()
            for t in range(T):
                cols = slice(t * P, (t + 1) * P)
                pairs = []
                for k in range(KC):
                    pairs += three(hT_hi[:, b, k, cols], hT_lo[:, b, k, cols], wg_hi[:, k, :], wg_lo[:, k, :])
                lg = product(bank.ap[:, t * E:(t + 1) * E], pairs, hT_ready[b], wgh, wgl, bank.after)
            prev_ = prior["small"]
            cp = dve.do(lambda e: e.tensor_copy(ext[:, :, 0:E], bank.ap[:, 0:T * E].rearrange("p (t e) -> p t e", t=T)),
                        lg, sent, *prev_)
            bank.free(cp)
            mx = [dve.do(lambda e, t=t: e.max(top8[:, t, :], ext[:, t, 0:E]), cp, *prev_) for t in range(T)]
            sub = dve.do(lambda e: e.tensor_tensor(ex[:, :, :], ext[:, :, 0:E],
                                                   top8[:, :, 0:1].to_broadcast([P, T, E]), ALU.subtract), mx)
            exp = act.do(lambda e: e.activation(ex[:, :, :], ex[:, :, :], ACT.Exp), sub)
            st = [dve.do(lambda e: e.tensor_copy(top8[:, :, 4:8], ext[:, :, E:E + 4]), mx, sent)]
            mr = [dve.do(lambda e, t=t: e.match_replace(rep[:, t, :], top8[:, t, :], ext[:, t, :], 3.0e38), st)
                  for t in range(T)]
            ne = dve.do(lambda e: e.tensor_tensor(sel[:, :, :], rep[:, :, 0:E], ext[:, :, 0:E], ALU.not_equal), mr)
            mu = dve.do(lambda e: e.tensor_tensor(ex[:, :, :], ex[:, :, :], sel[:, :, :], ALU.mult), ne, exp)
            sm = dve.do(lambda e: e.tensor_reduce(gs[:, 0, :], ex[:, :, :], axis=AX.X, op=ALU.add), mu)
            rc = dve.do(lambda e: e.reciprocal(gs[:, 1, :], gs[:, 0, :]), sm)
            g = dve.do(lambda e: e.tensor_tensor(gate[:, b * T:(b + 1) * T, :], ex[:, :, :],
                                                 gs[:, 1, :].unsqueeze(2).to_broadcast([P, T, E]), ALU.mult), rc)
            prior["small"] = [g]
            gate_ready[b] = g

        def up(e_, b):
            whi = w_hi[:, e_ % 2, :].rearrange("p (i k n) -> p i k n", i=3, k=KC)
            wlo = w_lo[:, e_ % 2, :].rearrange("p (i k n) -> p i k n", i=3, k=KC)
            hi, lo = a_hi.take(), a_lo.take()
            ready = []
            for m in range(HC):
                cols = slice(m * P, (m + 1) * P)
                got = []
                for i in range(2):
                    bank = aring.take()
                    pairs = []
                    for k in range(KC):
                        pairs += three(whi[:, i, k, cols], wlo[:, i, k, cols], hT_hi[:, b, k, :], hT_lo[:, b, k, :])
                    got.append((bank, product(bank.ap, pairs, hT_ready[b], w_ready[e_], bank.after)))
                (b1, t1), (b3, t3) = got
                s, f = silu.take(), full.take()
                sl = act.do(lambda e, s=s, b1=b1: e.activation(s.ap, b1.ap, ACT.Silu), t1, s.after)
                b1.free(sl)
                mu = dve.do(lambda e, s=s, f=f, b3=b3: e.tensor_tensor(f.ap, b3.ap, s.ap, ALU.mult), sl, t3, f.after)
                b3.free(mu)
                s.free(mu)
                h = act.do(lambda e, f=f, m=m: e.activation(hi.ap[:, m, :], f.ap, ACT.Copy), mu, hi.after)
                l = dve.do(lambda e, f=f, m=m: e.tensor_tensor(lo.ap[:, m, :], f.ap, hi.ap[:, m, :].bitcast(F32),
                                                               ALU.subtract), h, lo.after)
                f.free(h, l)
                ready += [h, l]
            return e_, b, hi, lo, ready

        def down(e_, b, hi, lo, ready):
            whi = w_hi[:, e_ % 2, :].rearrange("p (i k n) -> p i k n", i=3, k=KC)
            wlo = w_lo[:, e_ % 2, :].rearrange("p (i k n) -> p i k n", i=3, k=KC)
            for pair in range(0, T, 2):
                bank = yring.take()
                for t in (pair, pair + 1):
                    cols = slice(t * P, (t + 1) * P)
                    pairs = []
                    for m in range(HC):
                        pairs += three(hi.ap[:, m, cols], lo.ap[:, m, cols], whi[:, 2, m, :], wlo[:, 2, m, :])
                    tok = product(bank.ap[:, (t - pair) * D:(t - pair + 1) * D], pairs, ready, bank.after)
                for t in (pair, pair + 1):
                    i = b * T + t
                    y = bank.ap[:, (t - pair) * D:(t - pair + 1) * D]
                    add = dve.do(lambda e, y=y, i=i: e.scalar_tensor_tensor(
                        res[:, i, :], y, gate[:, i, e_:e_ + 1], res[:, i, :], ALU.mult, ALU.add),
                        tok, res_ready[i], gate_ready[b])
                    res_ready[i] = add
                    if e_ == E - 1:
                        res_ready[i] = dve.do(lambda e, i=i: e.scalar_tensor_tensor(
                            res[:, i, :], res[:, i, :], 0.5, xin[:, i, :], ALU.mult, ALU.add), add, xtok)
                bank.free(add)
            hi.free(tok)
            lo.free(tok)
            w_used[e_] = tok

        for b in range(B):
            norm_batch(b)
        split_e(0, slots[0])
        for b in range(B):
            route_batch(b)
        last = None
        for e_ in range(E):
            for b in range(B):
                cur = up(e_, b)
                if last:
                    down(*last)
                last = cur
                if b == 0 and e_ + 1 < E:
                    split_e(e_ + 1, slots[e_ + 1])
                if b == 1 and e_ + 2 < E:
                    slots[e_ + 2] = fetch_e(e_ + 2)
        down(*last)
        stack.close()

    def small_attention_phase(ph):
        stack = ExitStack()
        sb = allocator(stack, f"p{ph}")
        fence = [l.last() for l in lanes]
        KD = SKV * SD
        ROWS = PARTS * PARTS * SD
        SCALE = 1.0 / float(np.sqrt(SD))
        PRE = "L0_attn_"
        uT_hi, uT_lo = (Ring([sb(f"uT_{s}{i}", [P, KC, S], F32R)[:, :, :] for i in range(1)]) for s in ("hi", "lo"))
        WW = D + 2 * KD + D
        w_hi, w_lo = (sb(f"w_{s}", [P, KC, WW], F32R) for s in ("hi", "lo"))
        bq, bk = sb("bq", [P, D // P]), sb("bk", [KD, 1])
        bv, bo = sb("bv", [P, KD]), sb("bo", [P, D])
        q32, r32 = Ring([sb(f"q32_{i}", [P, S])[:, :] for i in range(2)]), sb("r32", [P, S])
        qp = Ring([sb(f"qp{i}", [P, PARTS, S], BF16)[:, :, :] for i in range(2)],
                  [Flag(sem(f"p{ph}_save{i}")) for i in range(2)])
        q_st = [sb(f"q_st{i}", [P, SH, S], BF16) for i in range(1)]
        k_st = [[sb(f"k_st{i}_{z}", [P, SKV, S], BF16) for z in range(2)] for i in range(1)]
        VR = 32
        v_aug = Ring([sb(f"v_aug{i}", [P, T, SKV, VR])[:, :, :, :] for i in range(2)])
        nmax = sb("nmax", [P, 2, T, 8])
        nm_p = [sb(f"nm_p{i}", [8, PARTS, S], BF16) for i in range(2)]
        nm_r = sb("nm_r", [8, S])
        prT = Ring([sb(f"prT{i}", [P, S])[:, :] for i in range(8)])
        o_sb = Ring([sb(f"o_sb{i}", [P, S])[:, :] for i in range(2)])
        rsum = Ring([sb(f"rsum{i}", [P, T, KV])[:, :, :] for i in range(2)])
        o_tm = Ring([sb(f"o_tm{i}", [P, T, D])[:, :, :] for i in range(1)])
        oT_hi, oT_lo = (Ring([sb(f"oT_{s}{i}", [P, KC, S], F32R)[:, :, :] for i in range(1)]) for s in ("hi", "lo"))
        norm = Norm(sb, "ln")
        n_tile = Ring([sb(f"n_tile{i}", [P, D])[:, :] for i in range(4)])
        sring, tring = Ring([b[:, :] for b in banks[0:3]]), Ring([b[:, :] for b in banks[3:6]])
        oring, wring = Ring([b[:, :] for b in banks[6:7]]), Ring([b[:, :] for b in banks[7:8]])

        def put(c0, cols):
            return lambda a: a[:, 0:KC * WW].rearrange("p (c n) -> p c n", c=KC)[:, :, c0:c0 + cols]
        slot = fetch([(slice(0, P), put(0, D), chunks(io[PRE + "Wq"])),
                      (slice(0, P), put(D, KD), chunks(io[PRE + "Wk"])),
                      (slice(0, P), put(D + KD, KD), chunks(io[PRE + "Wv"])),
                      (slice(0, P), put(D + 2 * KD, D), chunks(io[PRE + "Wo"]))])
        cflag = Flag(sem(f"p{ph}_const"))
        cflag.dma(sp, bq[:, :], io[PRE + "bq"].rearrange("(c p) -> p c", p=P), fence,
                             by_element=True)
        cflag.dma(sp, bk[:, :], io[PRE + "bk"].rearrange("(p a) -> p a", a=1), fence,
                  by_element=True)
        cflag.dma(sp, bv[:, :], io[PRE + "bv"].rearrange("(a n) -> a n", a=1).to_broadcast([P, KD]), fence)
        ctok = cflag.dma(sp, bo[:, :], io[PRE + "bo"].rearrange("(a n) -> a n", a=1).to_broadcast([P, D]), fence)
        for l in lanes:
            l.fence(fence)
        w_ready = split(slot, KC * WW, w_hi[:, :, :].rearrange("p c n -> p (c n)"),
                        w_lo[:, :, :].rearrange("p c n -> p (c n)"))
        zero = [pool.do(lambda e, m=m: e.memset(m[64:P, :, :], 0.0)) for m in (q_st[0], k_st[0][0], k_st[0][1])]
        ones = top_ones(sb)
        oflag = Flag(sem(f"p{ph}_ones"))
        one_rows = oflag.dma(sp, k_st[0][1][ROWS:ROWS + PARTS, :, :], ones[0][0:PARTS, :].rearrange(
            "p (g n) -> p g n", g=SKV), zero, ones[1])
        va = []
        for s in v_aug.slots:
            z = pool.do(lambda e, s=s: e.memset(s.ap, 0.0))
            va.append(pool.do(lambda e, s=s: e.memset(s.ap[:, :, :, SD], 1.0), z))

        qk_flag, nm_flag = Flag(sem(f"p{ph}_qk")), [Flag(sem(f"p{ph}_nm{i}")) for i in range(2)]
        prior = {"r32": [], "st_read": [], "nmax": [[], []], "nm_p": [[], []], "nm_r": [], "saved_read": {}}

        def cols(c0, n_):
            return slice(c0, c0 + n_)

        for b in range(B):
            tiles = [b * T + t for t in range(T)]
            ready = [[res_ready[i]] for i in tiles]
            rs = norm.run([res[:, i, :] for i in tiles], LN_EPS, ready)
            srcs = []
            for t, i in enumerate(tiles):
                nt = n_tile.take()
                h = dve.do(lambda e, t=t, i=i, nt=nt: e.tensor_scalar(
                    nt.ap, res[:, i, :], norm.mv[:, t, 0:1], norm.rs[:, t:t + 1], ALU.subtract, ALU.mult),
                    rs, ready[t], nt.after)
                srcs.append((nt, h))
            norm.read = [srcs[-1][1]]
            uh, ul = uT_hi.take(), uT_lo.take()
            u_ready, reads = feature_major(lambda t: srcs[t][0].ap, [s[1] for s in srcs], wring,
                                           uh.ap, ul.ap, None, None, uh.after, ul.after)
            for nt, _ in srcs:
                nt.free(*reads)
            saved = []
            last_mm = None
            for c0, width, bias, dst, sc in ((0, P, bq[:, 0:1], 0, SCALE), (P, P, bq[:, 1:2], P, SCALE),
                                             (D, KD, bk[:, 0:1], D, 1.0)):
                bank, q_, pp = wring.take(), q32.take(), qp.take()
                pairs = []
                for k in range(KC):
                    pairs += three(w_hi[:, k, cols(c0, width)], w_lo[:, k, cols(c0, width)], uh.ap[:, k, :], ul.ap[:, k, :])
                mm = product(bank.ap[0:width, :], pairs, u_ready, w_ready, bank.after)
                r = slice(0, width)
                a0 = dve.do(lambda e, q_=q_, bank=bank, r=r, bias=bias, sc=sc: e.tensor_scalar(
                    q_.ap[r, :], bank.ap[r, :], bias, sc, ALU.add, ALU.mult), mm, ctok, q_.after)
                bank.free(a0)
                a1 = act.do(lambda e, q_=q_, pp=pp, r=r: e.activation(pp.ap[r, 0, :], q_.ap[r, :], ACT.Copy), a0, pp.after)
                a2 = dve.do(lambda e, q_=q_, pp=pp, r=r: e.tensor_tensor(r32[r, :], q_.ap[r, :], pp.ap[r, 0, :],
                                                                        ALU.subtract), a1, *prior["r32"])
                a3 = act.do(lambda e, pp=pp, r=r: e.activation(pp.ap[r, 1, :], r32[r, :], ACT.Copy), a2, pp.after)
                a4 = dve.do(lambda e, pp=pp, r=r: e.tensor_tensor(pp.ap[r, 2, :], r32[r, :], pp.ap[r, 1, :],
                                                                 ALU.subtract), a3)
                prior["r32"] = [a4]
                q_.free(a1, a2)
                sv = pp.flag.dma(sp, parts_saved[b % 2, :, dst:dst + width, :].rearrange("m r n -> r m n"),
                                   pp.ap[r, :, :], a4, a1, a3, prior["saved_read"].get(b - 2))
                pp.free(sv)
                saved.append(sv)
            va_s = v_aug.take()
            bank = wring.take()
            for t in range(T):
                tk = slice(t * P, (t + 1) * P)
                pairs = []
                for k in range(KC):
                    pairs += three(uh.ap[:, k, tk], ul.ap[:, k, tk], w_hi[:, k, cols(D + KD, KD)], w_lo[:, k, cols(D + KD, KD)])
                mm = product(bank.ap[:, t * KD:(t + 1) * KD], pairs, bank.after)
            v_ready = [dve.do(lambda e, t=t, bank=bank, va_s=va_s: e.tensor_tensor(
                va_s.ap[:, t, :, 0:SD], bank.ap[:, t * KD:(t + 1) * KD].rearrange("p (g d) -> p g d", g=SKV),
                bv[:, :].rearrange("p (g d) -> p g d", g=SKV), ALU.add), mm, va, va_s.after) for t in range(T)]
            bank.free(*v_ready)
            uh.free(mm)
            ul.free(mm)
            qs, ks = q_st[0], k_st[0]
            st = []
            for a in range(PARTS):
                for m in range(PARTS):
                    rows = slice((a * PARTS + m) * SD, (a * PARTS + m + 1) * SD)
                    st.append(qk_flag.dma(sp, qs[rows, :, :], parts_saved[b % 2, a, 0:D, :].rearrange(
                        "(h d) n -> d h n", d=SD), saved, zero, *prior["st_read"]))
                    for z in range(2):
                        st.append(qk_flag.dma(sp, ks[z][rows, :, :], parts_saved[b % 2, m, D:D + KD, :].rearrange(
                            "(g d) n -> d g n", d=SD), saved, zero, *prior["st_read"]))
            st = st[-1]
            prior["saved_read"][b] = st
            otm = o_tm.take()
            o_toks = []

            def maxima(qt):
                s = qt % 2
                toks = []
                for hh in range(8):
                    head = qt * 8 + hh
                    for t in range(T):
                        bk_ = sring.take()
                        mm = product(bk_.ap, [(qs[:, head, t * P:(t + 1) * P], ks[0][:, head // KV, :])], st, bk_.after)
                        mx = dve.do(lambda e, t=t, hh=hh, bk_=bk_: e.tensor_reduce(
                            nmax[:, s, t, hh:hh + 1], bk_.ap, axis=AX.X, op=ALU.max, negate=True), mm, *prior["nmax"][s])
                        bk_.free(mx)
                        toks.append(mx)
                        yield
                wb = wring.take()
                for t in range(T):
                    tt = transpose(wb.ap[0:8, t * P:(t + 1) * P], nmax[:, s, t, :], P, toks[-1], wb.after,
                                   signal=t == T - 1)
                prior["nmax"][s] = [tt]
                np_ = nm_p[s]
                a1 = act.do(lambda e: e.activation(np_[:, 0, :], wb.ap[0:8, :], ACT.Copy), tt, *prior["nm_p"][s])
                a2 = dve.do(lambda e: e.tensor_tensor(nm_r[:, :], wb.ap[0:8, :], np_[:, 0, :], ALU.subtract), a1,
                            *prior["nm_r"])
                wb.free(a1, a2)
                a3 = act.do(lambda e: e.activation(np_[:, 1, :], nm_r[:, :], ACT.Copy), a2)
                a4 = dve.do(lambda e: e.tensor_tensor(np_[:, 2, :], nm_r[:, :], np_[:, 1, :], ALU.subtract), a3)
                prior["nm_r"] = [a4]
                done = None
                for m in range(PARTS):
                    done = nm_flag[s].dma(sp, qs[ROWS + m:ROWS + m + 1, qt * 8:(qt + 1) * 8, :],
                                          np_[:, m, :], a1, a3, a4, mm)
                prior["nm_p"][s] = [done]
                nm_done[qt] = done
                yield

            nm_done = {}

            def attend(qt):
                for g in range(2):
                    kv = qt * 2 + g
                    ob = oring.take()
                    for kt in range(T):
                        exps = []
                        for j in range(KV):
                            head = kv * KV + j
                            tb, pt = tring.take(), prT.take()
                            mm = product(tb.ap, [(ks[1][:, kv, kt * P:(kt + 1) * P], qs[:, head, :])],
                                         nm_done[qt], one_rows, tb.after)
                            ex = act.do(lambda e, tb=tb, pt=pt: e.activation(pt.ap, tb.ap, ACT.Exp), mm, pt.after)
                            tb.free(ex)
                            exps.append((pt, ex))
                            yield
                        for j, (pt, ex) in enumerate(exps):
                            av = pe.do(lambda e, j=j, pt=pt, kt=kt, kv=kv, ob=ob, va_s=va_s: e.matmul(
                                ob.ap[VR * j:VR * (j + 1), :], va_s.ap[:, kt, kv, :], pt.ap,
                                start=kt == 0, stop=kt == T - 1), ex, v_ready, ob.after, signal=j == KV - 1)
                        for pt, _ in exps:
                            pt.free(av)
                    os_ = o_sb.take()
                    c1 = act.do(lambda e, os_=os_, ob=ob: e.activation(os_.ap, ob.ap, ACT.Copy), av, os_.after)
                    ob.free(c1)
                    wb = wring.take()
                    for t in range(T):
                        tt = transpose(wb.ap[:, t * P:(t + 1) * P], os_.ap[:, t * P:(t + 1) * P], P, c1, wb.after,
                                       signal=t == T - 1)
                    os_.free(tt)
                    rr = rsum.take()
                    view = wb.ap.rearrange("p (t j r) -> p t j r", t=T, j=KV)
                    rc = dve.do(lambda e, rr=rr, view=view: e.reciprocal(rr.ap, view[:, :, :, SD]), tt, rr.after)
                    dst = otm.ap[:, :, kv * KV * SD:(kv + 1) * KV * SD].rearrange("p t (j d) -> p t j d", j=KV)
                    mu = [dve.do(lambda e, rr=rr, view=view, dst=dst, t=t: e.tensor_tensor(
                        dst[:, t], view[:, t, :, 0:SD], rr.ap[:, t, :].unsqueeze(2).to_broadcast([P, KV, SD]),
                        ALU.mult), rc, otm.after) for t in range(T)]
                    wb.free(*mu)
                    rr.free(mu[-1])
                    o_toks.append(mu[-1])
                    last_av[0] = av

            last_av = [None]
            for _ in maxima(0):
                pass
            for qt in range(4):
                front = attend(qt)
                back = maxima(qt + 1) if qt < 3 else iter(())
                for _ in front:
                    next(back, None)
                for _ in back:
                    pass
            va_s.free(last_av[0])
            prior["st_read"] = [last_av[0]]
            oh, ol = oT_hi.take(), oT_lo.take()
            o_ready, reads = feature_major(lambda t: otm.ap[:, t, :], [o_toks] * T, wring, oh.ap, ol.ap, None, None,
                                           oh.after, ol.after)
            otm.free(*reads)
            for t, i in enumerate(tiles):
                bank = wring.take()
                tk = slice(t * P, (t + 1) * P)
                pairs = []
                for k in range(KC):
                    pairs += three(oh.ap[:, k, tk], ol.ap[:, k, tk], w_hi[:, k, cols(D + 2 * KD, D)],
                                   w_lo[:, k, cols(D + 2 * KD, D)])
                mm = product(bank.ap[:, 0:D], pairs, o_ready, bank.after)
                a1 = dve.do(lambda e, i=i, bank=bank: e.tensor_tensor(res[:, i, :], bank.ap[:, 0:D], res[:, i, :],
                                                                      ALU.add), mm, res_ready[i])
                bank.free(a1)
                res_ready[i] = pool.do(lambda e, i=i: e.tensor_tensor(res[:, i, :], res[:, i, :], bo[:, :], ALU.add),
                                       a1, ctok)
            oh.free(mm)
            ol.free(mm)
        stack.close()

    def top_ones(sb):
        m = sb("ones_rows", [PARTS, SKV * S], BF16)
        t = pool.do(lambda e: e.memset(m[:, :], 1.0))
        return m, t

    def thought_phase(ph, final):
        stack = ExitStack()
        sb = allocator(stack, f"p{ph}")
        fence = [l.last() for l in lanes]
        PRE = "L1_ffn_"
        HH = 1024
        HN = HH // P
        u = sb("u", [P, NT, D])
        gt = sb("gate", [P, NT, D])
        uT_hi, uT_lo = (Ring([sb(f"uT_{s}{i}", [P, KC, S], F32R)[:, :, :] for i in range(2)]) for s in ("hi", "lo"))
        gw_hi, gw_lo = (sb(f"gw_{s}", [P, KC * D], F32R) for s in ("hi", "lo"))
        agg, bc = sb("agg", [P, KC, D]), sb("bc", [P, KC, D])
        d1, d2 = sb("d1", [P, KC, HH]), sb("d2", [P, HN, D])
        d1b = sb("d1b", [P, HN])
        gb, og, ob_ = sb("gb", [P, D]), sb("og", [P, D]), sb("ob", [P, D])
        rows = {k: sb("r_" + k, [B, D]) for k in ("in_gamma", "in_beta", "agg_b", "pn_gamma", "pn_beta", "d2_b", "bc_b")}
        last = sb("last", [B, D])
        th, nrm = sb("thought", [B, D]), sb("nrm", [B, D])
        tT = sb("tT", [P, KC, B])
        hid, hid2 = sb("hid", [P, HN, B]), sb("hid2", [P, HN, B])
        sel = sb("sel", [B, B, P])
        bc4 = sb("bc4", [B, D])
        bcast = sb("bcast", [P, B, D])
        norm, nrm4, norm2 = Norm(sb, "ln"), Norm(sb, "l4", parts=B, tiles=1), Norm(sb, "lo")
        wring, cring = Ring([b[:, :] for b in banks[0:6]]), Ring([b[:, :] for b in banks[6:8]])

        slot = fetch([(slice(0, P), lambda a: a[:, 0:KC * D].rearrange("p (c n) -> p c n", c=KC),
                       chunks(io[PRE + "gate_w"]))])
        cflag = Flag(sem(f"p{ph}_const"))
        for k, m in rows.items():
            cflag.dma(sp, m[:, :], io[PRE + k].rearrange("(a n) -> a n", a=1).to_broadcast([B, D]), fence)
        cflag.dma(sp, agg[:, :, :], chunks(io[PRE + "agg_w"]), fence)
        cflag.dma(sp, d1[:, :, :], chunks(io[PRE + "d1_w"]), fence)
        cflag.dma(sp, d2[:, :, :], chunks(io[PRE + "d2_w"]), fence)
        cflag.dma(sp, bc[:, :, :], chunks(io[PRE + "bc_w"]), fence)
        cflag.dma(sp, d1b[:, :], io[PRE + "d1_b"].rearrange("(c p) -> p c", p=P), fence,
                             by_element=True)
        for m, k in ((gb, "gate_b"), (og, "out_gamma"), (ob_, "out_beta")):
            ctok = cflag.dma(sp, m[:, :], io[PRE + k].rearrange("(a n) -> a n", a=1).to_broadcast([P, D]), fence)
        for l in lanes:
            l.fence(fence)
        z = pool.do(lambda e: e.memset(sel[:, :, :], 0.0))
        sel_ready = pool.do(lambda e: e.affine_select(out=sel[:, :, :], in_=sel[:, :, :], compare_op=ALU.not_equal,
                                                      fill=1.0, base=0, pattern=[[-1, B], [0, P]],
                                                      channel_multiplier=1), z)
        gw_ready = split(slot, KC * D, gw_hi[:, :], gw_lo[:, :])
        og_h = dve.do(lambda e: e.tensor_scalar(og[:, :], og[:, :], 0.5, None, ALU.mult), ctok)
        ob_h = dve.do(lambda e: e.tensor_scalar(ob_[:, :], ob_[:, :], 0.5, None, ALU.mult), ctok)

        u_ready = []
        uflag = Flag(sem(f"p{ph}_last"))
        for b in range(B):
            tiles = [b * T + t for t in range(T)]
            rs = norm.run([res[:, i, :] for i in tiles], LN_EPS, [[res_ready[i]] for i in tiles])
            for t, i in enumerate(tiles):
                u_ready.append(dve.do(lambda e, t=t, i=i: e.tensor_scalar(
                    u[:, i, :], res[:, i, :], norm.mv[:, t, 0:1], norm.rs[:, t:t + 1], ALU.subtract, ALU.mult),
                    rs, res_ready[i]))
            norm.read = [u_ready[-1]]
            lt = uflag.dma(sp, last[b:b + 1, :], u[P - 1:P, b * T + T - 1, :], u_ready[-1])

        g_ready = {}

        def gates(b):
            hi, lo = uT_hi.take(), uT_lo.take()
            ready, _ = feature_major(lambda t: u[:, b * T + t, :], [u_ready[b * T + t] for t in range(T)], wring,
                                     hi.ap, lo.ap, None, None, hi.after, lo.after)
            yield
            ghi = gw_hi[:, :].rearrange("p (k n) -> p k n", k=KC)
            glo = gw_lo[:, :].rearrange("p (k n) -> p k n", k=KC)
            for t in range(T):
                bank = wring.take()
                tk = slice(t * P, (t + 1) * P)
                pairs = []
                for k in range(KC):
                    pairs += three(hi.ap[:, k, tk], lo.ap[:, k, tk], ghi[:, k, :], glo[:, k, :])
                mm = product(bank.ap[:, 0:D], pairs, ready, gw_ready, bank.after)
                g = dve.do(lambda e, i=b * T + t, bank=bank: e.tensor_tensor(gt[:, i, :], bank.ap[:, 0:D], gb[:, :],
                                                                             ALU.add), mm, ctok)
                bank.free(g)
                g_ready[b * T + t] = g
                if t % 2:
                    yield
            hi.free(mm)
            lo.free(mm)

        def all_gates():
            for b in range(B):
                yield from gates(b)
        back = all_gates()

        def ln4(dst, src, ready, gamma, beta):
            rs = nrm4.run([src], FFN_EPS, [ready])
            a = dve.do(lambda e: e.tensor_scalar(dst, src, nrm4.mv[:, 0, 0:1], nrm4.rs[:, 0:1],
                                                 ALU.subtract, ALU.mult), rs)
            m = dve.do(lambda e: e.tensor_tensor(dst, dst, gamma[:, :], ALU.mult), a, ctok)
            nrm4.read = [a]
            return dve.do(lambda e: e.tensor_tensor(dst, dst, beta[:, :], ALU.add), m)

        prior = {"tT": [], "hid": [], "hid2": []}

        def columns(src, ready):
            bank = cring.take()
            for k in range(KC):
                tt = transpose(bank.ap[:, k * B:(k + 1) * B], src[:, k * P:(k + 1) * P], B, ready, bank.after,
                               signal=k == KC - 1)
            c = dve.do(lambda e: e.tensor_copy(tT[:, :, :], bank.ap[:, 0:KC * B].rearrange("p (k b) -> p k b", k=KC)),
                       tt, *prior["tT"])
            bank.free(c)
            return c

        def linear(w, ready):
            bank = cring.take()
            mm = product(bank.ap[0:B, 0:D], [(tT[:, k, :], w[:, k, :]) for k in range(KC)], ready, ctok, bank.after)
            prior["tT"] = [mm]
            return bank, mm

        n0 = ln4(nrm[:, :], last[:, :], lt, rows["in_gamma"], rows["in_beta"])
        bank, mm = linear(agg, columns(nrm, n0))
        thr = dve.do(lambda e, bank=bank: e.tensor_tensor(th[:, :], bank.ap[0:B, 0:D], rows["agg_b"][:, :], ALU.add), mm)
        bank.free(thr)
        for _ in range(4):
            next(back, None)
            n1 = ln4(nrm[:, :], th[:, :], thr, rows["pn_gamma"], rows["pn_beta"])
            next(back, None)
            c1 = columns(nrm, n1)
            bank = cring.take()
            for h_ in range(HN):
                mm = product(bank.ap[:, h_ * B:(h_ + 1) * B],
                             [(d1[:, k, h_ * P:(h_ + 1) * P], tT[:, k, :]) for k in range(KC)], c1, ctok, bank.after)
            prior["tT"] = [mm]
            a1 = dve.do(lambda e, bank=bank: e.tensor_tensor(
                hid[:, :, :], bank.ap[:, 0:HN * B].rearrange("p (h b) -> p h b", h=HN),
                d1b[:, :].unsqueeze(2).to_broadcast([P, HN, B]), ALU.add), mm, *prior["hid"])
            bank.free(a1)
            a2 = act.do(lambda e: e.activation(hid2[:, :, :], hid[:, :, :], ACT.Gelu), a1, *prior["hid2"])
            prior["hid"] = [a2]
            next(back, None)
            bank = cring.take()
            mm = product(bank.ap[0:B, 0:D], [(hid2[:, h_, :], d2[:, h_, :]) for h_ in range(HN)], a2, bank.after)
            prior["hid2"] = [mm]
            b1 = dve.do(lambda e, bank=bank: e.tensor_tensor(th[:, :], bank.ap[0:B, 0:D], th[:, :], ALU.add), mm, thr)
            bank.free(b1)
            thr = dve.do(lambda e: e.tensor_tensor(th[:, :], th[:, :], rows["d2_b"][:, :], ALU.add), b1)
        bank, mm = linear(bc, columns(th, thr))
        b4 = dve.do(lambda e, bank=bank: e.tensor_tensor(bc4[:, :], bank.ap[0:B, 0:D], rows["bc_b"][:, :], ALU.add), mm)
        bank.free(b4)
        b_ready = []
        for b in range(B):
            bank = cring.take()
            mm = product(bank.ap[:, 0:D], [(sel[:, b, :], bc4[:, :])], b4, sel_ready, bank.after)
            c = act.do(lambda e, b=b, bank=bank: e.activation(bcast[:, b, :], bank.ap[:, 0:D], ACT.Copy), mm)
            bank.free(c)
            b_ready.append(c)
        for _ in back:
            pass

        oflag = Flag(sem(f"p{ph}_out"))
        otok = None
        for b in range(B):
            tiles = [b * T + t for t in range(T)]
            ready = []
            for i in tiles:
                s = act.do(lambda e, i=i: e.activation(gt[:, i, :], gt[:, i, :], ACT.Sigmoid), g_ready[i])
                m = dve.do(lambda e, i=i, b=b: e.tensor_tensor(gt[:, i, :], gt[:, i, :], bcast[:, b, :], ALU.mult),
                           s, b_ready[b])
                ready.append([dve.do(lambda e, i=i: e.tensor_tensor(u[:, i, :], u[:, i, :], gt[:, i, :], ALU.add), m)])
            rs = norm2.run([u[:, i, :] for i in tiles], FFN_EPS, ready)
            for t, i in enumerate(tiles):
                a = dve.do(lambda e, t=t, i=i: e.tensor_scalar(
                    u[:, i, :], u[:, i, :], norm2.mv[:, t, 0:1], norm2.rs[:, t:t + 1], ALU.subtract, ALU.mult), rs)
                m = dve.do(lambda e, i=i: e.tensor_tensor(u[:, i, :], u[:, i, :], og[:, :], ALU.mult), a, og_h)
                r1 = pool.do(lambda e, i=i: e.tensor_tensor(res[:, i, :], res[:, i, :], ob_[:, :], ALU.add),
                             ob_h, res_ready[i], u_ready[i])
                res_ready[i] = dve.do(lambda e, i=i: e.tensor_tensor(res[:, i, :], res[:, i, :], u[:, i, :], ALU.add),
                                      m, r1)
            norm2.read = [a]
            if final:
                otok = oflag.dma(sp, out[b].rearrange("(t p) d -> p t d", p=P), res[:, b * T:(b + 1) * T, :],
                                 [res_ready[i] for i in tiles])
        if final:
            sp.fence(otok)
        stack.close()

    saved_tokens = []
    plan = ["moe_attn", "moe", "small", "moe_attn", "moe", "thought", "window", "thought"][:phases]
    for ph, what in enumerate(plan):
        if what == "moe_attn":
            attention_phase(ph, False, None)
        elif what == "moe":
            moe_phase(ph, None)
        elif what == "small":
            small_attention_phase(ph)
        elif what == "window":
            attention_phase(ph, True, None)
        else:
            thought_phase(ph, ph == 7)
    if len(plan) < 8:
        oflag = Flag(sem("dbg"))
        for b in range(B):
            otok = oflag.dma(sp, out[b].rearrange("(t p) d -> p t d", p=P), res[:, b * T:(b + 1) * T, :],
                             [res_ready[b * T + t] for t in range(T)])
        sp.fence(otok)

    with nc.Block() as block:
        block.sync(sp.play)
        block.gpsimd(pool.play)
        block.vector(dve.play)
        block.scalar(act.play)
        block.tensor(pe.play)
    ctx.close()


_PHASES = 8


def _rope_tables():
    f = np.float32
    pos = np.arange(S, dtype=f)[:, None]
    inv0 = f(1.0) / (f(150000.0) ** (np.arange(32, dtype=f) / f(32)))
    a0 = pos * inv0
    a0 = np.concatenate([a0, a0], -1)
    scale1 = f(10000.0) ** (np.arange(0, 128, 2, dtype=f) / f(128))
    a1 = pos / scale1[None, :]
    a1 = np.concatenate([a1, a1], -1)

    def signed(s):
        h = s.shape[1] // 2
        return np.concatenate([-s[:, :h], s[:, h:]], -1)
    return {"rope0_cos": np.cos(a0), "rope0_sin": signed(np.sin(a0)),
            "rope1_cos": np.cos(a1), "rope1_sin": signed(np.sin(a1))}


def kernel(**inputs):
    import concourse.bacc as bacc
    from concourse.bass_utils import run_bass_kernel_spmd

    nc = bacc.Bacc("TRN2", target_bir_lowering=False, num_devices=1)
    arrays, io = {}, {}
    for name, value in {**inputs, **_rope_tables()}.items():
        a = np.ascontiguousarray(value)
        arrays[f"in_{name}"] = a
        io[name] = nc.dram_tensor(f"in_{name}", a.shape, mybir.dt.from_np(a.dtype), kind="ExternalInput").ap()
    out = nc.dram_tensor("out", (B, S, D), mybir.dt.float32, kind="ExternalOutput").ap()
    build(nc, io, out, _PHASES)
    r = run_bass_kernel_spmd(nc, [arrays], core_ids=[0])
    return r.results[0]["out"]
```

```python
import numpy as np
import concourse.bass as bass
from concourse import mybir
from contextlib import ExitStack

P = 128
B, S, D = 4, 512, 256
T = S // P
NT = B * T
KC = D // P
E, TOPK, H = 16, 4, 256
HC = H // P
KV = 4
NEG = -1e30
LN_EPS, RMS_EPS, FFN_EPS = 1e-5, 1e-5, 1e-6
BANK = 512
NU = 4
QW = 512
KW = 128
SH, SKV, SD = 32, 8, 8
PARTS = 3
SENT = (-3.0e38, -3.1e38, -3.2e38, -3.3e38)


class Lane:

    def __init__(self, name, sem):
        self.name, self.sem, self.done, self.queue, self.seen = name, sem, 0, [], {}
        self.one_by_one = name == "pool"

    def waits(self, after):
        need = {}
        stack = list(after)
        while stack:
            t = stack.pop()
            if t is None:
                continue
            if isinstance(t, list):
                stack.extend(t)
            elif t[1] > max(need.get(t[0], (0, 0))[1], self.seen.get(t[0], 0)):
                need[t[0]] = t
        for k, t in need.items():
            self.seen[k] = t[1]
        return list(need.values())

    def do(self, emit, *after, signal=True):
        if self.one_by_one and self.done:
            after = (*after, self.last())
        self.queue.append((self.waits(after), emit, self.sem if signal else None, 1))
        if signal:
            self.done += 1
            return (self.sem, self.done)
        return None

    def fence(self, *after):
        self.queue.append((self.waits(after), None, None, 0))

    def last(self):
        return (self.sem, self.done)

    def play(self, eng):
        for waits, emit, sem, n in self.queue:
            for s, v in waits:
                eng.wait_ge(s, v)
            if emit is not None:
                ins = emit(eng)
                if sem is not None:
                    ins.then_inc(sem, n)


class Flag:

    def __init__(self, sem):
        self.sem, self.n = sem, 0

    def dma(self, lane, out, in_, *after, by_element=False):
        lane.queue.append((lane.waits(after), lambda e: e.dma_start(out, in_, allow_slow_non_contiguous=by_element),
                           self.sem, 16))
        self.n += 16
        return (self.sem, self.n)


class Slot:
    def __init__(self, ap, after, flag=None):
        self.ap, self.after, self.flag, self.users = ap, after, flag, None

    def free(self, *tokens):
        self.users = (self.users or []) + list(tokens)


class Ring:

    def __init__(self, aps, flags=None):
        self.slots, self.n = [Slot(a, [], f) for a, f in zip(aps, flags or [None] * len(aps))], 0
        for s in self.slots:
            s.users = []

    def take(self):
        i = self.n % len(self.slots)
        old = self.slots[i]
        assert old.users is not None, "a buffer is taken before its last use is queued"
        self.slots[i] = Slot(old.ap, old.users, old.flag)
        self.n += 1
        return self.slots[i]


def build(nc, io, out, phases=8):
    F32, F32R, BF16 = mybir.dt.float32, mybir.dt.float32r, mybir.dt.bfloat16
    ALU, ACT, AX = mybir.AluOpType, mybir.ActivationFunctionType, mybir.AxisListType
    ctx = ExitStack()

    def sem(name):
        return ctx.enter_context(nc.semaphore(name))

    pe, act, dve, pool, sp = (Lane(n, sem(n + "_done")) for n in ("pe", "act", "dve", "pool", "sp"))
    lanes = (pe, act, dve, pool)
    banks = [ctx.enter_context(nc.psum_tensor(f"bank{i}", [P, BANK], F32)) for i in range(8)]

    def allocator(stack, prefix):
        def sb(name, shape, dt=F32):
            return stack.enter_context(nc.sbuf_tensor(f"{prefix}_{name}", shape, dt))
        return sb

    top = allocator(ctx, "g")

    res = top("res", [P, NT, D])
    ident = top("ident", [P, P])
    identb = top("identb", [P, P], BF16)
    half = top("minus_half", [P, NT])
    STAGE_W = 1536
    stage_mem = [top(f"stage{i}", [P, STAGE_W]) for i in range(2)]
    stage = Ring([m[:, :] for m in stage_mem], [Flag(sem(f"stage{i}")) for i in range(2)])
    res_saved = nc.dram_tensor("res_saved", (NT, P, D), F32, kind="Internal").ap()
    parts_saved = nc.dram_tensor("parts_saved", (2, PARTS, D + SKV * SD, S), BF16, kind="Internal").ap()

    def make_ident(m):
        z = pool.do(lambda e: e.memset(m[:, :], 0.0))
        return pool.do(lambda e: e.affine_select(out=m[:, :], in_=m[:, :], compare_op=ALU.not_equal, fill=1.0,
                                                 base=0, pattern=[[-1, P]], channel_multiplier=1), z)
    ident_made = [make_ident(ident), make_ident(identb)]
    half_made = pool.do(lambda e: e.memset(half[:, :], -0.5))
    res_flag = Flag(sem("res_load"))
    loaded = None
    x_tiles = io["L0_attn_hidden_states"].rearrange("b (t p) d -> (b t) p d", p=P)
    for b in range(B):
        bt = slice(b * T, b * T + T)
        loaded = res_flag.dma(sp, res[:, bt, :], x_tiles[bt].rearrange("t p d -> p t d"))
    res_ready = [loaded for _ in range(NT)]
    res_read = [[] for _ in range(NT)]
    pe.fence(ident_made)

    def fetch(pieces):
        slot = stage.take()
        for rows, view, src in pieces:
            slot.token = slot.flag.dma(sp, view(slot.ap[rows, :]), src, slot.after)
        return slot

    def split(slot, width, hi, lo, *after):
        raw = slot.ap[:, 0:width]
        h = act.do(lambda e: e.activation(hi, raw, ACT.Copy), slot.token, *after)
        l = pool.do(lambda e: e.tensor_tensor(lo, raw, hi.bitcast(F32), ALU.subtract), h, *after)
        slot.free(h, l)
        return [h, l]

    def chunks(src):
        return src.rearrange("(c p) n -> p c n", p=P)

    def into(c0, cols, width):
        return lambda a: a[:, 0:KC * width].rearrange("p (c n) -> p c n", c=KC)[:, :, c0:c0 + cols]

    def product(out_ap, pairs, *after):
        tok = None
        for n, (l, r) in enumerate(pairs):
            last = n == len(pairs) - 1
            tok = pe.do(lambda e, l=l, r=r, n=n, last=last: e.matmul(out_ap, l, r, start=(n == 0), stop=last),
                        *(after if n == 0 else ()), signal=last)
        return tok

    def three(lh, ll, rh, rl):
        return [(lh, rh), (ll, rh), (lh, rl)]

    def transpose(out_ap, in_ap, n, *after, signal=True):
        return pe.do(lambda e: e.transpose(out_ap, in_ap, ident[0:n, 0:n]), *after, signal=signal)

    class Norm:

        def __init__(self, sb, name, parts=P, tiles=T):
            self.p, self.n = parts, tiles
            self.st = sb(name + "_st", [parts, tiles, 6])
            self.mv = sb(name + "_mv", [parts, tiles, 2])
            self.ve = sb(name + "_ve", [parts, tiles])
            self.rs = sb(name + "_rs", [parts, tiles])
            self.read = []

        def run(self, tiles, eps, ready):
            agg = []
            for i, x in enumerate(tiles):
                s = dve.do(lambda e, i=i, x=x: e.bn_stats(self.st[:, i, :], x), ready[i], *self.read)
                agg.append((i, s))
            done = [dve.do(lambda e, i=i: e.bn_aggr(self.mv[:, i, :], self.st[:, i, :]), s) for i, s in agg]
            v = dve.do(lambda e: e.tensor_scalar(self.ve[:, :], self.mv[:, :, 1], eps, None, ALU.add), done)
            r = pool.do(lambda e: e.tensor_tensor(self.rs[:, :], self.ve[:, :], half[0:self.p, 0:self.n], ALU.pow), v,
                        half_made)
            self.read = [v]
            return r

    def feature_major(*args):
        steps = feature_major_steps(*args)
        while True:
            try:
                next(steps)
            except StopIteration as end:
                return end.value

    def feature_major_steps(src, ready, ring, hi, lo, scale, *after):
        toks, reads = [], []
        for c in range(KC):
            bank = ring.take()
            for t in range(T):
                tt = transpose(bank.ap[:, t * P:(t + 1) * P], src(t)[:, c * P:(c + 1) * P], P,
                               ready[t], bank.after, signal=t == T - 1)
            reads.append(tt)
            sc = scale[:, c:c + 1] if scale is not None else 1.0
            h = act.do(lambda e, c=c, bank=bank, sc=sc: e.activation(hi[:, c, :], bank.ap, ACT.Copy, scale=sc), tt, *after)
            l = dve.do(lambda e, c=c, bank=bank, sc=sc: e.scalar_tensor_tensor(
                lo[:, c, :], bank.ap, sc, hi[:, c, :].bitcast(F32), ALU.mult, ALU.subtract), h, *after)
            bank.free(h, l)
            toks += [h, l]
            yield
        return toks, reads

    def attention_phase(ph, wide, pre):
        stack = ExitStack()
        sb = allocator(stack, f"p{ph}")
        hd = 128 if wide else 64
        nk = KW // hd
        nh = QW // hd
        n = "L1_attn_" if wide else "L0_ffn_"
        wq, wk, wv = (io[n + a] for a in (("q_kernel", "k_kernel", "v_kernel") if wide else ("wq", "wk", "wv")))
        wo = io["L1_attn_out_kernel"] if wide else io["L0_ffn_wo"]
        cs_dram, sn_dram = (io["rope1_cos"], io["rope1_sin"]) if wide else (io["rope0_cos"], io["rope0_sin"])
        scale = 1.0 / float(np.sqrt(hd))
        fence = [l.last() for l in lanes]

        aT_hi, aT_lo = (sb(f"aT_{s}", [P, B, KC, S], F32R) for s in ("hi", "lo"))
        w_hi, w_lo = (sb(f"w_{s}", [P, 2, KC * (QW + 2 * KW)], F32R) for s in ("hi", "lo"))
        o_hi, o_lo = (sb(f"o_{s}", [P, 2, KV * D], F32R) for s in ("hi", "lo"))
        cs = sb("cos", [P, T, hd])
        sn = sb("sin", [P, T, hd])
        lnw = sb("lnw", [P, KC])
        mask = sb("mask", [P, 2 * P], BF16)
        rope_a = Ring([sb(f"rope_a{i}", [P, QW + KW])[:, :] for i in range(2)])
        rope_b = Ring([sb(f"rope_b{i}", [P, QW + KW])[:, :] for i in range(1)])
        tm = Ring([sb(f"tm{i}", [P, QW + nk * P])[:, :] for i in range(2)])
        v_sb = Ring([sb(f"v{i}", [P, T, KW])[:, :, :] for i in range(3)])
        q_st = Ring([sb(f"q{i}", [P, 8, P], F32R)[:, :, :] for i in range(5)])
        k_st = Ring([sb(f"k{i}", [P, 2, 2, S], F32R)[:, :, :, :] for i in range(2)])
        prob = Ring([sb(f"prob{i}", [P, S])[:, :] for i in range(8)])
        prT = Ring([sb(f"prT{i}", [P, KV * P])[:, :] for i in range(8)])
        oT_hi, oT_lo = (Ring([sb(f"oT_{s}{i}", [P, KV * P], F32R)[:, :] for i in range(1)]) for s in ("hi", "lo"))
        small = Ring([sb(f"small{i}", [P, 3, KV])[:, :, :] for i in range(3)])
        norm = Norm(sb, "ln")
        r2 = sb("rms", [P, T])
        n_tile = Ring([sb(f"n_tile{i}", [P, D])[:, :] for i in range(4)])
        sring, tring, wring = Ring([b[:, :] for b in banks[0:3]]), Ring([b[:, :] for b in banks[3:5]]), \
            Ring([b[:, :] for b in banks[5:8]])

        cflag = Flag(sem(f"p{ph}_const"))
        ctok = cflag.dma(sp, cs[:, :, :], cs_dram.rearrange("(t p) d -> p t d", p=P), fence)
        ctok = cflag.dma(sp, sn[:, :, :], sn_dram.rearrange("(t p) d -> p t d", p=P), fence)
        if not wide:
            ctok = cflag.dma(sp, lnw[:, :], io["L0_ffn_ln_w"].rearrange("(c p) -> p c", p=P), fence,
                             by_element=True)
        for l in lanes:
            l.fence(fence)
        mz = pool.do(lambda e: e.memset(mask[:, :], 0.0))
        m1 = pool.do(lambda e: e.affine_select(out=mask[:, P:], in_=mask[:, P:], compare_op=ALU.is_ge, fill=NEG,
                                               base=0, pattern=[[-1, P]], channel_multiplier=1), mz)
        m2 = pool.do(lambda e: e.affine_select(out=mask[:, :P], in_=mask[:, :P], compare_op=ALU.is_ge, fill=NEG,
                                               base=0, pattern=[[1, P]], channel_multiplier=-1), mz)
        pe.fence(m1, m2)

        WQKV = QW + 2 * KW

        def fetch_qkv(c):
            return fetch([(slice(0, P), into(0, QW, WQKV), chunks(wq[:, c * QW:(c + 1) * QW])),
                          (slice(0, P), into(QW, KW, WQKV), chunks(wk[:, c * KW:(c + 1) * KW])),
                          (slice(0, P), into(QW + KW, KW, WQKV), chunks(wv[:, c * KW:(c + 1) * KW]))])

        def fetch_o(c):
            rows = KV * hd
            return fetch([(slice(i * hd, (i + 1) * hd),
                           lambda a: a[:, 0:KV * D].rearrange("p (j n) -> p j n", j=KV),
                           wo[c * QW + i * rows:c * QW + (i + 1) * rows, :].rearrange("(j d) n -> d j n", d=hd))
                          for i in range(nk)])

        w_ready, o_ready, w_used, o_used = {}, {}, {}, {}

        def split_qkv(c, slot):
            w_ready[c] = split(slot, KC * WQKV, w_hi[:, c % 2, :], w_lo[:, c % 2, :], w_used.get(c - 2))

        def split_o(c, slot):
            o_ready[c] = split(slot, KV * D, o_hi[:, c % 2, :], o_lo[:, c % 2, :], o_used.get(c - 2))

        slot_qkv, slot_o = pre or (fetch_qkv(0), fetch_o(0))
        split_qkv(0, slot_qkv)
        split_o(0, slot_o)

        aT_ready = {}
        saves = [Flag(sem(f"p{ph}_save{b}")) for b in range(0 if wide else B)]

        def norm_batch(b):
            tiles = [b * T + t for t in range(T)]
            ready = [[res_ready[i]] for i in tiles]
            rs = norm.run([res[:, i, :] for i in tiles], LN_EPS, ready)
            done = []
            if not wide:
                save = saves[b].dma(sp, res_saved[b * T:(b + 1) * T].rearrange("t p d -> p t d"),
                                 res[:, b * T:(b + 1) * T, :], ready)
                saved_tokens[b:b + 1] = [save]
                a1 = dve.do(lambda e: e.tensor_tensor(r2[:, :], norm.mv[:, :, 1], norm.rs[:, :], ALU.mult), rs, *norm_reads)
                a2 = dve.do(lambda e: e.tensor_tensor(norm.ve[:, :], r2[:, :], norm.rs[:, :], ALU.mult), a1)
                a3 = dve.do(lambda e: e.tensor_scalar(norm.ve[:, :], norm.ve[:, :], RMS_EPS, None, ALU.add), a2)
                rr = pool.do(lambda e: e.tensor_tensor(r2[:, :], norm.ve[:, :], half[:, 0:T], ALU.pow), a3)
                srcs = []
                for t, i in enumerate(tiles):
                    u = dve.do(lambda e, t=t, i=i: e.tensor_scalar(
                        res[:, i, :], res[:, i, :], norm.mv[:, t, 0:1], norm.rs[:, t:t + 1],
                        ALU.subtract, ALU.mult), rs, ready[t], save)
                    res_ready[i] = u
                    nt = n_tile.take()
                    h = act.do(lambda e, t=t, i=i, nt=nt: e.activation(nt.ap, res[:, i, :], ACT.Copy,
                                                                      scale=r2[:, t:t + 1]), u, rr, nt.after)
                    srcs.append((nt, h))
                norm_reads[:] = [srcs[-1][1]]
                norm.read = [srcs[-1][1], u]
            else:
                srcs = []
                for t, i in enumerate(tiles):
                    nt = n_tile.take()
                    h = dve.do(lambda e, t=t, i=i, nt=nt: e.tensor_scalar(
                        nt.ap, res[:, i, :], norm.mv[:, t, 0:1], norm.rs[:, t:t + 1],
                        ALU.subtract, ALU.mult), rs, ready[t], nt.after)
                    srcs.append((nt, h))
                norm.read = [srcs[-1][1]]
            yield
            toks, reads = feature_major(lambda t: srcs[t][0].ap, [s[1] for s in srcs], tring,
                                        aT_hi[:, b], aT_lo[:, b], None if wide else lnw, ctok)
            for nt, _ in srcs:
                nt.free(*reads)
            aT_ready[b] = toks

        norm_reads = []

        class Unit:
            pass

        def prepare(c, b, unit):
            if c == 0:
                for _ in normed.pop(b):
                    pass
            unit.k, unit.v = k_st.take(), v_sb.take()
            unit.q, unit.q_tok, unit.k_tok, unit.v_tok = [], [], [], []
            rotated = {}
            for t in range(T + 1):
                if t < T:
                    yield from products_of(c, b, unit, t, rotated)
                if t:
                    yield from turned(unit, t - 1, rotated[t - 1])

        def products_of(c, b, unit, t, rotated):
            whi = w_hi[:, c % 2, :].rearrange("p (k n) -> p k n", k=KC)
            wlo = w_lo[:, c % 2, :].rearrange("p (k n) -> p k n", k=KC)
            tok = slice(t * P, (t + 1) * P)

            def project(bank, c0, cols):
                pairs = []
                for k in range(KC):
                    pairs += three(aT_hi[:, b, k, tok], aT_lo[:, b, k, tok],
                                   whi[:, k, c0:c0 + cols], wlo[:, k, c0:c0 + cols])
                return product(bank.ap[:, 0:cols], pairs, aT_ready[b], w_ready[c], bank.after)
            qb = wring.take()
            qp = project(qb, 0, QW)
            yield
            ra, rb, tb = rope_a.take(), rope_b.take(), tm.take()
            hf = hd // 2

            def rotate(bank, ready, width, at):
                heads = width // hd
                x = bank.ap[:, 0:width].rearrange("p (h d) -> p h d", d=hd)
                a = ra.ap[:, at:at + width].rearrange("p (h d) -> p h d", d=hd)
                bb = rb.ap[:, at:at + width].rearrange("p (h d) -> p h d", d=hd)

                def table(m, lo_, hi_):
                    return m[:, t, lo_:hi_].unsqueeze(1).to_broadcast([P, heads, hi_ - lo_])
                c_all, s_left, s_right = table(cs, 0, hd), table(sn, 0, hf), table(sn, hf, hd)
                r1 = dve.do(lambda e: e.tensor_tensor(a, x, c_all, ALU.mult), ready, ctok, ra.after)
                r2_ = dve.do(lambda e: e.tensor_tensor(bb[:, :, 0:hf], x[:, :, hf:hd], s_left, ALU.mult),
                             ready, rb.after)
                r3 = dve.do(lambda e: e.tensor_tensor(bb[:, :, hf:hd], x[:, :, 0:hf], s_right, ALU.mult),
                            ready, rb.after)
                return [r1, r2_, r3]
            qr = rotate(qb, qp, QW, 0)
            qb.free(*qr)
            kb = wring.take()
            kp = project(kb, QW, 2 * KW)
            yield
            kr = rotate(kb, kp, KW, QW)
            w_used[c] = kp
            sums = [pool.do(lambda e, ra=ra, rb=rb, tb=tb: e.tensor_tensor(
                tb.ap[:, 0:QW], ra.ap[:, 0:QW], rb.ap[:, 0:QW], ALU.add), qr, tb.after)]
            k_to = tb.ap[:, QW:QW + nk * P].rearrange("p (g r d) -> p g r d", g=nk, r=nk)
            k_a, k_b = (r.ap[:, QW:QW + KW].rearrange("p (g d) -> p g d", g=nk).unsqueeze(2)
                        .to_broadcast([P, nk, nk, hd]) for r in (ra, rb))
            sums.append(pool.do(lambda e, k_to=k_to, k_a=k_a, k_b=k_b: e.tensor_tensor(k_to, k_a, k_b, ALU.add),
                                kr, tb.after))
            ra.free(sums[-1])
            rb.free(sums[-1])
            rotated[t] = tb, sums
            yield
            vc = act.do(lambda e, t=t, kb=kb: e.activation(unit.v.ap[:, t, :], kb.ap[:, KW:2 * KW], ACT.Copy),
                        kr, unit.v.after)
            kb.free(vc, *kr)
            unit.v_tok.append(vc)
            yield

        def turned(unit, t, made_by):
            tb, sums = made_by
            tok = slice(t * P, (t + 1) * P)
            tq, q = wring.take(), q_st.take()
            for j in range(QW // P):
                qt = transpose(tq.ap[:, j * P:(j + 1) * P], tb.ap[:, j * P:(j + 1) * P], P, sums, tq.after,
                               signal=j == QW // P - 1)
            xq = tq.ap.rearrange("p (j n) -> p j n", j=QW // P)
            if wide:
                hs = [act.do(lambda e: e.activation(q.ap[:, 0:4, :], xq, ACT.Copy), qt, q.after)]
                yield
                ls = [dve.do(lambda e: e.tensor_tensor(q.ap[:, 4:8, :], xq, q.ap[:, 0:4, :].bitcast(F32),
                                                       ALU.subtract), hs, q.after)]
            else:
                qv = q.ap.rearrange("p (j s) n -> p j s n", s=2)
                halves = [xq[0:hd], xq[hd:P]]
                hs = [act.do(lambda e, s=s: e.activation(qv[0:hd, :, s, :], halves[s], ACT.Copy), qt, q.after)
                      for s in range(2)]
                yield
                ls = [dve.do(lambda e, s=s: e.tensor_tensor(
                    qv[hd:P, :, s, :], halves[s], qv[0:hd, :, s, :].bitcast(F32), ALU.subtract), hs, q.after)
                    for s in range(2)]
            made = hs + ls
            tq.free(*made)
            tk = wring.take()
            for g in range(nk):
                kt = transpose(tk.ap[:, g * P:(g + 1) * P], tb.ap[:, QW + g * P:QW + (g + 1) * P], P, sums,
                               tk.after, signal=g == nk - 1)
            tb.free(kt)
            xk = tk.ap[:, 0:nk * P].rearrange("p (g n) -> p g n", g=nk)
            h = act.do(lambda e: e.activation(unit.k.ap[:, 0, 0:nk, tok], xk, ACT.Copy, scale=scale),
                       kt, unit.k.after)
            yield
            l = dve.do(lambda e: e.scalar_tensor_tensor(
                unit.k.ap[:, 1, 0:nk, tok], xk, scale, unit.k.ap[:, 0, 0:nk, tok].bitcast(F32),
                ALU.mult, ALU.subtract), h, unit.k.after)
            tk.free(h, l)
            unit.q.append(q)
            unit.q_tok.append(made)
            unit.k_tok += [h, l]
            yield
            yield

        class Group:
            pass

        def group(c, b, unit, t, g):
            o = Group()
            o.c, o.b, o.u, o.t, o.g = c, b, unit, t, g
            o.k0 = max(0, t - 1) if wide else 0
            o.nkt = t + 1 - o.k0
            o.probs, o.exps = [], []
            o.sm = small.take()
            return o

        def scores(o, j):
            keys = slice(o.k0 * P, (o.t + 1) * P)
            w = o.nkt * P
            bank, pr = sring.take(), prob.take()
            q, k = o.u.q[o.t].ap, o.u.k.ap
            khi, klo = k[:, 0, o.g, keys], k[:, 1, o.g, keys]
            if wide:
                pairs = three(q[:, j, :], q[:, 4 + j, :], khi, klo)
            else:
                head = o.g * KV + j
                pairs = [(q[:, head, :], khi), (q[:, head, :], klo)]
            for n_, (l, r) in enumerate(pairs):
                pe.do(lambda e, l=l, r=r, n_=n_: e.matmul(bank.ap[:, 0:w], l, r, start=(n_ == 0), stop=False),
                      o.u.q_tok[o.t], o.u.k_tok[0:2 * (o.t + 1)], bank.after, signal=False)
            mw = min(w, 2 * P) if wide else P
            done = pe.do(lambda e: e.matmul(bank.ap[:, w - mw:w], identb[:, :], mask[:, 2 * P - mw:2 * P],
                                            start=False, stop=True))
            sm = o.sm.ap
            mx = dve.do(lambda e: e.tensor_reduce(sm[:, 0, j:j + 1], bank.ap[:, 0:w], axis=AX.X, op=ALU.max,
                                                  negate=True), done, o.sm.after)
            ex = act.do(lambda e: e.activation(pr.ap[:, 0:w], bank.ap[:, 0:w], ACT.Exp, bias=sm[:, 0, j:j + 1],
                                               accum_out=sm[:, 1, j:j + 1]), mx, pr.after, o.sm.after)
            bank.free(mx, ex)
            o.probs.append(pr)
            o.exps.append(ex)
            o.score_tok = done

        def normalise(o):
            w = o.nkt * P
            sm = o.sm.ap
            r = dve.do(lambda e: e.reciprocal(sm[:, 2, :], sm[:, 1, :]), o.exps)
            o.norms = [dve.do(lambda e, j=j: e.tensor_scalar(o.probs[j].ap[:, 0:w], o.probs[j].ap[:, 0:w],
                                                             sm[:, 2, j:j + 1], None, ALU.mult), r, o.exps[j])
                       for j in range(KV)]
            o.sm.free(*o.norms)
            o.prT, o.prT_tok = [], []

        evacs = [0]

        def turn(o, kt):
            bank, dst = tring.take(), prT.take()
            for j in range(KV):
                tt = transpose(bank.ap[:, j * P:(j + 1) * P], o.probs[j].ap[:, kt * P:(kt + 1) * P], P,
                               o.norms[j], bank.after, signal=j == KV - 1)
            if kt == o.nkt - 1:
                for pr in o.probs:
                    pr.free(tt)
            evacs[0] += 1
            if evacs[0] % 1000000 == 0:
                cp = dve.do(lambda e: e.tensor_copy(dst.ap, bank.ap), tt, dst.after)
            else:
                cp = act.do(lambda e: e.activation(dst.ap, bank.ap, ACT.Copy), tt, dst.after)
            bank.free(cp)
            o.prT.append(dst)
            o.prT_tok.append(cp)

        def weigh(os):
            bank = wring.take()
            first = os[0]
            for kt in range(first.nkt):
                for o in os:
                    rows = slice(o.g * hd, (o.g + 1) * hd)
                    last = kt == first.nkt - 1 and o is os[-1]
                    tok = pe.do(lambda e, o=o, rows=rows, kt=kt: e.matmul(
                        bank.ap[rows, :], o.u.v.ap[:, o.k0 + kt, o.g * hd:(o.g + 1) * hd], o.prT[kt].ap,
                        start=kt == 0, stop=kt == o.nkt - 1),
                        o.prT_tok[kt], o.u.v_tok[0:o.t + 1], bank.after, signal=last)
            for o in os:
                for s in o.prT:
                    s.free(tok)
            hi, lo = oT_hi.take(), oT_lo.take()
            h = act.do(lambda e: e.activation(hi.ap, bank.ap, ACT.Copy), tok, hi.after)
            for o in os:
                if o.g == nk - 1 and o.t == T - 1:
                    o.u.v.free(tok)
            return first, bank, hi, lo, h

        def low_parts(w):
            o, bank, hi, lo, h = w
            l = dve.do(lambda e: e.tensor_tensor(lo.ap, bank.ap, hi.ap.bitcast(F32), ALU.subtract), h, lo.after)
            bank.free(h, l)
            return o, hi, lo, [h, l]

        def project_out(w):
            o, hi, lo, ready = w
            bank = wring.take()
            ohi = o_hi[:, o.c % 2, :].rearrange("p (j n) -> p j n", j=KV)
            olo = o_lo[:, o.c % 2, :].rearrange("p (j n) -> p j n", j=KV)
            pairs = []
            for j in range(KV):
                cols = slice(j * P, (j + 1) * P)
                pairs += three(hi.ap[:, cols], lo.ap[:, cols], ohi[:, j, :], olo[:, j, :])
            tok = product(bank.ap[:, 0:D], pairs, ready, o_ready[o.c], bank.after)
            hi.free(tok)
            lo.free(tok)
            o_used[o.c] = tok
            i = o.b * T + o.t
            add = dve.do(lambda e: e.tensor_tensor(res[:, i, :], bank.ap[:, 0:D], res[:, i, :], ALU.add),
                         tok, res_ready[i])
            bank.free(add)
            res_ready[i] = add

        units = [(c, b) for c in range(NU) for b in range(B)]
        normed = {b: norm_batch(b) for b in range(B)}
        made = Unit()
        for _ in prepare(0, 0, made):
            pass
        next(normed[1])
        prev = None
        pend, full = [], None
        for n_u, (c, b) in enumerate(units):
            unit = made
            made = Unit()
            nxt = units[n_u + 1] if n_u + 1 < len(units) else None
            if b == 1 and c + 1 < NU:
                slot_qkv, slot_o = fetch_qkv(c + 1), fetch_o(c + 1)
            if b == 2 and c + 1 < NU:
                split_qkv(c + 1, slot_qkv)
                split_o(c + 1, slot_o)
            back = prepare(*nxt, made) if nxt else iter(())
            steps = [(t, g) for t in range(T) for g in range(nk)]
            pieces = 8 * T // (KV * len(steps))

            def beside():
                for _ in range(pieces):
                    next(back, None)
            for t, g in steps:
                if (t, g) == steps[-1] and c == 0 and b + 2 < B:
                    next(normed[b + 2])
                cur = group(c, b, unit, t, g)
                nturn = prev.nkt if prev else 0
                scores(cur, 0)
                weighed = weigh(full) if full else None
                if prev:
                    normalise(prev)
                beside()
                scores(cur, 1)
                if weighed:
                    weighed = low_parts(weighed)
                beside()
                for kt in range(0, min(2, nturn)):
                    turn(prev, kt)
                scores(cur, 2)
                beside()
                for kt in range(2, nturn):
                    turn(prev, kt)
                scores(cur, 3)
                if weighed:
                    project_out(weighed)
                beside()
                pend = pend + [prev] if prev else []
                full = None
                if prev and prev.g == nk - 1:
                    full, pend = pend, []
                if g == nk - 1:
                    unit.q[t].free(cur.score_tok)
                prev = cur
            unit.k.free(cur.score_tok)
            for _ in back:
                pass
        if full:
            project_out(low_parts(weigh(full)))
        normalise(prev)
        for kt in range(prev.nkt):
            turn(prev, kt)
        project_out(low_parts(weigh(pend + [prev])))
        stack.close()

    def moe_phase(ph, pre):
        stack = ExitStack()
        sb = allocator(stack, f"p{ph}")
        fence = [l.last() for l in lanes]
        hT_hi, hT_lo = (sb(f"hT_{s}", [P, B, KC, S], F32R) for s in ("hi", "lo"))
        w_hi, w_lo = (sb(f"w_{s}", [P, 2, 3 * KC * H], F32R) for s in ("hi", "lo"))
        xin = sb("xin", [P, NT, D])
        wg_raw = sb("wg", [P, KC, E])
        wg_hi, wg_lo = (sb(f"wg_{s}", [P, KC, E], F32R) for s in ("hi", "lo"))
        lnw = sb("lnw", [P, KC])
        sq = sb("sq", [P, D])
        ms, rs = sb("ms", [P, T]), sb("rs", [P, T])
        n_tile = Ring([sb(f"n_tile{i}", [P, D])[:, :] for i in range(4)])
        silu = Ring([sb(f"silu{i}", [P, S])[:, :] for i in range(3)])
        full = Ring([sb(f"full{i}", [P, S])[:, :] for i in range(3)])
        a_hi, a_lo = (Ring([sb(f"a_{s}{i}", [P, HC, S], F32R)[:, :, :] for i in range(2)]) for s in ("hi", "lo"))
        ext = sb("ext", [P, T, E + 4])
        rep = sb("rep", [P, T, E + 4])
        top8 = sb("top8", [P, T, 8])
        ex, sel, gate = sb("ex", [P, T, E]), sb("sel", [P, T, E]), sb("gate", [P, NT, E])
        gs = sb("gs", [P, 2, T])
        aring, yring = Ring([b[:, :] for b in banks[0:5]]), Ring([b[:, :] for b in banks[5:8]])

        cflag = Flag(sem(f"p{ph}_const"))
        cflag.dma(sp, wg_raw[:, :, :], chunks(io["L0_ffn_wg"]), fence)
        ctok = cflag.dma(sp, lnw[:, :], io["L0_ffn_ff_ln_w"].rearrange("(c p) -> p c", p=P), fence,
                             by_element=True)
        xflag = Flag(sem(f"p{ph}_x"))
        xtok = xflag.dma(sp, xin[:, :, :], res_saved.rearrange("t p d -> p t d"), fence, saved_tokens)
        for l in lanes:
            l.fence(fence)
        wgh = act.do(lambda e: e.activation(wg_hi[:, :, :], wg_raw[:, :, :], ACT.Copy), ctok)
        wgl = dve.do(lambda e: e.tensor_tensor(wg_lo[:, :, :], wg_raw[:, :, :], wg_hi[:, :, :].bitcast(F32),
                                               ALU.subtract), wgh, ctok)
        sent = [dve.do(lambda e, k=k: e.memset(ext[:, :, E + k], SENT[k])) for k in range(4)]

        w1, w3, w2 = io["L0_ffn_w1"], io["L0_ffn_w3"], io["L0_ffn_w2"]

        def fetch_e(e_):
            def at(i):
                return lambda a: a[:, i * KC * H:(i + 1) * KC * H].rearrange("p (c n) -> p c n", c=KC)
            return fetch([(slice(0, P), at(i), chunks(w[e_])) for i, w in enumerate((w1, w3, w2))])

        w_ready, w_used = {}, {}

        def split_e(e_, slot):
            w_ready[e_] = split(slot, 3 * KC * H, w_hi[:, e_ % 2, :], w_lo[:, e_ % 2, :], w_used.get(e_ - 2))

        slots = {0: pre or fetch_e(0)}
        slots[1] = fetch_e(1)
        hT_ready, gate_ready = {}, {}
        prior = {"sq": None, "ms": [], "small": []}

        def norm_batch(b):
            tiles = [b * T + t for t in range(T)]
            s = []
            for t, i in enumerate(tiles):
                q_ = act.do(lambda e, t=t, i=i: e.activation(sq[:, :], res[:, i, :], ACT.Square,
                                                             accum_out=ms[:, t:t + 1]),
                            res_ready[i], prior["sq"], *prior["ms"])
                prior["sq"] = q_
                s.append(q_)
            m = dve.do(lambda e: e.tensor_scalar(ms[:, :], ms[:, :], 1.0 / D, RMS_EPS, ALU.mult, ALU.add), s)
            r = pool.do(lambda e: e.tensor_tensor(rs[:, :], ms[:, :], half[:, 0:T], ALU.pow), m, *prior["ms"])
            srcs = []
            for t, i in enumerate(tiles):
                nt = n_tile.take()
                h = dve.do(lambda e, t=t, i=i, nt=nt: e.tensor_scalar(nt.ap, res[:, i, :], rs[:, t:t + 1], None,
                                                                     ALU.mult), r, nt.after)
                srcs.append((nt, h))
            prior["ms"] = [r, srcs[-1][1]]
            toks, reads = feature_major(lambda t: srcs[t][0].ap, [s_[1] for s_ in srcs], aring,
                                        hT_hi[:, b], hT_lo[:, b], lnw, ctok)
            for nt, _ in srcs:
                nt.free(*reads)
            hT_ready[b] = toks

        def route_batch(b):
            bank = aring.take()
            for t in range(T):
                cols = slice(t * P, (t + 1) * P)
                pairs = []
                for k in range(KC):
                    pairs += three(hT_hi[:, b, k, cols], hT_lo[:, b, k, cols], wg_hi[:, k, :], wg_lo[:, k, :])
                lg = product(bank.ap[:, t * E:(t + 1) * E], pairs, hT_ready[b], wgh, wgl, bank.after)
            prev_ = prior["small"]
            cp = dve.do(lambda e: e.tensor_copy(ext[:, :, 0:E], bank.ap[:, 0:T * E].rearrange("p (t e) -> p t e", t=T)),
                        lg, sent, *prev_)
            bank.free(cp)
            mx = [dve.do(lambda e, t=t: e.max(top8[:, t, :], ext[:, t, 0:E]), cp, *prev_) for t in range(T)]
            sub = dve.do(lambda e: e.tensor_tensor(ex[:, :, :], ext[:, :, 0:E],
                                                   top8[:, :, 0:1].to_broadcast([P, T, E]), ALU.subtract), mx)
            exp = act.do(lambda e: e.activation(ex[:, :, :], ex[:, :, :], ACT.Exp), sub)
            st = [dve.do(lambda e: e.tensor_copy(top8[:, :, 4:8], ext[:, :, E:E + 4]), mx, sent)]
            mr = [dve.do(lambda e, t=t: e.match_replace(rep[:, t, :], top8[:, t, :], ext[:, t, :], 3.0e38), st)
                  for t in range(T)]
            ne = dve.do(lambda e: e.tensor_tensor(sel[:, :, :], rep[:, :, 0:E], ext[:, :, 0:E], ALU.not_equal), mr)
            mu = dve.do(lambda e: e.tensor_tensor(ex[:, :, :], ex[:, :, :], sel[:, :, :], ALU.mult), ne, exp)
            sm = dve.do(lambda e: e.tensor_reduce(gs[:, 0, :], ex[:, :, :], axis=AX.X, op=ALU.add), mu)
            rc = dve.do(lambda e: e.reciprocal(gs[:, 1, :], gs[:, 0, :]), sm)
            g = dve.do(lambda e: e.tensor_tensor(gate[:, b * T:(b + 1) * T, :], ex[:, :, :],
                                                 gs[:, 1, :].unsqueeze(2).to_broadcast([P, T, E]), ALU.mult), rc)
            prior["small"] = [g]
            gate_ready[b] = g

        def up(e_, b):
            whi = w_hi[:, e_ % 2, :].rearrange("p (i k n) -> p i k n", i=3, k=KC)
            wlo = w_lo[:, e_ % 2, :].rearrange("p (i k n) -> p i k n", i=3, k=KC)
            hi, lo = a_hi.take(), a_lo.take()
            ready = []
            for m in range(HC):
                cols = slice(m * P, (m + 1) * P)
                got = []
                for i in range(2):
                    bank = aring.take()
                    pairs = []
                    for k in range(KC):
                        pairs += three(whi[:, i, k, cols], wlo[:, i, k, cols], hT_hi[:, b, k, :], hT_lo[:, b, k, :])
                    got.append((bank, product(bank.ap, pairs, hT_ready[b], w_ready[e_], bank.after)))
                (b1, t1), (b3, t3) = got
                s, f = silu.take(), full.take()
                sl = act.do(lambda e, s=s, b1=b1: e.activation(s.ap, b1.ap, ACT.Silu), t1, s.after)
                b1.free(sl)
                mu = dve.do(lambda e, s=s, f=f, b3=b3: e.tensor_tensor(f.ap, b3.ap, s.ap, ALU.mult), sl, t3, f.after)
                b3.free(mu)
                s.free(mu)
                h = act.do(lambda e, f=f, m=m: e.activation(hi.ap[:, m, :], f.ap, ACT.Copy), mu, hi.after)
                l = dve.do(lambda e, f=f, m=m: e.tensor_tensor(lo.ap[:, m, :], f.ap, hi.ap[:, m, :].bitcast(F32),
                                                               ALU.subtract), h, lo.after)
                f.free(h, l)
                ready += [h, l]
            return e_, b, hi, lo, ready

        def down(e_, b, hi, lo, ready):
            whi = w_hi[:, e_ % 2, :].rearrange("p (i k n) -> p i k n", i=3, k=KC)
            wlo = w_lo[:, e_ % 2, :].rearrange("p (i k n) -> p i k n", i=3, k=KC)
            for pair in range(0, T, 2):
                bank = yring.take()
                for t in (pair, pair + 1):
                    cols = slice(t * P, (t + 1) * P)
                    pairs = []
                    for m in range(HC):
                        pairs += three(hi.ap[:, m, cols], lo.ap[:, m, cols], whi[:, 2, m, :], wlo[:, 2, m, :])
                    tok = product(bank.ap[:, (t - pair) * D:(t - pair + 1) * D], pairs, ready, bank.after)
                for t in (pair, pair + 1):
                    i = b * T + t
                    y = bank.ap[:, (t - pair) * D:(t - pair + 1) * D]
                    add = dve.do(lambda e, y=y, i=i: e.scalar_tensor_tensor(
                        res[:, i, :], y, gate[:, i, e_:e_ + 1], res[:, i, :], ALU.mult, ALU.add),
                        tok, res_ready[i], gate_ready[b])
                    res_ready[i] = add
                    if e_ == E - 1:
                        res_ready[i] = dve.do(lambda e, i=i: e.scalar_tensor_tensor(
                            res[:, i, :], res[:, i, :], 0.5, xin[:, i, :], ALU.mult, ALU.add), add, xtok)
                bank.free(add)
            hi.free(tok)
            lo.free(tok)
            w_used[e_] = tok

        for b in range(B):
            norm_batch(b)
        split_e(0, slots[0])
        for b in range(B):
            route_batch(b)
        last = None
        for e_ in range(E):
            for b in range(B):
                cur = up(e_, b)
                if last:
                    down(*last)
                last = cur
                if b == 0 and e_ + 1 < E:
                    split_e(e_ + 1, slots[e_ + 1])
                if b == 1 and e_ + 2 < E:
                    slots[e_ + 2] = fetch_e(e_ + 2)
        down(*last)
        stack.close()

    def small_attention_phase(ph):
        stack = ExitStack()
        sb = allocator(stack, f"p{ph}")
        fence = [l.last() for l in lanes]
        KD = SKV * SD
        ROWS = PARTS * PARTS * SD
        SCALE = 1.0 / float(np.sqrt(SD))
        PRE = "L0_attn_"
        uT_hi, uT_lo = (Ring([sb(f"uT_{s}{i}", [P, KC, S], F32R)[:, :, :] for i in range(1)]) for s in ("hi", "lo"))
        WW = D + 2 * KD + D
        w_hi, w_lo = (sb(f"w_{s}", [P, KC, WW], F32R) for s in ("hi", "lo"))
        bq, bk = sb("bq", [P, D // P]), sb("bk", [KD, 1])
        bv, bo = sb("bv", [P, KD]), sb("bo", [P, D])
        q32, r32 = Ring([sb(f"q32_{i}", [P, S])[:, :] for i in range(2)]), sb("r32", [P, S])
        qp = Ring([sb(f"qp{i}", [P, PARTS, S], BF16)[:, :, :] for i in range(2)],
                  [Flag(sem(f"p{ph}_save{i}")) for i in range(2)])
        q_st = [sb(f"q_st{i}", [P, SH, S], BF16) for i in range(2)]
        k_st = [sb(f"k_st{i}", [P, SKV, S], BF16) for i in range(2)]
        fill = sb("fill", [PARTS, 2, S], BF16)
        VR = 32
        v_aug = Ring([sb(f"v_aug{i}", [P, T, SKV, VR])[:, :, :, :] for i in range(2)])
        nmax = sb("nmax", [P, 2, T, 8])
        nm_p = [sb(f"nm_p{i}", [8, PARTS, S], BF16) for i in range(2)]
        nm_r = sb("nm_r", [8, S])
        prT = Ring([sb(f"prT{i}", [P, S])[:, :] for i in range(12)])
        o_sb = Ring([sb(f"o_sb{i}", [P, S])[:, :] for i in range(2)])
        rsum = Ring([sb(f"rsum{i}", [P, T, KV])[:, :, :] for i in range(2)])
        o_tm = Ring([sb(f"o_tm{i}", [P, T, D])[:, :, :] for i in range(2)])
        oT_hi, oT_lo = (Ring([sb(f"oT_{s}{i}", [P, KC, S], F32R)[:, :, :] for i in range(1)]) for s in ("hi", "lo"))
        norm = Norm(sb, "ln")
        n_tile = Ring([sb(f"n_tile{i}", [P, D])[:, :] for i in range(4)])
        sring, tring = Ring([b[:, :] for b in banks[0:3]]), Ring([b[:, :] for b in banks[3:5]])
        oring, wring = Ring([b[:, :] for b in banks[5:6]]), Ring([b[:, :] for b in banks[6:8]])

        def put(c0, cols):
            return lambda a: a[:, 0:KC * WW].rearrange("p (c n) -> p c n", c=KC)[:, :, c0:c0 + cols]
        slot = fetch([(slice(0, P), put(0, D), chunks(io[PRE + "Wq"])),
                      (slice(0, P), put(D, KD), chunks(io[PRE + "Wk"])),
                      (slice(0, P), put(D + KD, KD), chunks(io[PRE + "Wv"])),
                      (slice(0, P), put(D + 2 * KD, D), chunks(io[PRE + "Wo"]))])
        cflag = Flag(sem(f"p{ph}_const"))
        cflag.dma(sp, bq[:, :], io[PRE + "bq"].rearrange("(c p) -> p c", p=P), fence,
                             by_element=True)
        cflag.dma(sp, bk[:, :], io[PRE + "bk"].rearrange("(p a) -> p a", a=1), fence,
                  by_element=True)
        cflag.dma(sp, bv[:, :], io[PRE + "bv"].rearrange("(a n) -> a n", a=1).to_broadcast([P, KD]), fence)
        ctok = cflag.dma(sp, bo[:, :], io[PRE + "bo"].rearrange("(a n) -> a n", a=1).to_broadcast([P, D]), fence)
        for l in lanes:
            l.fence(fence)
        w_ready = split(slot, KC * WW, w_hi[:, :, :].rearrange("p c n -> p (c n)"),
                        w_lo[:, :, :].rearrange("p c n -> p (c n)"))
        zero = [pool.do(lambda e, m=m: e.memset(m[64:P, :, :], 0.0)) for m in (*q_st, *k_st)]
        filled = [pool.do(lambda e, i=i: e.memset(fill[:, i, :], float(i))) for i in range(2)]
        oflag = Flag(sem(f"p{ph}_ones"))
        for m in k_st:
            one_rows = oflag.dma(sp, m[ROWS:ROWS + PARTS, :, :],
                                 fill[:, 1:2, :].to_broadcast([PARTS, SKV, S]), zero, filled)
        va = []
        for s in v_aug.slots:
            z = pool.do(lambda e, s=s: e.memset(s.ap, 0.0))
            va.append(pool.do(lambda e, s=s: e.memset(s.ap[:, :, :, SD], 1.0), z))

        qk_flag, nm_flag = ([Flag(sem(f"p{ph}_{n}{i}")) for i in range(2)] for n in ("qk", "nm"))
        prior = {"r32": [], "nmax": [[], []], "nm_p": [[], []], "nm_r": []}
        stack_ready, stack_read, v_aug_of, v_ready, o_tm_of, o_toks, nm_done = {}, {}, {}, {}, {}, {}, {}

        def cols(c0, n_):
            return slice(c0, c0 + n_)

        def prelude(b):
            tiles = [b * T + t for t in range(T)]
            ready = [[res_ready[i]] for i in tiles]
            rs = norm.run([res[:, i, :] for i in tiles], LN_EPS, ready)
            yield
            srcs = []
            for t, i in enumerate(tiles):
                nt = n_tile.take()
                h = dve.do(lambda e, t=t, i=i, nt=nt: e.tensor_scalar(
                    nt.ap, res[:, i, :], norm.mv[:, t, 0:1], norm.rs[:, t:t + 1], ALU.subtract, ALU.mult),
                    rs, ready[t], nt.after)
                srcs.append((nt, h))
                if t % 2:
                    yield
            norm.read = [srcs[-1][1]]
            uh, ul = uT_hi.take(), uT_lo.take()
            u_ready, reads = yield from feature_major_steps(
                lambda t: srcs[t][0].ap, [s[1] for s in srcs], wring, uh.ap, ul.ap, None, uh.after, ul.after)
            for nt, _ in srcs:
                nt.free(*reads)
            saved = []
            for c0, width, bias, dst, sc in ((D, KD, bk[:, 0:1], D, 1.0), (0, P, bq[:, 0:1], 0, SCALE),
                                             (P, P, bq[:, 1:2], P, SCALE)):
                bank, q_, pp = wring.take(), q32.take(), qp.take()
                pairs = []
                for k in range(KC):
                    pairs += three(w_hi[:, k, cols(c0, width)], w_lo[:, k, cols(c0, width)], uh.ap[:, k, :], ul.ap[:, k, :])
                mm = product(bank.ap[0:width, :], pairs, u_ready, w_ready, bank.after)
                r = slice(0, width)
                a0 = dve.do(lambda e, q_=q_, bank=bank, r=r, bias=bias, sc=sc: e.tensor_scalar(
                    q_.ap[r, :], bank.ap[r, :], bias, sc, ALU.add, ALU.mult), mm, ctok, q_.after)
                bank.free(a0)
                yield
                a1 = act.do(lambda e, q_=q_, pp=pp, r=r: e.activation(pp.ap[r, 0, :], q_.ap[r, :], ACT.Copy), a0, pp.after)
                a2 = dve.do(lambda e, q_=q_, pp=pp, r=r: e.tensor_tensor(r32[r, :], q_.ap[r, :], pp.ap[r, 0, :],
                                                                        ALU.subtract), a1, *prior["r32"])
                yield
                a3 = act.do(lambda e, pp=pp, r=r: e.activation(pp.ap[r, 1, :], r32[r, :], ACT.Copy), a2, pp.after)
                a4 = dve.do(lambda e, pp=pp, r=r: e.tensor_tensor(pp.ap[r, 2, :], r32[r, :], pp.ap[r, 1, :],
                                                                 ALU.subtract), a3)
                prior["r32"] = [a4]
                q_.free(a1, a2)
                sv = pp.flag.dma(sp, parts_saved[b % 2, :, dst:dst + width, :].rearrange("m r n -> r m n"),
                                 pp.ap[r, :, :], a4, a1, a3, stack_ready.get(b - 2))
                pp.free(sv)
                saved.append(sv)
                yield
            qs, ks, flag = q_st[b % 2], k_st[b % 2], qk_flag[b % 2]
            free = stack_read.get(b - 2)
            flag.dma(sp, qs[ROWS:ROWS + PARTS, :, :], fill[:, 0:1, :].to_broadcast([PARTS, SH, S]), zero, filled, free)
            for a in range(PARTS):
                for m in range(PARTS):
                    rows = slice((a * PARTS + m) * SD, (a * PARTS + m + 1) * SD)
                    flag.dma(sp, ks[rows, :, :], parts_saved[b % 2, m, D:D + KD, :].rearrange(
                        "(g d) n -> d g n", d=SD), saved, zero, free)
                    stack_ready[b] = flag.dma(sp, qs[rows, :, :], parts_saved[b % 2, a, 0:D, :].rearrange(
                        "(h d) n -> d h n", d=SD), saved, zero, free)
            va_s = v_aug.take()
            bank = wring.take()
            for t in range(T):
                tk = slice(t * P, (t + 1) * P)
                pairs = []
                for k in range(KC):
                    pairs += three(uh.ap[:, k, tk], ul.ap[:, k, tk], w_hi[:, k, cols(D + KD, KD)], w_lo[:, k, cols(D + KD, KD)])
                mm = product(bank.ap[:, t * KD:(t + 1) * KD], pairs, bank.after)
                if t % 2 and t < T - 1:
                    yield
            v_ready[b] = [dve.do(lambda e, t=t, bank=bank, va_s=va_s: e.tensor_tensor(
                va_s.ap[:, t, :, 0:SD], bank.ap[:, t * KD:(t + 1) * KD].rearrange("p (g d) -> p g d", g=SKV),
                bv[:, :].rearrange("p (g d) -> p g d", g=SKV), ALU.add), mm, va, va_s.after) for t in range(T)]
            bank.free(*v_ready[b])
            v_aug_of[b] = va_s
            uh.free(mm)
            ul.free(mm)

        def maxima(b, qt):
            s = qt % 2
            qs, ks = q_st[b % 2], k_st[b % 2]
            for hh in range(8):
                head = qt * 8 + hh
                for t in range(T):
                    bk_ = sring.take()
                    mm = product(bk_.ap, [(qs[:, head, t * P:(t + 1) * P], ks[:, head // KV, :])],
                                 stack_ready[b], one_rows, bk_.after)
                    mx = dve.do(lambda e, t=t, hh=hh, bk_=bk_: e.tensor_reduce(
                        nmax[:, s, t, hh:hh + 1], bk_.ap, axis=AX.X, op=ALU.max, negate=True), mm, *prior["nmax"][s])
                    bk_.free(mx)
                    if hh < 7 or t < T - 1:
                        yield
            wb = wring.take()
            for t in range(T):
                tt = transpose(wb.ap[0:8, t * P:(t + 1) * P], nmax[:, s, t, :], P, mx, wb.after, signal=t == T - 1)
            prior["nmax"][s] = [tt]
            np_ = nm_p[s]
            a1 = act.do(lambda e: e.activation(np_[:, 0, :], wb.ap[0:8, :], ACT.Copy), tt, *prior["nm_p"][s])
            a2 = dve.do(lambda e: e.tensor_tensor(nm_r[:, :], wb.ap[0:8, :], np_[:, 0, :], ALU.subtract), a1,
                        *prior["nm_r"])
            wb.free(a1, a2)
            a3 = act.do(lambda e: e.activation(np_[:, 1, :], nm_r[:, :], ACT.Copy), a2)
            a4 = dve.do(lambda e: e.tensor_tensor(np_[:, 2, :], nm_r[:, :], np_[:, 1, :], ALU.subtract), a3)
            prior["nm_r"] = [a4]
            for m in range(PARTS):
                done = nm_flag[s].dma(pool, qs[ROWS + m:ROWS + m + 1, qt * 8:(qt + 1) * 8, :],
                                      np_[:, m, :], a1, a3, a4, mm)
            prior["nm_p"][s] = [done]
            nm_done[b, qt] = done
            yield

        def attend(b, qt):
            if qt == 0:
                o_tm_of[b], o_toks[b] = o_tm.take(), []
            otm, va_s, qs, ks = o_tm_of[b], v_aug_of[b], q_st[b % 2], k_st[b % 2]
            late = []

            def value(kv, kt, exps, ob):
                for j, (pt, ex) in enumerate(exps):
                    av = pe.do(lambda e, j=j, pt=pt: e.matmul(
                        ob.ap[VR * j:VR * (j + 1), :], va_s.ap[:, kt, kv, :], pt.ap,
                        start=kt == 0, stop=kt == T - 1), ex, v_ready[b], ob.after, signal=j == KV - 1)
                for pt, _ in exps:
                    pt.free(av)
                if kt == T - 1:
                    os_ = o_sb.take()
                    c1 = act.do(lambda e: e.activation(os_.ap, ob.ap, ACT.Copy), av, os_.after)
                    ob.free(c1)
                    if kv % 2 and qt == 3:
                        stack_read[b] = av
                        va_s.free(av)
                    later.append([3, lambda: finish(kv, os_, c1)])

            def finish(kv, os_, c1):
                wb = wring.take()
                for t in range(T):
                    tt = transpose(wb.ap[:, t * P:(t + 1) * P], os_.ap[:, t * P:(t + 1) * P], P, c1, wb.after,
                                   signal=t == T - 1)
                os_.free(tt)
                rr = rsum.take()
                view = wb.ap.rearrange("p (t j r) -> p t j r", t=T, j=KV)
                rc = dve.do(lambda e: e.reciprocal(rr.ap, view[:, :, :, SD]), tt, rr.after)
                dst = otm.ap[:, :, kv * KV * SD:(kv + 1) * KV * SD].rearrange("p t (j d) -> p t j d", j=KV)
                mu = [dve.do(lambda e, t=t: e.tensor_tensor(
                    dst[:, t], view[:, t, :, 0:SD], rr.ap[:, t, :].unsqueeze(2).to_broadcast([P, KV, SD]),
                    ALU.mult), rc, otm.after) for t in range(T)]
                wb.free(*mu)
                rr.free(mu[-1])
                o_toks[b].append(mu[-1])

            for g in range(2):
                kv = qt * 2 + g
                obs = [None]
                for kt in range(T):
                    exps = []
                    for j in range(KV):
                        head = kv * KV + j
                        tb, pt = tring.take(), prT.take()
                        mm = product(tb.ap, [(ks[:, kv, kt * P:(kt + 1) * P], qs[:, head, :])],
                                     nm_done[b, qt], tb.after)
                        ex = act.do(lambda e, tb=tb, pt=pt: e.activation(pt.ap, tb.ap, ACT.Exp), mm, pt.after)
                        tb.free(ex)
                        exps.append((pt, ex))
                        if j == KV - 1:
                            later.append([2, lambda kv=kv, kt=kt, exps=exps, obs=obs: value(
                                kv, kt, exps, first_bank(obs))])
                        tick()
                        yield

        later = []

        def first_bank(obs):
            if obs[0] is None:
                obs[0] = oring.take()
            return obs[0]

        def tick():
            for item in list(later):
                item[0] -= 1
                if item[0] < 0:
                    later.remove(item)
                    item[1]()

        def tail(b):
            oh, ol = oT_hi.take(), oT_lo.take()
            otm = o_tm_of[b]
            o_ready, reads = yield from feature_major_steps(lambda t: otm.ap[:, t, :], [o_toks[b]] * T, wring,
                                                            oh.ap, ol.ap, None, oh.after, ol.after)
            otm.free(*reads)
            for t in range(T):
                i = b * T + t
                bank = wring.take()
                tk = slice(t * P, (t + 1) * P)
                pairs = []
                for k in range(KC):
                    pairs += three(oh.ap[:, k, tk], ol.ap[:, k, tk], w_hi[:, k, cols(D + 2 * KD, D)],
                                   w_lo[:, k, cols(D + 2 * KD, D)])
                mm = product(bank.ap[:, 0:D], pairs, o_ready, bank.after)
                a1 = dve.do(lambda e, i=i, bank=bank: e.tensor_tensor(res[:, i, :], bank.ap[:, 0:D], res[:, i, :],
                                                                      ALU.add), mm, res_ready[i])
                bank.free(a1)
                res_ready[i] = pool.do(lambda e, i=i: e.tensor_tensor(res[:, i, :], res[:, i, :], bo[:, :], ALU.add),
                                       a1, ctok)
                yield
            oh.free(mm)
            ol.free(mm)

        LEAD, QSTEPS = 44, 8 * T
        for _ in prelude(0):
            pass
        peaks = (None for b in range(B) for qt in range(4) for _ in maxima(b, qt))
        for _ in range(LEAD):
            next(peaks, None)
        for b in range(B):
            def beside():
                for _ in range(6):
                    yield
                if b:
                    yield from tail(b - 1)
                if b + 1 < B:
                    yield from prelude(b + 1)
            side = beside()
            n_step = 0
            for qt in range(4):
                for _ in attend(b, qt):
                    next(peaks, None)
                    if n_step % 2 == 0:
                        next(side, None)
                    n_step += 1
            for _ in side:
                pass
        while later:
            tick()
        for _ in tail(B - 1):
            pass
        stack.close()

    def thought_phase(ph, final):
        stack = ExitStack()
        sb = allocator(stack, f"p{ph}")
        fence = [l.last() for l in lanes]
        PRE = "L1_ffn_"
        HH = 1024
        HN = HH // P
        u = sb("u", [P, NT, D])
        gt = sb("gate", [P, NT, D])
        uT_hi, uT_lo = (Ring([sb(f"uT_{s}{i}", [P, KC, S], F32R)[:, :, :] for i in range(2)]) for s in ("hi", "lo"))
        gw_hi, gw_lo = (sb(f"gw_{s}", [P, KC * D], F32R) for s in ("hi", "lo"))
        agg, bc = sb("agg", [P, KC, D]), sb("bc", [P, KC, D])
        d1, d2 = sb("d1", [P, KC, HH]), sb("d2", [P, HN, D])
        d1b = sb("d1b", [P, HN])
        gb, og, ob_ = sb("gb", [P, D]), sb("og", [P, D]), sb("ob", [P, D])
        rows = {k: sb("r_" + k, [B, D]) for k in ("in_gamma", "in_beta", "agg_b", "pn_gamma", "pn_beta", "d2_b", "bc_b")}
        last = sb("last", [B, D])
        th, nrm = sb("thought", [B, D]), sb("nrm", [B, D])
        tT = sb("tT", [P, KC, B])
        hid, hid2 = sb("hid", [P, HN, B]), sb("hid2", [P, HN, B])
        sel = sb("sel", [B, B, P])
        bc4 = sb("bc4", [B, D])
        bcast = sb("bcast", [P, B, D])
        norm, nrm4, norm2 = Norm(sb, "ln"), Norm(sb, "l4", parts=B, tiles=1), Norm(sb, "lo")
        wring, cring = Ring([b[:, :] for b in banks[0:6]]), Ring([b[:, :] for b in banks[6:8]])

        slot = fetch([(slice(0, P), lambda a: a[:, 0:KC * D].rearrange("p (c n) -> p c n", c=KC),
                       chunks(io[PRE + "gate_w"]))])
        cflag = Flag(sem(f"p{ph}_const"))
        for k, m in rows.items():
            cflag.dma(sp, m[:, :], io[PRE + k].rearrange("(a n) -> a n", a=1).to_broadcast([B, D]), fence)
        cflag.dma(sp, agg[:, :, :], chunks(io[PRE + "agg_w"]), fence)
        cflag.dma(sp, d1[:, :, :], chunks(io[PRE + "d1_w"]), fence)
        cflag.dma(sp, d2[:, :, :], chunks(io[PRE + "d2_w"]), fence)
        cflag.dma(sp, bc[:, :, :], chunks(io[PRE + "bc_w"]), fence)
        cflag.dma(sp, d1b[:, :], io[PRE + "d1_b"].rearrange("(c p) -> p c", p=P), fence,
                             by_element=True)
        for m, k in ((gb, "gate_b"), (og, "out_gamma"), (ob_, "out_beta")):
            ctok = cflag.dma(sp, m[:, :], io[PRE + k].rearrange("(a n) -> a n", a=1).to_broadcast([P, D]), fence)
        for l in lanes:
            l.fence(fence)
        z = pool.do(lambda e: e.memset(sel[:, :, :], 0.0))
        sel_ready = pool.do(lambda e: e.affine_select(out=sel[:, :, :], in_=sel[:, :, :], compare_op=ALU.not_equal,
                                                      fill=1.0, base=0, pattern=[[-1, B], [0, P]],
                                                      channel_multiplier=1), z)
        gw_ready = split(slot, KC * D, gw_hi[:, :], gw_lo[:, :])
        og_h = dve.do(lambda e: e.tensor_scalar(og[:, :], og[:, :], 0.5, None, ALU.mult), ctok)
        ob_h = dve.do(lambda e: e.tensor_scalar(ob_[:, :], ob_[:, :], 0.5, None, ALU.mult), ctok)

        u_ready = []
        uflag = Flag(sem(f"p{ph}_last"))
        for b in range(B):
            tiles = [b * T + t for t in range(T)]
            rs = norm.run([res[:, i, :] for i in tiles], LN_EPS, [[res_ready[i]] for i in tiles])
            for t, i in enumerate(tiles):
                u_ready.append(dve.do(lambda e, t=t, i=i: e.tensor_scalar(
                    u[:, i, :], res[:, i, :], norm.mv[:, t, 0:1], norm.rs[:, t:t + 1], ALU.subtract, ALU.mult),
                    rs, res_ready[i]))
            norm.read = [u_ready[-1]]
            lt = uflag.dma(sp, last[b:b + 1, :], u[P - 1:P, b * T + T - 1, :], u_ready[-1])

        g_ready = {}

        def gates(b):
            hi, lo = uT_hi.take(), uT_lo.take()
            ready, _ = feature_major(lambda t: u[:, b * T + t, :], [u_ready[b * T + t] for t in range(T)], wring,
                                     hi.ap, lo.ap, None, hi.after, lo.after)
            yield
            ghi = gw_hi[:, :].rearrange("p (k n) -> p k n", k=KC)
            glo = gw_lo[:, :].rearrange("p (k n) -> p k n", k=KC)
            for t in range(T):
                bank = wring.take()
                tk = slice(t * P, (t + 1) * P)
                pairs = []
                for k in range(KC):
                    pairs += three(hi.ap[:, k, tk], lo.ap[:, k, tk], ghi[:, k, :], glo[:, k, :])
                mm = product(bank.ap[:, 0:D], pairs, ready, gw_ready, bank.after)
                g = dve.do(lambda e, i=b * T + t, bank=bank: e.tensor_tensor(gt[:, i, :], bank.ap[:, 0:D], gb[:, :],
                                                                             ALU.add), mm, ctok)
                bank.free(g)
                g_ready[b * T + t] = g
                if t % 2:
                    yield
            hi.free(mm)
            lo.free(mm)

        def all_gates():
            for b in range(B):
                yield from gates(b)
        back = all_gates()

        def ln4(dst, src, ready, gamma, beta):
            rs = nrm4.run([src], FFN_EPS, [ready])
            a = dve.do(lambda e: e.tensor_scalar(dst, src, nrm4.mv[:, 0, 0:1], nrm4.rs[:, 0:1],
                                                 ALU.subtract, ALU.mult), rs)
            m = dve.do(lambda e: e.tensor_tensor(dst, dst, gamma[:, :], ALU.mult), a, ctok)
            nrm4.read = [a]
            return dve.do(lambda e: e.tensor_tensor(dst, dst, beta[:, :], ALU.add), m)

        prior = {"tT": [], "hid": [], "hid2": []}

        def columns(src, ready):
            bank = cring.take()
            for k in range(KC):
                tt = transpose(bank.ap[:, k * B:(k + 1) * B], src[:, k * P:(k + 1) * P], B, ready, bank.after,
                               signal=k == KC - 1)
            c = dve.do(lambda e: e.tensor_copy(tT[:, :, :], bank.ap[:, 0:KC * B].rearrange("p (k b) -> p k b", k=KC)),
                       tt, *prior["tT"])
            bank.free(c)
            return c

        def linear(w, ready):
            bank = cring.take()
            mm = product(bank.ap[0:B, 0:D], [(tT[:, k, :], w[:, k, :]) for k in range(KC)], ready, ctok, bank.after)
            prior["tT"] = [mm]
            return bank, mm

        n0 = ln4(nrm[:, :], last[:, :], lt, rows["in_gamma"], rows["in_beta"])
        bank, mm = linear(agg, columns(nrm, n0))
        thr = dve.do(lambda e, bank=bank: e.tensor_tensor(th[:, :], bank.ap[0:B, 0:D], rows["agg_b"][:, :], ALU.add), mm)
        bank.free(thr)
        for _ in range(4):
            next(back, None)
            n1 = ln4(nrm[:, :], th[:, :], thr, rows["pn_gamma"], rows["pn_beta"])
            next(back, None)
            c1 = columns(nrm, n1)
            bank = cring.take()
            for h_ in range(HN):
                mm = product(bank.ap[:, h_ * B:(h_ + 1) * B],
                             [(d1[:, k, h_ * P:(h_ + 1) * P], tT[:, k, :]) for k in range(KC)], c1, ctok, bank.after)
            prior["tT"] = [mm]
            a1 = dve.do(lambda e, bank=bank: e.tensor_tensor(
                hid[:, :, :], bank.ap[:, 0:HN * B].rearrange("p (h b) -> p h b", h=HN),
                d1b[:, :].unsqueeze(2).to_broadcast([P, HN, B]), ALU.add), mm, *prior["hid"])
            bank.free(a1)
            a2 = act.do(lambda e: e.activation(hid2[:, :, :], hid[:, :, :], ACT.Gelu), a1, *prior["hid2"])
            prior["hid"] = [a2]
            next(back, None)
            bank = cring.take()
            mm = product(bank.ap[0:B, 0:D], [(hid2[:, h_, :], d2[:, h_, :]) for h_ in range(HN)], a2, bank.after)
            prior["hid2"] = [mm]
            b1 = dve.do(lambda e, bank=bank: e.tensor_tensor(th[:, :], bank.ap[0:B, 0:D], th[:, :], ALU.add), mm, thr)
            bank.free(b1)
            thr = dve.do(lambda e: e.tensor_tensor(th[:, :], th[:, :], rows["d2_b"][:, :], ALU.add), b1)
        bank, mm = linear(bc, columns(th, thr))
        b4 = dve.do(lambda e, bank=bank: e.tensor_tensor(bc4[:, :], bank.ap[0:B, 0:D], rows["bc_b"][:, :], ALU.add), mm)
        bank.free(b4)
        b_ready = []
        for b in range(B):
            bank = cring.take()
            mm = product(bank.ap[:, 0:D], [(sel[:, b, :], bc4[:, :])], b4, sel_ready, bank.after)
            c = act.do(lambda e, b=b, bank=bank: e.activation(bcast[:, b, :], bank.ap[:, 0:D], ACT.Copy), mm)
            bank.free(c)
            b_ready.append(c)
        for _ in back:
            pass

        oflag = Flag(sem(f"p{ph}_out"))
        otok = None
        for b in range(B):
            tiles = [b * T + t for t in range(T)]
            ready = []
            for i in tiles:
                s = act.do(lambda e, i=i: e.activation(gt[:, i, :], gt[:, i, :], ACT.Sigmoid), g_ready[i])
                m = dve.do(lambda e, i=i, b=b: e.tensor_tensor(gt[:, i, :], gt[:, i, :], bcast[:, b, :], ALU.mult),
                           s, b_ready[b])
                ready.append([dve.do(lambda e, i=i: e.tensor_tensor(u[:, i, :], u[:, i, :], gt[:, i, :], ALU.add), m)])
            rs = norm2.run([u[:, i, :] for i in tiles], FFN_EPS, ready)
            for t, i in enumerate(tiles):
                a = dve.do(lambda e, t=t, i=i: e.tensor_scalar(
                    u[:, i, :], u[:, i, :], norm2.mv[:, t, 0:1], norm2.rs[:, t:t + 1], ALU.subtract, ALU.mult), rs)
                m = dve.do(lambda e, i=i: e.tensor_tensor(u[:, i, :], u[:, i, :], og[:, :], ALU.mult), a, og_h)
                r1 = pool.do(lambda e, i=i: e.tensor_tensor(res[:, i, :], res[:, i, :], ob_[:, :], ALU.add),
                             ob_h, res_ready[i], u_ready[i])
                res_ready[i] = dve.do(lambda e, i=i: e.tensor_tensor(res[:, i, :], res[:, i, :], u[:, i, :], ALU.add),
                                      m, r1)
            norm2.read = [a]
            if final:
                otok = oflag.dma(sp, out[b].rearrange("(t p) d -> p t d", p=P), res[:, b * T:(b + 1) * T, :],
                                 [res_ready[i] for i in tiles])
        if final:
            sp.fence(otok)
        stack.close()

    saved_tokens = []
    plan = ["moe_attn", "moe", "small", "moe_attn", "moe", "thought", "window", "thought"][:phases]
    for ph, what in enumerate(plan):
        if what == "moe_attn":
            attention_phase(ph, False, None)
        elif what == "moe":
            moe_phase(ph, None)
        elif what == "small":
            small_attention_phase(ph)
        elif what == "window":
            attention_phase(ph, True, None)
        else:
            thought_phase(ph, ph == 7)
    if len(plan) < 8:
        oflag = Flag(sem("dbg"))
        for b in range(B):
            otok = oflag.dma(sp, out[b].rearrange("(t p) d -> p t d", p=P), res[:, b * T:(b + 1) * T, :],
                             [res_ready[b * T + t] for t in range(T)])
        sp.fence(otok)

    with nc.Block() as block:
        block.sync(sp.play)
        block.gpsimd(pool.play)
        block.vector(dve.play)
        block.scalar(act.play)
        block.tensor(pe.play)
    ctx.close()


_PHASES = 8


def _rope_tables():
    f = np.float32
    pos = np.arange(S, dtype=f)[:, None]
    inv0 = f(1.0) / (f(150000.0) ** (np.arange(32, dtype=f) / f(32)))
    a0 = pos * inv0
    a0 = np.concatenate([a0, a0], -1)
    scale1 = f(10000.0) ** (np.arange(0, 128, 2, dtype=f) / f(128))
    a1 = pos / scale1[None, :]
    a1 = np.concatenate([a1, a1], -1)

    def signed(s):
        h = s.shape[1] // 2
        return np.concatenate([-s[:, :h], s[:, h:]], -1)
    return {"rope0_cos": np.cos(a0), "rope0_sin": signed(np.sin(a0)),
            "rope1_cos": np.cos(a1), "rope1_sin": signed(np.sin(a1))}


def kernel(**inputs):
    import concourse.bacc as bacc
    from concourse.bass_utils import run_bass_kernel_spmd

    nc = bacc.Bacc("TRN2", target_bir_lowering=False, num_devices=1)
    arrays, io = {}, {}
    for name, value in {**inputs, **_rope_tables()}.items():
        a = np.ascontiguousarray(value)
        arrays[f"in_{name}"] = a
        io[name] = nc.dram_tensor(f"in_{name}", a.shape, mybir.dt.from_np(a.dtype), kind="ExternalInput").ap()
    out = nc.dram_tensor("out", (B, S, D), mybir.dt.float32, kind="ExternalOutput").ap()
    build(nc, io, out, _PHASES)
    r = run_bass_kernel_spmd(nc, [arrays], core_ids=[0])
    return r.results[0]["out"]
```

```python
import numpy as np
import concourse.bass as bass
from concourse import mybir
from contextlib import ExitStack

P = 128
B, S, D = 4, 512, 256
T = S // P
NT = B * T
KC = D // P
E, TOPK, H = 16, 4, 256
HC = H // P
KV = 4
NEG = -1e30
LN_EPS, RMS_EPS, FFN_EPS = 1e-5, 1e-5, 1e-6
BANK = 512
NU = 4
QW = 512
KW = 128
SH, SKV, SD = 32, 8, 8
PARTS = 3
BESIDE = (5,2)
SENT = (-3.0e38, -3.1e38, -3.2e38, -3.3e38)


class Lane:

    def __init__(self, name, sem):
        self.name, self.sem, self.done, self.queue, self.seen = name, sem, 0, [], {}
        self.one_by_one = name == "pool"

    def waits(self, after):
        need = {}
        stack = list(after)
        while stack:
            t = stack.pop()
            if t is None:
                continue
            if isinstance(t, list):
                stack.extend(t)
            elif t[1] > max(need.get(t[0], (0, 0))[1], self.seen.get(t[0], 0)):
                need[t[0]] = t
        for k, t in need.items():
            self.seen[k] = t[1]
        return list(need.values())

    def do(self, emit, *after, signal=True):
        if self.one_by_one and self.done:
            after = (*after, self.last())
        self.queue.append((self.waits(after), emit, self.sem if signal else None, 1))
        if signal:
            self.done += 1
            return (self.sem, self.done)
        return None

    def fence(self, *after):
        self.queue.append((self.waits(after), None, None, 0))

    def last(self):
        return (self.sem, self.done)

    def play(self, eng):
        for waits, emit, sem, n in self.queue:
            for s, v in waits:
                eng.wait_ge(s, v)
            if emit is not None:
                ins = emit(eng)
                if sem is not None:
                    ins.then_inc(sem, n)


class Flag:

    def __init__(self, sem):
        self.sem, self.n = sem, 0

    def dma(self, lane, out, in_, *after, by_element=False):
        lane.queue.append((lane.waits(after), lambda e: e.dma_start(out, in_, allow_slow_non_contiguous=by_element),
                           self.sem, 16))
        self.n += 16
        return (self.sem, self.n)


class Slot:
    def __init__(self, ap, after, flag=None):
        self.ap, self.after, self.flag, self.users = ap, after, flag, None

    def free(self, *tokens):
        self.users = (self.users or []) + list(tokens)


class Ring:

    def __init__(self, aps, flags=None):
        self.slots, self.n = [Slot(a, [], f) for a, f in zip(aps, flags or [None] * len(aps))], 0
        for s in self.slots:
            s.users = []

    def take(self):
        i = self.n % len(self.slots)
        old = self.slots[i]
        assert old.users is not None, "a buffer is taken before its last use is queued"
        self.slots[i] = Slot(old.ap, old.users, old.flag)
        self.n += 1
        return self.slots[i]


def build(nc, io, out):
    F32, F32R, BF16 = mybir.dt.float32, mybir.dt.float32r, mybir.dt.bfloat16
    ALU, ACT, AX = mybir.AluOpType, mybir.ActivationFunctionType, mybir.AxisListType
    ctx = ExitStack()

    def sem(name):
        return ctx.enter_context(nc.semaphore(name))

    pe, act, dve, pool, sp = (Lane(n, sem(n + "_done")) for n in ("pe", "act", "dve", "pool", "sp"))
    lanes = (pe, act, dve, pool)
    banks = [ctx.enter_context(nc.psum_tensor(f"bank{i}", [P, BANK], F32)) for i in range(8)]

    def allocator(stack, prefix, side="left"):
        def sb(name, shape, dt=F32):
            return stack.enter_context(nc.sbuf_tensor(f"{prefix}_{name}", shape, dt, side=side))
        return sb

    top = allocator(ctx, "g")

    res = top("res", [P, NT, D])
    ident = top("ident", [P, P])
    identb = top("identb", [P, P], BF16)
    half = top("minus_half", [P, NT])
    STAGE_W = 1536
    stage_mem = [top(f"stage{i}", [P, STAGE_W]) for i in range(2)]
    stage = Ring([m[:, :] for m in stage_mem], [Flag(sem(f"stage{i}")) for i in range(2)])
    res_saved = nc.dram_tensor("res_saved", (NT, P, D), F32, kind="Internal").ap()
    parts_saved = nc.dram_tensor("parts_saved", (2, PARTS, D + SKV * SD, S), BF16, kind="Internal").ap()

    def make_ident(m):
        z = pool.do(lambda e: e.memset(m[:, :], 0.0))
        return pool.do(lambda e: e.affine_select(out=m[:, :], in_=m[:, :], compare_op=ALU.not_equal, fill=1.0,
                                                 base=0, pattern=[[-1, P]], channel_multiplier=1), z)
    ident_made = [make_ident(ident), make_ident(identb)]
    half_made = pool.do(lambda e: e.memset(half[:, :], -0.5))
    res_flags = [Flag(sem(f"res_load{b}")) for b in range(B)]
    x_tiles = io["L0_attn_hidden_states"].rearrange("b (t p) d -> (b t) p d", p=P)
    res_ready = [None] * NT

    def load(b):
        bt = slice(b * T, b * T + T)
        res_ready[bt] = [res_flags[b].dma(sp, res[:, bt, :], x_tiles[bt].rearrange("t p d -> p t d"))] * T
    pe.fence(ident_made)

    def fetch(pieces):
        slot = stage.take()
        for rows, view, src in pieces:
            slot.token = slot.flag.dma(sp, view(slot.ap[rows, :]), src, slot.after)
        return slot

    def split(slot, width, hi, lo, *after):
        raw = slot.ap[:, 0:width]
        h = act.do(lambda e: e.activation(hi, raw, ACT.Copy), slot.token, *after)
        l = pool.do(lambda e: e.tensor_tensor(lo, raw, hi.bitcast(F32), ALU.subtract), h, *after)
        slot.free(h, l)
        return [h, l]

    def chunks(src):
        return src.rearrange("(c p) n -> p c n", p=P)

    def into(c0, cols, width):
        return lambda a: a[:, 0:KC * width].rearrange("p (c n) -> p c n", c=KC)[:, :, c0:c0 + cols]

    def product(out_ap, pairs, *after):
        tok = None
        for n, (l, r) in enumerate(pairs):
            last = n == len(pairs) - 1
            tok = pe.do(lambda e, l=l, r=r, n=n, last=last: e.matmul(out_ap, l, r, start=(n == 0), stop=last),
                        *(after if n == 0 else ()), signal=last)
        return tok

    def three(lh, ll, rh, rl):
        return [(lh, rh), (ll, rh), (lh, rl)]

    def transpose(out_ap, in_ap, n, *after, signal=True):
        return pe.do(lambda e: e.transpose(out_ap, in_ap, ident[0:n, 0:n]), *after, signal=signal)

    class Norm:

        def __init__(self, sb, name, parts=P, tiles=T):
            self.p, self.n = parts, tiles
            self.st = sb(name + "_st", [parts, tiles, 6])
            self.mv = sb(name + "_mv", [parts, tiles, 2])
            self.ve = sb(name + "_ve", [parts, tiles])
            self.rs = sb(name + "_rs", [parts, tiles])
            self.read = []

        def run(self, tiles, eps, ready):
            agg = []
            for i, x in enumerate(tiles):
                s = dve.do(lambda e, i=i, x=x: e.bn_stats(self.st[:, i, :], x), ready[i], *self.read)
                agg.append((i, s))
            done = [dve.do(lambda e, i=i: e.bn_aggr(self.mv[:, i, :], self.st[:, i, :]), s) for i, s in agg]
            v = dve.do(lambda e: e.tensor_scalar(self.ve[:, :], self.mv[:, :, 1], eps, None, ALU.add), done)
            r = pool.do(lambda e: e.tensor_tensor(self.rs[:, :], self.ve[:, :], half[0:self.p, 0:self.n], ALU.pow), v,
                        half_made)
            self.read = [v]
            return r

    boundary = []

    def begin():
        boundary[:] = [l.last() for l in lanes]
        for l in lanes:
            l.fence(boundary)
        return list(boundary)

    def feature_major(*args):
        steps = feature_major_steps(*args)
        while True:
            try:
                next(steps)
            except StopIteration as end:
                return end.value

    def feature_major_steps(src, ready, ring, hi, lo, scale, *after):
        toks, reads = [], []
        for c in range(KC):
            bank = ring.take()
            for t in range(T):
                tt = transpose(bank.ap[:, t * P:(t + 1) * P], src(t)[:, c * P:(c + 1) * P], P,
                               ready[t], bank.after, signal=t == T - 1)
            reads.append(tt)
            sc = scale[:, c:c + 1] if scale is not None else 1.0
            h = act.do(lambda e, c=c, bank=bank, sc=sc: e.activation(hi[:, c, :], bank.ap, ACT.Copy, scale=sc), tt, *after)
            l = dve.do(lambda e, c=c, bank=bank, sc=sc: e.scalar_tensor_tensor(
                lo[:, c, :], bank.ap, sc, hi[:, c, :].bitcast(F32), ALU.mult, ALU.subtract), h, *after)
            bank.free(h, l)
            toks += [h, l]
            yield
        return toks, reads

    def attention_phase(ph, wide, roomy, ahead):
        stack = ExitStack()
        sb = allocator(stack, f"p{ph}", ("left", "right")[ph % 2])
        hd = 128 if wide else 64
        nk = KW // hd
        nh = QW // hd
        n = "L1_attn_" if wide else "L0_ffn_"
        wq, wk, wv = (io[n + a] for a in (("q_kernel", "k_kernel", "v_kernel") if wide else ("wq", "wk", "wv")))
        wo = io["L1_attn_out_kernel"] if wide else io["L0_ffn_wo"]
        cs_dram, sn_dram = (io["rope1_cos"], io["rope1_sin"]) if wide else (io["rope0_cos"], io["rope0_sin"])
        scale = 1.0 / float(np.sqrt(hd))
        WQKV = QW + 2 * KW

        def fetch_qkv(c):
            return fetch([(slice(0, P), into(0, QW, WQKV), chunks(wq[:, c * QW:(c + 1) * QW])),
                          (slice(0, P), into(QW, KW, WQKV), chunks(wk[:, c * KW:(c + 1) * KW])),
                          (slice(0, P), into(QW + KW, KW, WQKV), chunks(wv[:, c * KW:(c + 1) * KW]))])

        def fetch_o(c):
            rows = KV * hd
            return fetch([(slice(i * hd, (i + 1) * hd),
                           lambda a: a[:, 0:KV * D].rearrange("p (j n) -> p j n", j=KV),
                           wo[c * QW + i * rows:c * QW + (i + 1) * rows, :].rearrange("(j d) n -> d j n", d=hd))
                          for i in range(nk)])

        slot_qkv, slot_o = fetch_qkv(0), fetch_o(0)
        if not roomy:
            yield
        fence = list(boundary) if roomy else begin()

        w_hi, w_lo = (sb(f"w_{s}", [P, 2, KC * (QW + 2 * KW)], F32R) for s in ("hi", "lo"))
        o_hi, o_lo = (sb(f"o_{s}", [P, 2, KV * D], F32R) for s in ("hi", "lo"))
        cs = sb("cos", [P, T, hd])
        sn = sb("sin", [P, T, hd])
        lnw = sb("lnw", [P, KC])
        mask = sb("mask", [P, 2 * P], BF16)
        cflag = Flag(sem(f"p{ph}_const"))
        ctok = cflag.dma(sp, cs[:, :, :], cs_dram.rearrange("(t p) d -> p t d", p=P), fence)
        ctok = cflag.dma(sp, sn[:, :, :], sn_dram.rearrange("(t p) d -> p t d", p=P), fence)
        if not wide:
            ctok = cflag.dma(sp, lnw[:, :], io["L0_ffn_ln_w"].rearrange("(c p) -> p c", p=P), fence,
                             by_element=True)
        mz = pool.do(lambda e: e.memset(mask[:, :], 0.0))
        m1 = pool.do(lambda e: e.affine_select(out=mask[:, P:], in_=mask[:, P:], compare_op=ALU.is_ge, fill=NEG,
                                               base=0, pattern=[[-1, P]], channel_multiplier=1), mz)
        m2 = pool.do(lambda e: e.affine_select(out=mask[:, :P], in_=mask[:, :P], compare_op=ALU.is_ge, fill=NEG,
                                               base=0, pattern=[[1, P]], channel_multiplier=-1), mz)

        w_ready, o_ready, w_used, o_used = {}, {}, {}, {}

        def split_qkv(c, slot):
            w_ready[c] = split(slot, KC * WQKV, w_hi[:, c % 2, :], w_lo[:, c % 2, :], w_used.get(c - 2))

        def split_o(c, slot):
            o_ready[c] = split(slot, KV * D, o_hi[:, c % 2, :], o_lo[:, c % 2, :], o_used.get(c - 2))

        split_qkv(0, slot_qkv)
        split_o(0, slot_o)
        if roomy:
            yield
            begin()
        pe.fence(m1, m2)

        aT_hi, aT_lo = (sb(f"aT_{s}", [P, B, KC, S], F32R) for s in ("hi", "lo"))
        rope_a = Ring([sb(f"rope_a{i}", [P, QW + KW])[:, :] for i in range(2)])
        rope_b = Ring([sb(f"rope_b{i}", [P, QW + KW])[:, :] for i in range(1)])
        tm = Ring([sb(f"tm{i}", [P, QW + nk * P])[:, :] for i in range(2)])
        v_sb = Ring([sb(f"v{i}", [P, T, KW])[:, :, :] for i in range(3)])
        q_st = Ring([sb(f"q{i}", [P, 8, P], F32R)[:, :, :] for i in range(5)])
        k_st = Ring([sb(f"k{i}", [P, 2, 2, S], F32R)[:, :, :, :] for i in range(2)])
        prob = Ring([sb(f"prob{i}", [P, S])[:, :] for i in range(8)])
        prT = Ring([sb(f"prT{i}", [P, KV * P])[:, :] for i in range(8)])
        oT_hi, oT_lo = (Ring([sb(f"oT_{s}{i}", [P, KV * P], F32R)[:, :] for i in range(2)]) for s in ("hi", "lo"))
        small = Ring([sb(f"small{i}", [P, 3, KV])[:, :, :] for i in range(3)])
        norm = Norm(sb, "ln")
        r2 = sb("rms", [P, T])
        n_tile = Ring([sb(f"n_tile{i}", [P, D])[:, :] for i in range(4)])
        n_s = 2 if wide else 3
        sring, tring, wring = (Ring([b[:, :] for b in banks[i:j]]) for i, j in ((0, n_s), (n_s, n_s + 2), (n_s + 2, 8)))

        aT_ready = {}
        saves = [Flag(sem(f"p{ph}_save{b}")) for b in range(0 if wide else B)]

        def norm_batch(b):
            tiles = [b * T + t for t in range(T)]
            ready = [[res_ready[i]] for i in tiles]
            rs = norm.run([res[:, i, :] for i in tiles], LN_EPS, ready)
            done = []
            if not wide:
                save = saves[b].dma(sp, res_saved[b * T:(b + 1) * T].rearrange("t p d -> p t d"),
                                 res[:, b * T:(b + 1) * T, :], ready)
                saved_tokens[b:b + 1] = [save]
                a1 = dve.do(lambda e: e.tensor_tensor(r2[:, :], norm.mv[:, :, 1], norm.rs[:, :], ALU.mult), rs, *norm_reads)
                a2 = dve.do(lambda e: e.tensor_tensor(norm.ve[:, :], r2[:, :], norm.rs[:, :], ALU.mult), a1)
                a3 = dve.do(lambda e: e.tensor_scalar(norm.ve[:, :], norm.ve[:, :], RMS_EPS, None, ALU.add), a2)
                rr = pool.do(lambda e: e.tensor_tensor(r2[:, :], norm.ve[:, :], half[:, 0:T], ALU.pow), a3)
                srcs = []
                for t, i in enumerate(tiles):
                    u = dve.do(lambda e, t=t, i=i: e.tensor_scalar(
                        res[:, i, :], res[:, i, :], norm.mv[:, t, 0:1], norm.rs[:, t:t + 1],
                        ALU.subtract, ALU.mult), rs, ready[t], save)
                    res_ready[i] = u
                    nt = n_tile.take()
                    h = act.do(lambda e, t=t, i=i, nt=nt: e.activation(nt.ap, res[:, i, :], ACT.Copy,
                                                                      scale=r2[:, t:t + 1]), u, rr, nt.after)
                    srcs.append((nt, h))
                norm_reads[:] = [srcs[-1][1]]
                norm.read = [srcs[-1][1], u]
            else:
                srcs = []
                for t, i in enumerate(tiles):
                    nt = n_tile.take()
                    h = dve.do(lambda e, t=t, i=i, nt=nt: e.tensor_scalar(
                        nt.ap, res[:, i, :], norm.mv[:, t, 0:1], norm.rs[:, t:t + 1],
                        ALU.subtract, ALU.mult), rs, ready[t], nt.after)
                    srcs.append((nt, h))
                norm.read = [srcs[-1][1]]
            yield
            toks, reads = feature_major(lambda t: srcs[t][0].ap, [s[1] for s in srcs], tring,
                                        aT_hi[:, b], aT_lo[:, b], None if wide else lnw, ctok)
            for nt, _ in srcs:
                nt.free(*reads)
            aT_ready[b] = toks

        norm_reads = []

        class Unit:
            pass

        def prepare(c, b, unit):
            if c == 0:
                for _ in normed.pop(b):
                    pass
            unit.k, unit.v = k_st.take(), v_sb.take()
            unit.q, unit.q_tok, unit.k_tok, unit.v_tok = [], [], [], []
            rotated = {}
            for t in range(T + 1):
                if t < T:
                    yield from products_of(c, b, unit, t, rotated)
                if t:
                    yield from turned(unit, t - 1, rotated[t - 1])

        def products_of(c, b, unit, t, rotated):
            whi = w_hi[:, c % 2, :].rearrange("p (k n) -> p k n", k=KC)
            wlo = w_lo[:, c % 2, :].rearrange("p (k n) -> p k n", k=KC)
            tok = slice(t * P, (t + 1) * P)

            def project(bank, c0, cols):
                pairs = []
                for k in range(KC):
                    pairs += three(aT_hi[:, b, k, tok], aT_lo[:, b, k, tok],
                                   whi[:, k, c0:c0 + cols], wlo[:, k, c0:c0 + cols])
                return product(bank.ap[:, 0:cols], pairs, aT_ready[b], w_ready[c], bank.after)
            qb = wring.take()
            qp = project(qb, 0, QW)
            yield
            ra, rb, tb = rope_a.take(), rope_b.take(), tm.take()
            hf = hd // 2

            def rotate(bank, ready, width, at):
                heads = width // hd
                x = bank.ap[:, 0:width].rearrange("p (h d) -> p h d", d=hd)
                a = ra.ap[:, at:at + width].rearrange("p (h d) -> p h d", d=hd)
                bb = rb.ap[:, at:at + width].rearrange("p (h d) -> p h d", d=hd)

                def table(m, lo_, hi_):
                    return m[:, t, lo_:hi_].unsqueeze(1).to_broadcast([P, heads, hi_ - lo_])
                c_all, s_left, s_right = table(cs, 0, hd), table(sn, 0, hf), table(sn, hf, hd)
                r1 = dve.do(lambda e: e.tensor_tensor(a, x, c_all, ALU.mult), ready, ctok, ra.after)
                r2_ = dve.do(lambda e: e.tensor_tensor(bb[:, :, 0:hf], x[:, :, hf:hd], s_left, ALU.mult),
                             ready, rb.after)
                r3 = dve.do(lambda e: e.tensor_tensor(bb[:, :, hf:hd], x[:, :, 0:hf], s_right, ALU.mult),
                            ready, rb.after)
                return [r1, r2_, r3]
            qr = rotate(qb, qp, QW, 0)
            qb.free(*qr)
            kb = wring.take()
            kp = project(kb, QW, 2 * KW)
            yield
            kr = rotate(kb, kp, KW, QW)
            w_used[c] = kp
            sums = [pool.do(lambda e, ra=ra, rb=rb, tb=tb: e.tensor_tensor(
                tb.ap[:, 0:QW], ra.ap[:, 0:QW], rb.ap[:, 0:QW], ALU.add), qr, tb.after)]
            k_to = tb.ap[:, QW:QW + nk * P].rearrange("p (g r d) -> p g r d", g=nk, r=nk)
            k_a, k_b = (r.ap[:, QW:QW + KW].rearrange("p (g d) -> p g d", g=nk).unsqueeze(2)
                        .to_broadcast([P, nk, nk, hd]) for r in (ra, rb))
            sums.append(pool.do(lambda e, k_to=k_to, k_a=k_a, k_b=k_b: e.tensor_tensor(k_to, k_a, k_b, ALU.add),
                                kr, tb.after))
            ra.free(sums[-1])
            rb.free(sums[-1])
            rotated[t] = tb, sums
            yield
            vc = act.do(lambda e, t=t, kb=kb: e.activation(unit.v.ap[:, t, :], kb.ap[:, KW:2 * KW], ACT.Copy),
                        kr, unit.v.after)
            kb.free(vc, *kr)
            unit.v_tok.append(vc)
            yield

        def turned(unit, t, made_by):
            tb, sums = made_by
            tok = slice(t * P, (t + 1) * P)
            tq, q = wring.take(), q_st.take()
            for j in range(QW // P):
                qt = transpose(tq.ap[:, j * P:(j + 1) * P], tb.ap[:, j * P:(j + 1) * P], P, sums, tq.after,
                               signal=j == QW // P - 1)
            xq = tq.ap.rearrange("p (j n) -> p j n", j=QW // P)
            if wide:
                hs = [act.do(lambda e: e.activation(q.ap[:, 0:4, :], xq, ACT.Copy), qt, q.after)]
                yield
                ls = [dve.do(lambda e: e.tensor_tensor(q.ap[:, 4:8, :], xq, q.ap[:, 0:4, :].bitcast(F32),
                                                       ALU.subtract), hs, q.after)]
            else:
                qv = q.ap.rearrange("p (j s) n -> p j s n", s=2)
                halves = [xq[0:hd], xq[hd:P]]
                hs = [act.do(lambda e, s=s: e.activation(qv[0:hd, :, s, :], halves[s], ACT.Copy), qt, q.after)
                      for s in range(2)]
                yield
                ls = [dve.do(lambda e, s=s: e.tensor_tensor(
                    qv[hd:P, :, s, :], halves[s], qv[0:hd, :, s, :].bitcast(F32), ALU.subtract), hs, q.after)
                    for s in range(2)]
            made = hs + ls
            tq.free(*made)
            tk = wring.take()
            for g in range(nk):
                kt = transpose(tk.ap[:, g * P:(g + 1) * P], tb.ap[:, QW + g * P:QW + (g + 1) * P], P, sums,
                               tk.after, signal=g == nk - 1)
            tb.free(kt)
            xk = tk.ap[:, 0:nk * P].rearrange("p (g n) -> p g n", g=nk)
            h = act.do(lambda e: e.activation(unit.k.ap[:, 0, 0:nk, tok], xk, ACT.Copy, scale=scale),
                       kt, unit.k.after)
            yield
            l = dve.do(lambda e: e.scalar_tensor_tensor(
                unit.k.ap[:, 1, 0:nk, tok], xk, scale, unit.k.ap[:, 0, 0:nk, tok].bitcast(F32),
                ALU.mult, ALU.subtract), h, unit.k.after)
            tk.free(h, l)
            unit.q.append(q)
            unit.q_tok.append(made)
            unit.k_tok += [h, l]
            yield
            yield

        class Group:
            pass

        def group(c, b, unit, t, g):
            o = Group()
            o.c, o.b, o.u, o.t, o.g = c, b, unit, t, g
            o.k0 = max(0, t - 1) if wide else 0
            o.nkt = t + 1 - o.k0
            o.probs, o.exps = [], []
            o.sm = small.take()
            return o

        def scores(o, j):
            mm_w = max(o.nkt * P, 2 * P)
            keys = slice(o.k0 * P, o.k0 * P + mm_w)
            w = o.nkt * P
            bank, pr = sring.take(), prob.take()
            q, k = o.u.q[o.t].ap, o.u.k.ap
            khi, klo = k[:, 0, o.g, keys], k[:, 1, o.g, keys]
            if wide:
                pairs = three(q[:, j, :], q[:, 4 + j, :], khi, klo)
            else:
                head = o.g * KV + j
                pairs = [(q[:, head, :], khi), (q[:, head, :], klo)]
            for n_, (l, r) in enumerate(pairs):
                pe.do(lambda e, l=l, r=r, n_=n_: e.matmul(bank.ap[:, 0:mm_w], l, r, start=(n_ == 0), stop=False),
                      o.u.q_tok[o.t], o.u.k_tok[0:max(4, 2 * (o.t + 1))], bank.after, signal=False)
            mw = min(w, 2 * P) if wide else P
            done = pe.do(lambda e: e.matmul(bank.ap[:, w - mw:w], identb[:, :], mask[:, 2 * P - mw:2 * P],
                                            start=False, stop=True))
            sm = o.sm.ap
            mx = dve.do(lambda e: e.tensor_reduce(sm[:, 0, j:j + 1], bank.ap[:, 0:w], axis=AX.X, op=ALU.max,
                                                  negate=True), done, o.sm.after)
            o.probs.append(pr)
            o.score_tok = done
            waiting.append((o, j, w, bank, pr, mx))

        waiting = []

        def exponentials():
            for o, j, w, bank, pr, mx in waiting:
                sm = o.sm.ap
                ex = act.do(lambda e, sm=sm, j=j, w=w, bank=bank, pr=pr: e.activation(
                    pr.ap[:, 0:w], bank.ap[:, 0:w], ACT.Exp, bias=sm[:, 0, j:j + 1], accum_out=sm[:, 1, j:j + 1]),
                    mx, pr.after, o.sm.after)
                bank.free(mx, ex)
                o.exps.append(ex)
            waiting.clear()

        def normalise(o):
            w = o.nkt * P
            sm = o.sm.ap
            r = dve.do(lambda e: e.reciprocal(sm[:, 2, :], sm[:, 1, :]), o.exps)
            o.norms = [dve.do(lambda e, j=j: e.tensor_scalar(o.probs[j].ap[:, 0:w], o.probs[j].ap[:, 0:w],
                                                             sm[:, 2, j:j + 1], None, ALU.mult), r, o.exps[j])
                       for j in range(KV)]
            o.sm.free(*o.norms)
            o.prT, o.prT_tok = [], []

        def turn(o, kt):
            bank, dst = tring.take(), prT.take()
            for j in range(KV):
                tt = transpose(bank.ap[:, j * P:(j + 1) * P], o.probs[j].ap[:, kt * P:(kt + 1) * P], P,
                               o.norms[j], bank.after, signal=j == KV - 1)
            if kt == o.nkt - 1:
                for pr in o.probs:
                    pr.free(tt)
            cp = act.do(lambda e: e.activation(dst.ap, bank.ap, ACT.Copy), tt, dst.after)
            bank.free(cp)
            o.prT.append(dst)
            o.prT_tok.append(cp)

        def weigh(os):
            bank = wring.take()
            first = os[0]
            for kt in range(first.nkt):
                for o in os:
                    rows = slice(o.g * hd, (o.g + 1) * hd)
                    last = kt == first.nkt - 1 and o is os[-1]
                    tok = pe.do(lambda e, o=o, rows=rows, kt=kt: e.matmul(
                        bank.ap[rows, :], o.u.v.ap[:, o.k0 + kt, o.g * hd:(o.g + 1) * hd], o.prT[kt].ap,
                        start=kt == 0, stop=kt == o.nkt - 1),
                        o.prT_tok[kt], o.u.v_tok[0:o.t + 1], bank.after, signal=last)
            for o in os:
                for s in o.prT:
                    s.free(tok)
            hi, lo = oT_hi.take(), oT_lo.take()
            h = act.do(lambda e: e.activation(hi.ap, bank.ap, ACT.Copy), tok, hi.after)
            for o in os:
                if o.g == nk - 1 and o.t == T - 1:
                    o.u.v.free(tok)
            return first, bank, hi, lo, h

        def low_parts(w):
            o, bank, hi, lo, h = w
            l = dve.do(lambda e: e.tensor_tensor(lo.ap, bank.ap, hi.ap.bitcast(F32), ALU.subtract), h, lo.after)
            bank.free(h, l)
            return o, hi, lo, [h, l]

        def project_out(w):
            o, hi, lo, ready = w
            bank = wring.take()
            ohi = o_hi[:, o.c % 2, :].rearrange("p (j n) -> p j n", j=KV)
            olo = o_lo[:, o.c % 2, :].rearrange("p (j n) -> p j n", j=KV)
            pairs = []
            for j in range(KV):
                cols = slice(j * P, (j + 1) * P)
                pairs += three(hi.ap[:, cols], lo.ap[:, cols], ohi[:, j, :], olo[:, j, :])
            tok = product(bank.ap[:, 0:D], pairs, ready, o_ready[o.c], bank.after)
            hi.free(tok)
            lo.free(tok)
            o_used[o.c] = tok
            i = o.b * T + o.t
            add = dve.do(lambda e: e.tensor_tensor(res[:, i, :], bank.ap[:, 0:D], res[:, i, :], ALU.add),
                         tok, res_ready[i])
            bank.free(add)
            res_ready[i] = add

        units = [(c, b) for c in range(NU) for b in range(B)]
        normed = {b: norm_batch(b) for b in range(B)}
        made = Unit()
        for n_piece, _ in enumerate(prepare(0, 0, made)):
            if n_piece == 6:
                next(normed[1])
        prev = None
        settled = None
        pend, full = [], None
        for n_u, (c, b) in enumerate(units):
            unit = made
            made = Unit()
            nxt = units[n_u + 1] if n_u + 1 < len(units) else None
            if n_u == len(units) - 1:
                ahead()
            if b == 1 and c + 1 < NU:
                slot_qkv, slot_o = fetch_qkv(c + 1), fetch_o(c + 1)
            if b == 2 and c + 1 < NU:
                split_qkv(c + 1, slot_qkv)
                split_o(c + 1, slot_o)
            back = prepare(*nxt, made) if nxt else iter(())
            steps = [(t, g) for t in range(T) for g in range(nk)]
            pieces = 8 * T // (KV * len(steps))

            def beside():
                for _ in range(pieces):
                    next(back, None)
            for t, g in steps:
                if (t, g) == steps[-1] and c == 0 and b + 2 < B:
                    next(normed[b + 2])
                cur = group(c, b, unit, t, g)
                nturn = prev.nkt if prev else 0
                scores(cur, 0)
                weighed = weigh(full) if full else None
                if prev:
                    normalise(prev)
                beside()
                exponentials()
                if weighed:
                    weighed = low_parts(weighed)
                scores(cur, 1)
                if settled:
                    project_out(settled)
                    settled = None
                beside()
                for kt in range(0, min(2, nturn)):
                    turn(prev, kt)
                exponentials()
                scores(cur, 2)
                beside()
                if wide and weighed:
                    project_out(weighed)
                    weighed = None
                for kt in range(2, nturn):
                    turn(prev, kt)
                exponentials()
                scores(cur, 3)
                exponentials()
                beside()
                settled = weighed
                pend = pend + [prev] if prev else []
                full = None
                if prev and prev.g == nk - 1:
                    full, pend = pend, []
                if g == nk - 1:
                    unit.q[t].free(cur.score_tok)
                prev = cur
            unit.k.free(cur.score_tok)
            for _ in back:
                pass
        if settled:
            project_out(settled)
        if full:
            project_out(low_parts(weigh(full)))
        normalise(prev)
        for kt in range(prev.nkt):
            turn(prev, kt)
        project_out(low_parts(weigh(pend + [prev])))
        stack.close()

    def moe_phase(ph, ahead):
        stack = ExitStack()
        sb = allocator(stack, f"p{ph}", ("left", "right")[ph % 2])
        w1, w3, w2 = io["L0_ffn_w1"], io["L0_ffn_w3"], io["L0_ffn_w2"]

        def fetch_e(e_):
            def at(i):
                return lambda a: a[:, i * KC * H:(i + 1) * KC * H].rearrange("p (c n) -> p c n", c=KC)
            return fetch([(slice(0, P), at(i), chunks(w[e_])) for i, w in enumerate((w1, w3, w2))])

        slots = {0: fetch_e(0), 1: fetch_e(1)}
        yield
        fence = begin()
        hT_hi, hT_lo = (sb(f"hT_{s}", [P, B, KC, S], F32R) for s in ("hi", "lo"))
        w_hi, w_lo = (sb(f"w_{s}", [P, 2, 3 * KC * H], F32R) for s in ("hi", "lo"))
        xin = sb("xin", [P, NT, D])
        wg_raw = sb("wg", [P, KC, E])
        wg_hi, wg_lo = (sb(f"wg_{s}", [P, KC, E], F32R) for s in ("hi", "lo"))
        lnw = sb("lnw", [P, KC])
        sq = sb("sq", [P, D])
        ms, rs = sb("ms", [P, T]), sb("rs", [P, T])
        n_tile = Ring([sb(f"n_tile{i}", [P, D])[:, :] for i in range(4)])
        silu = Ring([sb(f"silu{i}", [P, S])[:, :] for i in range(3)])
        full = Ring([sb(f"full{i}", [P, S])[:, :] for i in range(3)])
        a_hi, a_lo = (Ring([sb(f"a_{s}{i}", [P, HC, S], F32R)[:, :, :] for i in range(2)]) for s in ("hi", "lo"))
        ext = sb("ext", [P, T, E + 4])
        rep = sb("rep", [P, T, E + 4])
        top8 = sb("top8", [P, T, 8])
        ex, sel, gate = sb("ex", [P, T, E]), sb("sel", [P, T, E]), sb("gate", [P, NT, E])
        gs = sb("gs", [P, 2, T])
        aring, yring = Ring([b[:, :] for b in banks[0:5]]), Ring([b[:, :] for b in banks[5:8]])

        cflag = Flag(sem(f"p{ph}_const"))
        cflag.dma(sp, wg_raw[:, :, :], chunks(io["L0_ffn_wg"]), fence)
        ctok = cflag.dma(sp, lnw[:, :], io["L0_ffn_ff_ln_w"].rearrange("(c p) -> p c", p=P), fence,
                             by_element=True)
        xflag = Flag(sem(f"p{ph}_x"))
        xtok = xflag.dma(sp, xin[:, :, :], res_saved.rearrange("t p d -> p t d"), fence, saved_tokens)
        wgh = act.do(lambda e: e.activation(wg_hi[:, :, :], wg_raw[:, :, :], ACT.Copy), ctok)
        wgl = dve.do(lambda e: e.tensor_tensor(wg_lo[:, :, :], wg_raw[:, :, :], wg_hi[:, :, :].bitcast(F32),
                                               ALU.subtract), wgh, ctok)
        sent = [dve.do(lambda e, k=k: e.memset(ext[:, :, E + k], SENT[k])) for k in range(4)]

        w_ready, w_used = {}, {}

        def split_e(e_, slot):
            w_ready[e_] = split(slot, 3 * KC * H, w_hi[:, e_ % 2, :], w_lo[:, e_ % 2, :], w_used.get(e_ - 2))

        hT_ready, gate_ready = {}, {}
        prior = {"sq": None, "ms": [], "small": []}

        def norm_batch(b):
            tiles = [b * T + t for t in range(T)]
            s = []
            for t, i in enumerate(tiles):
                q_ = act.do(lambda e, t=t, i=i: e.activation(sq[:, :], res[:, i, :], ACT.Square,
                                                             accum_out=ms[:, t:t + 1]),
                            res_ready[i], prior["sq"], *prior["ms"])
                prior["sq"] = q_
                s.append(q_)
            m = dve.do(lambda e: e.tensor_scalar(ms[:, :], ms[:, :], 1.0 / D, RMS_EPS, ALU.mult, ALU.add), s)
            r = pool.do(lambda e: e.tensor_tensor(rs[:, :], ms[:, :], half[:, 0:T], ALU.pow), m, *prior["ms"])
            srcs = []
            for t, i in enumerate(tiles):
                nt = n_tile.take()
                h = dve.do(lambda e, t=t, i=i, nt=nt: e.tensor_scalar(nt.ap, res[:, i, :], rs[:, t:t + 1], None,
                                                                     ALU.mult), r, nt.after)
                srcs.append((nt, h))
            prior["ms"] = [r, srcs[-1][1]]
            yield
            toks, reads = feature_major(lambda t: srcs[t][0].ap, [s_[1] for s_ in srcs], aring,
                                        hT_hi[:, b], hT_lo[:, b], lnw, ctok)
            for nt, _ in srcs:
                nt.free(*reads)
            hT_ready[b] = toks

        def route_batch(b):
            bank = aring.take()
            for t in range(T):
                cols = slice(t * P, (t + 1) * P)
                pairs = []
                for k in range(KC):
                    pairs += three(hT_hi[:, b, k, cols], hT_lo[:, b, k, cols], wg_hi[:, k, :], wg_lo[:, k, :])
                lg = product(bank.ap[:, t * E:(t + 1) * E], pairs, hT_ready[b], wgh, wgl, bank.after)
            prev_ = prior["small"]
            cp = dve.do(lambda e: e.tensor_copy(ext[:, :, 0:E], bank.ap[:, 0:T * E].rearrange("p (t e) -> p t e", t=T)),
                        lg, sent, *prev_)
            bank.free(cp)
            mx = [dve.do(lambda e, t=t: e.max(top8[:, t, :], ext[:, t, 0:E]), cp, *prev_) for t in range(T)]
            sub = dve.do(lambda e: e.tensor_tensor(ex[:, :, :], ext[:, :, 0:E],
                                                   top8[:, :, 0:1].to_broadcast([P, T, E]), ALU.subtract), mx)
            exp = act.do(lambda e: e.activation(ex[:, :, :], ex[:, :, :], ACT.Exp), sub)
            st = [dve.do(lambda e: e.tensor_copy(top8[:, :, 4:8], ext[:, :, E:E + 4]), mx, sent)]
            mr = [dve.do(lambda e, t=t: e.match_replace(rep[:, t, :], top8[:, t, :], ext[:, t, :], 3.0e38), st)
                  for t in range(T)]
            ne = dve.do(lambda e: e.tensor_tensor(sel[:, :, :], rep[:, :, 0:E], ext[:, :, 0:E], ALU.not_equal), mr)
            mu = dve.do(lambda e: e.tensor_tensor(ex[:, :, :], ex[:, :, :], sel[:, :, :], ALU.mult), ne, exp)
            sm = dve.do(lambda e: e.tensor_reduce(gs[:, 0, :], ex[:, :, :], axis=AX.X, op=ALU.add), mu)
            rc = dve.do(lambda e: e.reciprocal(gs[:, 1, :], gs[:, 0, :]), sm)
            g = dve.do(lambda e: e.tensor_tensor(gate[:, b * T:(b + 1) * T, :], ex[:, :, :],
                                                 gs[:, 1, :].unsqueeze(2).to_broadcast([P, T, E]), ALU.mult), rc)
            prior["small"] = [g]
            gate_ready[b] = g

        def up(e_, b):
            whi = w_hi[:, e_ % 2, :].rearrange("p (i k n) -> p i k n", i=3, k=KC)
            wlo = w_lo[:, e_ % 2, :].rearrange("p (i k n) -> p i k n", i=3, k=KC)
            hi, lo = a_hi.take(), a_lo.take()
            ready = []
            for m in range(HC):
                cols = slice(m * P, (m + 1) * P)
                got = []
                for i in range(2):
                    bank = aring.take()
                    pairs = []
                    for k in range(KC):
                        pairs += three(whi[:, i, k, cols], wlo[:, i, k, cols], hT_hi[:, b, k, :], hT_lo[:, b, k, :])
                    got.append((bank, product(bank.ap, pairs, hT_ready[b], w_ready[e_], bank.after)))
                (b1, t1), (b3, t3) = got
                s, f = silu.take(), full.take()
                sl = act.do(lambda e, s=s, b1=b1: e.activation(s.ap, b1.ap, ACT.Silu), t1, s.after)
                b1.free(sl)
                mu = dve.do(lambda e, s=s, f=f, b3=b3: e.tensor_tensor(f.ap, b3.ap, s.ap, ALU.mult), sl, t3, f.after)
                b3.free(mu)
                s.free(mu)
                h = act.do(lambda e, f=f, m=m: e.activation(hi.ap[:, m, :], f.ap, ACT.Copy), mu, hi.after)
                l = dve.do(lambda e, f=f, m=m: e.tensor_tensor(lo.ap[:, m, :], f.ap, hi.ap[:, m, :].bitcast(F32),
                                                               ALU.subtract), h, lo.after)
                f.free(h, l)
                ready += [h, l]
            return e_, b, hi, lo, ready

        def down(e_, b, hi, lo, ready):
            whi = w_hi[:, e_ % 2, :].rearrange("p (i k n) -> p i k n", i=3, k=KC)
            wlo = w_lo[:, e_ % 2, :].rearrange("p (i k n) -> p i k n", i=3, k=KC)
            for pair in range(0, T, 2):
                bank = yring.take()
                for t in (pair, pair + 1):
                    cols = slice(t * P, (t + 1) * P)
                    pairs = []
                    for m in range(HC):
                        pairs += three(hi.ap[:, m, cols], lo.ap[:, m, cols], whi[:, 2, m, :], wlo[:, 2, m, :])
                    tok = product(bank.ap[:, (t - pair) * D:(t - pair + 1) * D], pairs, ready, bank.after)
                for t in (pair, pair + 1):
                    i = b * T + t
                    y = bank.ap[:, (t - pair) * D:(t - pair + 1) * D]
                    add = dve.do(lambda e, y=y, i=i: e.scalar_tensor_tensor(
                        res[:, i, :], y, gate[:, i, e_:e_ + 1], res[:, i, :], ALU.mult, ALU.add),
                        tok, res_ready[i], gate_ready[b])
                    res_ready[i] = add
                    if e_ == E - 1:
                        res_ready[i] = dve.do(lambda e, i=i: e.scalar_tensor_tensor(
                            res[:, i, :], res[:, i, :], 0.5, xin[:, i, :], ALU.mult, ALU.add), add, xtok)
                bank.free(add)
            hi.free(tok)
            lo.free(tok)
            w_used[e_] = tok

        normed = [norm_batch(b) for b in range(B)]
        next(normed[0])
        split_e(0, slots[0])
        for _ in normed[0]:
            pass
        last = None
        for e_ in range(E):
            for b in range(B):
                if e_ == 0 and b + 1 < B:
                    next(normed[b + 1])
                if (e_, b) == (E - 2, 2):
                    ahead()
                cur = up(e_, b)
                if e_ == 0:
                    for _ in normed[b + 1] if b + 1 < B else ():
                        pass
                    route_batch(b)
                if last:
                    down(*last)
                last = cur
                if b == 0 and e_ + 1 < E:
                    split_e(e_ + 1, slots[e_ + 1])
                if b == 1 and e_ + 2 < E:
                    slots[e_ + 2] = fetch_e(e_ + 2)
        down(*last)
        stack.close()

    def small_attention_phase(ph, ahead):
        stack = ExitStack()
        sb = allocator(stack, f"p{ph}", ("left", "right")[ph % 2])
        fence = list(boundary)
        KD = SKV * SD
        ROWS = PARTS * PARTS * SD
        SCALE = 1.0 / float(np.sqrt(SD))
        PRE = "L0_attn_"
        WW = D + 2 * KD + D
        w_hi, w_lo = (sb(f"w_{s}", [P, KC, WW], F32R) for s in ("hi", "lo"))
        bq, bk = sb("bq", [P, D // P]), sb("bk", [KD, 1])
        bv, bo = sb("bv", [P, KD]), sb("bo", [P, D])
        q_st = [sb("q_st0", [P, SH, S], BF16)]
        k_st = [sb(f"k_st{i}", [P, SKV, S], BF16) for i in range(2)]
        fill = sb("fill", [PARTS, 2, S], BF16)
        VR = 32
        v_aug = Ring([sb(f"v_aug{i}", [P, T, SKV, VR])[:, :, :, :] for i in range(2)])
        def put(c0, cols):
            return lambda a: a[:, 0:KC * WW].rearrange("p (c n) -> p c n", c=KC)[:, :, c0:c0 + cols]
        slot = fetch([(slice(0, P), put(0, D), chunks(io[PRE + "Wq"])),
                      (slice(0, P), put(D, KD), chunks(io[PRE + "Wk"])),
                      (slice(0, P), put(D + KD, KD), chunks(io[PRE + "Wv"])),
                      (slice(0, P), put(D + 2 * KD, D), chunks(io[PRE + "Wo"]))])
        cflag = Flag(sem(f"p{ph}_const"))
        cflag.dma(sp, bq[:, :], io[PRE + "bq"].rearrange("(c p) -> p c", p=P), fence,
                             by_element=True)
        cflag.dma(sp, bk[:, :], io[PRE + "bk"].rearrange("(p a) -> p a", a=1), fence,
                  by_element=True)
        cflag.dma(sp, bv[:, :], io[PRE + "bv"].rearrange("(a n) -> a n", a=1).to_broadcast([P, KD]), fence)
        ctok = cflag.dma(sp, bo[:, :], io[PRE + "bo"].rearrange("(a n) -> a n", a=1).to_broadcast([P, D]), fence)
        w_ready = split(slot, KC * WW, w_hi[:, :, :].rearrange("p c n -> p (c n)"),
                        w_lo[:, :, :].rearrange("p c n -> p (c n)"))
        zero = [pool.do(lambda e, m=m: e.memset(m[64:P, :, :], 0.0)) for m in (*q_st, *k_st)]
        filled = [pool.do(lambda e, i=i: e.memset(fill[:, i, :], float(i))) for i in range(2)]
        oflag = Flag(sem(f"p{ph}_ones"))
        for m in k_st:
            one_rows = oflag.dma(sp, m[ROWS:ROWS + PARTS, :, :],
                                 fill[:, 1:2, :].to_broadcast([PARTS, SKV, S]), zero, filled)
        va = []
        for s in v_aug.slots:
            z = pool.do(lambda e, s=s: e.memset(s.ap, 0.0))
            va.append(pool.do(lambda e, s=s: e.memset(s.ap[:, :, :, SD], 1.0), z))

        yield
        begin()

        uT_hi, uT_lo = (Ring([sb(f"uT_{s}{i}", [P, KC, S], F32R)[:, :, :] for i in range(1)]) for s in ("hi", "lo"))
        q32, r32 = Ring([sb(f"q32_{i}", [P, S])[:, :] for i in range(2)]), sb("r32", [P, S])
        qp = Ring([sb(f"qp{i}", [P, PARTS, S], BF16)[:, :, :] for i in range(2)],
                  [Flag(sem(f"p{ph}_save{i}")) for i in range(2)])
        q_st.append(sb("q_st1", [P, SH, S], BF16))
        nmax = sb("nmax", [P, 2, T, 8])
        nm_p = [sb(f"nm_p{i}", [8, PARTS, S], BF16) for i in range(2)]
        nm_r = sb("nm_r", [8, S])
        prT = Ring([sb(f"prT{i}", [P, S])[:, :] for i in range(12)])
        o_sb = Ring([sb(f"o_sb{i}", [P, S])[:, :] for i in range(2)])
        rsum = Ring([sb(f"rsum{i}", [P, T, KV])[:, :, :] for i in range(2)])
        o_tm = Ring([sb(f"o_tm{i}", [P, T, D])[:, :, :] for i in range(2)])
        oT_hi, oT_lo = (Ring([sb(f"oT_{s}{i}", [P, KC, S], F32R)[:, :, :] for i in range(1)]) for s in ("hi", "lo"))
        norm = Norm(sb, "ln")
        n_tile = Ring([sb(f"n_tile{i}", [P, D])[:, :] for i in range(4)])
        sring, tring = Ring([b[:, :] for b in banks[0:3]]), Ring([b[:, :] for b in banks[3:5]])
        oring, wring = Ring([b[:, :] for b in banks[5:6]]), Ring([b[:, :] for b in banks[6:8]])

        qk_flag, nm_flag = ([Flag(sem(f"p{ph}_{n}{i}")) for i in range(2)] for n in ("qk", "nm"))
        prior = {"r32": [], "nmax": [[], []], "nm_p": [[], []], "nm_r": []}
        stack_ready, stack_read, v_aug_of, v_ready, o_tm_of, o_toks, nm_done = {}, {}, {}, {}, {}, {}, {}

        def cols(c0, n_):
            return slice(c0, c0 + n_)

        def prelude(b):
            tiles = [b * T + t for t in range(T)]
            ready = [[res_ready[i]] for i in tiles]
            rs = norm.run([res[:, i, :] for i in tiles], LN_EPS, ready)
            yield
            srcs = []
            for t, i in enumerate(tiles):
                nt = n_tile.take()
                h = dve.do(lambda e, t=t, i=i, nt=nt: e.tensor_scalar(
                    nt.ap, res[:, i, :], norm.mv[:, t, 0:1], norm.rs[:, t:t + 1], ALU.subtract, ALU.mult),
                    rs, ready[t], nt.after)
                srcs.append((nt, h))
                if t % 2:
                    yield
            norm.read = [srcs[-1][1]]
            uh, ul = uT_hi.take(), uT_lo.take()
            u_ready, reads = yield from feature_major_steps(
                lambda t: srcs[t][0].ap, [s[1] for s in srcs], wring, uh.ap, ul.ap, None, uh.after, ul.after)
            for nt, _ in srcs:
                nt.free(*reads)
            saved = []
            for c0, width, bias, dst, sc in ((D, KD, bk[:, 0:1], D, 1.0), (0, P, bq[:, 0:1], 0, SCALE),
                                             (P, P, bq[:, 1:2], P, SCALE)):
                bank, q_, pp = wring.take(), q32.take(), qp.take()
                pairs = []
                for k in range(KC):
                    pairs += three(w_hi[:, k, cols(c0, width)], w_lo[:, k, cols(c0, width)], uh.ap[:, k, :], ul.ap[:, k, :])
                mm = product(bank.ap[0:width, :], pairs, u_ready, w_ready, bank.after)
                r = slice(0, width)
                a0 = dve.do(lambda e, q_=q_, bank=bank, r=r, bias=bias, sc=sc: e.tensor_scalar(
                    q_.ap[r, :], bank.ap[r, :], bias, sc, ALU.add, ALU.mult), mm, ctok, q_.after)
                bank.free(a0)
                yield
                a1 = act.do(lambda e, q_=q_, pp=pp, r=r: e.activation(pp.ap[r, 0, :], q_.ap[r, :], ACT.Copy), a0, pp.after)
                a2 = dve.do(lambda e, q_=q_, pp=pp, r=r: e.tensor_tensor(r32[r, :], q_.ap[r, :], pp.ap[r, 0, :],
                                                                        ALU.subtract), a1, *prior["r32"])
                yield
                a3 = act.do(lambda e, pp=pp, r=r: e.activation(pp.ap[r, 1, :], r32[r, :], ACT.Copy), a2, pp.after)
                a4 = dve.do(lambda e, pp=pp, r=r: e.tensor_tensor(pp.ap[r, 2, :], r32[r, :], pp.ap[r, 1, :],
                                                                 ALU.subtract), a3)
                prior["r32"] = [a4]
                q_.free(a1, a2)
                sv = pp.flag.dma(sp, parts_saved[b % 2, :, dst:dst + width, :].rearrange("m r n -> r m n"),
                                 pp.ap[r, :, :], a4, a1, a3, stack_ready.get(b - 2))
                pp.free(sv)
                saved.append(sv)
                yield
            qs, ks, flag = q_st[b % 2], k_st[b % 2], qk_flag[b % 2]
            free = stack_read.get(b - 2)
            flag.dma(sp, qs[ROWS:ROWS + PARTS, :, :], fill[:, 0:1, :].to_broadcast([PARTS, SH, S]), zero, filled, free)
            for a in range(PARTS):
                for m in range(PARTS):
                    rows = slice((a * PARTS + m) * SD, (a * PARTS + m + 1) * SD)
                    flag.dma(sp, ks[rows, :, :], parts_saved[b % 2, m, D:D + KD, :].rearrange(
                        "(g d) n -> d g n", d=SD), saved, zero, free)
                    stack_ready[b] = flag.dma(sp, qs[rows, :, :], parts_saved[b % 2, a, 0:D, :].rearrange(
                        "(h d) n -> d h n", d=SD), saved, zero, free)
            va_s = v_aug.take()
            bank = wring.take()
            for t in range(T):
                tk = slice(t * P, (t + 1) * P)
                pairs = []
                for k in range(KC):
                    pairs += three(uh.ap[:, k, tk], ul.ap[:, k, tk], w_hi[:, k, cols(D + KD, KD)], w_lo[:, k, cols(D + KD, KD)])
                mm = product(bank.ap[:, t * KD:(t + 1) * KD], pairs, bank.after)
                if t % 2 and t < T - 1:
                    yield
            v_ready[b] = [dve.do(lambda e, t=t, bank=bank, va_s=va_s: e.tensor_tensor(
                va_s.ap[:, t, :, 0:SD], bank.ap[:, t * KD:(t + 1) * KD].rearrange("p (g d) -> p g d", g=SKV),
                bv[:, :].rearrange("p (g d) -> p g d", g=SKV), ALU.add), mm, va, va_s.after) for t in range(T)]
            bank.free(*v_ready[b])
            v_aug_of[b] = va_s
            uh.free(mm)
            ul.free(mm)

        def maxima(b, qt):
            s = qt % 2
            qs, ks = q_st[b % 2], k_st[b % 2]
            for hh in range(8):
                head = qt * 8 + hh
                for t in range(T):
                    bk_ = sring.take()
                    mm = product(bk_.ap, [(qs[:, head, t * P:(t + 1) * P], ks[:, head // KV, :])],
                                 stack_ready[b], one_rows, bk_.after)
                    mx = dve.do(lambda e, t=t, hh=hh, bk_=bk_: e.tensor_reduce(
                        nmax[:, s, t, hh:hh + 1], bk_.ap, axis=AX.X, op=ALU.max, negate=True), mm, *prior["nmax"][s])
                    bk_.free(mx)
                    yield
            return lambda: store_maxima(b, qt, mx, mm)

        def store_maxima(b, qt, mx, mm):
            s, qs = qt % 2, q_st[b % 2]
            wb = wring.take()
            for t in range(T):
                tt = transpose(wb.ap[0:8, t * P:(t + 1) * P], nmax[:, s, t, :], P, mx, wb.after, signal=t == T - 1)
            prior["nmax"][s] = [tt]
            np_ = nm_p[s]
            a1 = act.do(lambda e: e.activation(np_[:, 0, :], wb.ap[0:8, :], ACT.Copy), tt, *prior["nm_p"][s])
            a2 = dve.do(lambda e: e.tensor_tensor(nm_r[:, :], wb.ap[0:8, :], np_[:, 0, :], ALU.subtract), a1,
                        *prior["nm_r"])
            wb.free(a1, a2)
            a3 = act.do(lambda e: e.activation(np_[:, 1, :], nm_r[:, :], ACT.Copy), a2)
            a4 = dve.do(lambda e: e.tensor_tensor(np_[:, 2, :], nm_r[:, :], np_[:, 1, :], ALU.subtract), a3)
            prior["nm_r"] = [a4]
            for m in range(PARTS):
                done = nm_flag[s].dma(pool, qs[ROWS + m:ROWS + m + 1, qt * 8:(qt + 1) * 8, :],
                                      np_[:, m, :], a1, a3, a4, mm)
            prior["nm_p"][s] = [done]
            nm_done[b, qt] = done

        def peaks_of_all():
            store = None
            for b in range(B):
                for qt in range(4):
                    steps = maxima(b, qt)
                    if store:
                        for _ in range(3):
                            next(steps)
                            yield
                        store()
                    store = yield from steps
            store()
            yield

        def attend(b, qt):
            if qt == 0:
                o_tm_of[b], o_toks[b] = o_tm.take(), []
            otm, va_s, qs, ks = o_tm_of[b], v_aug_of[b], q_st[b % 2], k_st[b % 2]
            late = []

            def value(kv, kt, exps, ob):
                for j, (pt, ex) in enumerate(exps):
                    av = pe.do(lambda e, j=j, pt=pt: e.matmul(
                        ob.ap[VR * j:VR * (j + 1), :], va_s.ap[:, kt, kv, :], pt.ap,
                        start=kt == 0, stop=kt == T - 1), ex, v_ready[b], ob.after, signal=j == KV - 1)
                for pt, _ in exps:
                    pt.free(av)
                if kt == T - 1:
                    os_ = o_sb.take()
                    c1 = act.do(lambda e: e.activation(os_.ap, ob.ap, ACT.Copy), av, os_.after)
                    ob.free(c1)
                    if kv % 2 and qt == 3:
                        stack_read[b] = av
                        va_s.free(av)
                    later.append([3, lambda: finish(kv, os_, c1)])

            def finish(kv, os_, c1):
                wb = wring.take()
                for t in range(T):
                    tt = transpose(wb.ap[:, t * P:(t + 1) * P], os_.ap[:, t * P:(t + 1) * P], P, c1, wb.after,
                                   signal=t == T - 1)
                os_.free(tt)
                rr = rsum.take()
                view = wb.ap.rearrange("p (t j r) -> p t j r", t=T, j=KV)
                rc = dve.do(lambda e: e.reciprocal(rr.ap, view[:, :, :, SD]), tt, rr.after)
                dst = otm.ap[:, :, kv * KV * SD:(kv + 1) * KV * SD].rearrange("p t (j d) -> p t j d", j=KV)
                mu = [dve.do(lambda e, t=t: e.tensor_tensor(
                    dst[:, t], view[:, t, :, 0:SD], rr.ap[:, t, :].unsqueeze(2).to_broadcast([P, KV, SD]),
                    ALU.mult), rc, otm.after) for t in range(T)]
                wb.free(*mu)
                rr.free(mu[-1])
                o_toks[b].append(mu[-1])

            for g in range(2):
                kv = qt * 2 + g
                obs = [None]
                for kt in range(T):
                    exps = []
                    for j in range(KV):
                        head = kv * KV + j
                        tb, pt = tring.take(), prT.take()
                        mm = product(tb.ap, [(ks[:, kv, kt * P:(kt + 1) * P], qs[:, head, :])],
                                     nm_done[b, qt], tb.after)
                        ex = act.do(lambda e, tb=tb, pt=pt: e.activation(pt.ap, tb.ap, ACT.Exp), mm, pt.after)
                        tb.free(ex)
                        exps.append((pt, ex))
                        if j == KV - 1:
                            later.append([2, lambda kv=kv, kt=kt, exps=exps, obs=obs: value(
                                kv, kt, exps, first_bank(obs))])
                        tick()
                        yield

        later = []

        def first_bank(obs):
            if obs[0] is None:
                obs[0] = oring.take()
            return obs[0]

        def tick():
            for item in list(later):
                item[0] -= 1
                if item[0] < 0:
                    later.remove(item)
                    item[1]()

        def tail(b):
            oh, ol = oT_hi.take(), oT_lo.take()
            otm = o_tm_of[b]
            o_ready, reads = yield from feature_major_steps(lambda t: otm.ap[:, t, :], [o_toks[b]] * T, wring,
                                                            oh.ap, ol.ap, None, oh.after, ol.after)
            otm.free(*reads)
            for t in range(T):
                i = b * T + t
                bank = wring.take()
                tk = slice(t * P, (t + 1) * P)
                pairs = []
                for k in range(KC):
                    pairs += three(oh.ap[:, k, tk], ol.ap[:, k, tk], w_hi[:, k, cols(D + 2 * KD, D)],
                                   w_lo[:, k, cols(D + 2 * KD, D)])
                mm = product(bank.ap[:, 0:D], pairs, o_ready, bank.after)
                a1 = dve.do(lambda e, i=i, bank=bank: e.tensor_tensor(res[:, i, :], bank.ap[:, 0:D], res[:, i, :],
                                                                      ALU.add), mm, res_ready[i])
                bank.free(a1)
                res_ready[i] = pool.do(lambda e, i=i: e.tensor_tensor(res[:, i, :], res[:, i, :], bo[:, :], ALU.add),
                                       a1, ctok)
                yield
            oh.free(mm)
            ol.free(mm)

        LEAD = 52
        for _ in prelude(0):
            pass
        zero.append(pool.do(lambda e: e.memset(q_st[1][64:P, :, :], 0.0)))
        peaks = peaks_of_all()
        for _ in range(LEAD):
            next(peaks, None)
        for b in range(B):
            def beside():
                for _ in range(6):
                    yield
                if b:
                    yield from tail(b - 1)
                if b + 1 < B:
                    yield from prelude(b + 1)
            side = beside()
            n_step = 0
            if b == B - 1:
                ahead()
            for qt in range(4):
                for _ in attend(b, qt):
                    next(peaks, None)
                    if n_step % 2 == 0:
                        next(side, None)
                    n_step += 1
            for _ in side:
                pass
        while later:
            tick()
        for _ in tail(B - 1):
            pass
        stack.close()

    def thought_phase(ph, final, roomy, ahead):
        stack = ExitStack()
        sb = allocator(stack, f"p{ph}", ("left", "right")[ph % 2])
        PRE = "L1_ffn_"
        HH = 1024
        HN = HH // P
        slot = fetch([(slice(0, P), lambda a: a[:, 0:KC * D].rearrange("p (c n) -> p c n", c=KC),
                       chunks(io[PRE + "gate_w"]))])
        if not roomy:
            yield
        fence = list(boundary) if roomy else begin()

        gw_hi, gw_lo = (sb(f"gw_{s}", [P, KC * D], F32R) for s in ("hi", "lo"))
        agg, bc = sb("agg", [P, KC, D]), sb("bc", [P, KC, D])
        d1, d2 = sb("d1", [P, KC, HH]), sb("d2", [P, HN, D])
        d1b = sb("d1b", [P, HN])
        gb, og, ob_ = sb("gb", [P, D]), sb("og", [P, D]), sb("ob", [P, D])
        rows = {k: sb("r_" + k, [B, D]) for k in ("in_gamma", "in_beta", "agg_b", "pn_gamma", "pn_beta", "d2_b", "bc_b")}
        sel = sb("sel", [B, B, P])

        def row(flag, k):
            return flag.dma(sp, rows[k][:, :], io[PRE + k].rearrange("(a n) -> a n", a=1).to_broadcast([B, D]), fence)
        first_flag, cflag = Flag(sem(f"p{ph}_first")), Flag(sem(f"p{ph}_const"))
        for k in ("in_gamma", "in_beta", "agg_b"):
            row(first_flag, k)
        first_tok = first_flag.dma(sp, agg[:, :, :], chunks(io[PRE + "agg_w"]), fence)
        for k in ("pn_gamma", "pn_beta", "d2_b", "bc_b"):
            row(cflag, k)
        cflag.dma(sp, d1[:, :, :], chunks(io[PRE + "d1_w"]), fence)
        cflag.dma(sp, d1b[:, :], io[PRE + "d1_b"].rearrange("(c p) -> p c", p=P), fence, by_element=True)
        cflag.dma(sp, d2[:, :, :], chunks(io[PRE + "d2_w"]), fence)
        for m, k in ((gb, "gate_b"), (og, "out_gamma"), (ob_, "out_beta")):
            cflag.dma(sp, m[:, :], io[PRE + k].rearrange("(a n) -> a n", a=1).to_broadcast([P, D]), fence)
        ctok = cflag.dma(sp, bc[:, :, :], chunks(io[PRE + "bc_w"]), fence)
        z = pool.do(lambda e: e.memset(sel[:, :, :], 0.0))
        sel_ready = pool.do(lambda e: e.affine_select(out=sel[:, :, :], in_=sel[:, :, :], compare_op=ALU.not_equal,
                                                      fill=1.0, base=0, pattern=[[-1, B], [0, P]],
                                                      channel_multiplier=1), z)
        if roomy:
            gw_ready = split(slot, KC * D, gw_hi[:, :], gw_lo[:, :])
            yield
            begin()

        u = sb("u", [P, NT, D])
        gt = sb("gate", [P, NT, D])
        uT_hi, uT_lo = (Ring([sb(f"uT_{s}{i}", [P, KC, S], F32R)[:, :, :] for i in range(2)]) for s in ("hi", "lo"))
        last = sb("last", [B, D])
        th, nrm = sb("thought", [B, D]), sb("nrm", [B, D])
        tT = sb("tT", [P, KC, B])
        hid, hid2 = sb("hid", [P, HN, B]), sb("hid2", [P, HN, B])
        bc4 = sb("bc4", [B, D])
        bcast = sb("bcast", [P, B, D])
        norm_last, norm, nrm4 = Norm(sb, "ll", tiles=B), Norm(sb, "ln", tiles=T - 1), Norm(sb, "l4", parts=B, tiles=1)
        norm_out = [Norm(sb, f"lo{i}") for i in range(2)]
        wring, cring = Ring([b[:, :] for b in banks[0:6]]), Ring([b[:, :] for b in banks[6:8]])

        u_ready = {}
        uflag = Flag(sem(f"p{ph}_last"))

        def layer_norm(stats, tiles):
            rs = stats.run([res[:, i, :] for i in tiles], LN_EPS, [[res_ready[i]] for i in tiles])
            for n, i in enumerate(tiles):
                u_ready[i] = dve.do(lambda e, n=n, i=i: e.tensor_scalar(
                    u[:, i, :], res[:, i, :], stats.mv[:, n, 0:1], stats.rs[:, n:n + 1], ALU.subtract, ALU.mult),
                    rs, res_ready[i])
            stats.read = [u_ready[tiles[-1]]]

        ends = [b * T + T - 1 for b in range(B)]
        layer_norm(norm_last, ends)
        lt = uflag.dma(sp, last[:, :], u[P - 1:P, T - 1:NT:T, :], [u_ready[i] for i in ends])

        g_ready = {}

        def gates(b):
            layer_norm(norm, [b * T + t for t in range(T - 1)])
            yield
            hi, lo = uT_hi.take(), uT_lo.take()
            ready, _ = yield from feature_major_steps(
                lambda t: u[:, b * T + t, :], [u_ready[b * T + t] for t in range(T)], wring,
                hi.ap, lo.ap, None, hi.after, lo.after)
            ghi = gw_hi[:, :].rearrange("p (k n) -> p k n", k=KC)
            glo = gw_lo[:, :].rearrange("p (k n) -> p k n", k=KC)
            for t in range(T):
                bank = wring.take()
                tk = slice(t * P, (t + 1) * P)
                pairs = []
                for k in range(KC):
                    pairs += three(hi.ap[:, k, tk], lo.ap[:, k, tk], ghi[:, k, :], glo[:, k, :])
                mm = product(bank.ap[:, 0:D], pairs, ready, gw_ready, bank.after)
                g = dve.do(lambda e, i=b * T + t, bank=bank: e.tensor_tensor(gt[:, i, :], bank.ap[:, 0:D], gb[:, :],
                                                                             ALU.add), mm, ctok)
                bank.free(g)
                g_ready[b * T + t] = g
                if t < T - 1:
                    yield
            hi.free(mm)
            lo.free(mm)
            for i in range(b * T, (b + 1) * T):
                res_ready[i] = pool.do(lambda e, i=i: e.tensor_tensor(res[:, i, :], res[:, i, :], ob_[:, :], ALU.add),
                                       ob_h, u_ready[i])
            yield

        def all_gates():
            for b in range(B):
                yield from gates(b)
        back = all_gates()

        def beside(n):
            for _ in range(n):
                next(back, None)

        def ln4(dst, src, ready, gamma, beta, tok):
            rs = nrm4.run([src], FFN_EPS, [ready])
            a = dve.do(lambda e: e.scalar_tensor_tensor(dst, src, nrm4.mv[:, 0, 0:1], gamma[:, :],
                                                        ALU.subtract, ALU.mult), tok, nrm4.read)
            m = dve.do(lambda e: e.scalar_tensor_tensor(dst, dst, nrm4.rs[:, 0:1], beta[:, :],
                                                        ALU.mult, ALU.add), rs, a)
            nrm4.read = [m]
            return m

        prior = {"tT": [], "hid": [], "hid2": []}

        def columns(src, ready):
            bank = cring.take()
            for k in range(KC):
                tt = transpose(bank.ap[:, k * B:(k + 1) * B], src[:, k * P:(k + 1) * P], B, ready, bank.after,
                               signal=k == KC - 1)
            c = act.do(lambda e: e.activation(tT[:, :, :], bank.ap[:, 0:KC * B].rearrange("p (k b) -> p k b", k=KC),
                                              ACT.Copy), tt, *prior["tT"])
            bank.free(c)
            return c

        def linear(w, ready, tok):
            bank = cring.take()
            mm = product(bank.ap[0:B, 0:D], [(tT[:, k, :], w[:, k, :]) for k in range(KC)], ready, tok, bank.after)
            prior["tT"] = [mm]
            return bank, mm

        if not roomy:
            gw_ready = split(slot, KC * D, gw_hi[:, :], gw_lo[:, :])
        beside(1)
        n0 = ln4(nrm[:, :], last[:, :], lt, rows["in_gamma"], rows["in_beta"], first_tok)
        beside(2)
        bank, mm = linear(agg, columns(nrm, n0), first_tok)
        thr = dve.do(lambda e, bank=bank: e.tensor_tensor(th[:, :], bank.ap[0:B, 0:D], rows["agg_b"][:, :], ALU.add), mm)
        bank.free(thr)
        og_h = dve.do(lambda e: e.tensor_scalar(og[:, :], og[:, :], 0.5, None, ALU.mult), ctok)
        ob_h = dve.do(lambda e: e.tensor_scalar(ob_[:, :], ob_[:, :], 0.5, None, ALU.mult), ctok)
        for step in range(4):
            n1 = ln4(nrm[:, :], th[:, :], thr, rows["pn_gamma"], rows["pn_beta"], ctok)
            thr = dve.do(lambda e: e.tensor_tensor(th[:, :], th[:, :], rows["d2_b"][:, :], ALU.add), n1)
            beside(BESIDE[0])
            c1 = columns(nrm, n1)
            bank = cring.take()
            for h_ in range(HN):
                mm = product(bank.ap[:, h_ * B:(h_ + 1) * B],
                             [(d1[:, k, h_ * P:(h_ + 1) * P], tT[:, k, :]) for k in range(KC)], c1, ctok, bank.after)
            prior["tT"] = [mm]
            a1 = dve.do(lambda e, bank=bank: e.tensor_tensor(
                hid[:, :, :], bank.ap[:, 0:HN * B].rearrange("p (h b) -> p h b", h=HN),
                d1b[:, :].unsqueeze(2).to_broadcast([P, HN, B]), ALU.add), mm, *prior["hid"])
            bank.free(a1)
            a2 = act.do(lambda e: e.activation(hid2[:, :, :], hid[:, :, :], ACT.Gelu), a1, *prior["hid2"])
            prior["hid"] = [a2]
            if step == 0:
                ahead()
            beside(BESIDE[1])
            bank = cring.take()
            mm = product(bank.ap[0:B, 0:D], [(hid2[:, h_, :], d2[:, h_, :]) for h_ in range(HN)], a2, bank.after)
            prior["hid2"] = [mm]
            thr = dve.do(lambda e, bank=bank: e.tensor_tensor(th[:, :], bank.ap[0:B, 0:D], th[:, :], ALU.add), mm, thr)
            bank.free(thr)
        for _ in back:
            pass
        gated = [act.do(lambda e, i=i: e.activation(gt[:, i, :], gt[:, i, :], ACT.Sigmoid), g_ready[i])
                 for i in range(NT)]
        bank, mm = linear(bc, columns(th, thr), ctok)
        b4 = dve.do(lambda e, bank=bank: e.tensor_tensor(bc4[:, :], bank.ap[0:B, 0:D], rows["bc_b"][:, :], ALU.add), mm)
        bank.free(b4)
        b_ready = []
        for b in range(B):
            bank = cring.take()
            mm = product(bank.ap[:, 0:D], [(sel[:, b, :], bc4[:, :])], b4, sel_ready, bank.after)
            c = act.do(lambda e, b=b, bank=bank: e.activation(bcast[:, b, :], bank.ap[:, 0:D], ACT.Copy), mm)
            bank.free(c)
            b_ready.append(c)

        oflag = Flag(sem(f"p{ph}_out"))
        weighted, out_rs = {}, {}

        def weight(b):
            for i in range(b * T, (b + 1) * T):
                weighted[i] = pool.do(lambda e, i=i: e.tensor_tensor(gt[:, i, :], gt[:, i, :], bcast[:, b, :], ALU.mult),
                                      gated[i], b_ready[b])

        def statistics(b):
            tiles = range(b * T, (b + 1) * T)
            ready = [[dve.do(lambda e, i=i: e.tensor_tensor(u[:, i, :], u[:, i, :], gt[:, i, :], ALU.add),
                                            weighted[i])] for i in tiles]
            out_rs[b] = norm_out[b % 2].run([u[:, i, :] for i in tiles], FFN_EPS, ready)

        weight(0)
        weight(1)
        statistics(0)
        for b in range(B):
            if b + 2 < B:
                weight(b + 2)
            if b + 1 < B:
                statistics(b + 1)
            nm = norm_out[b % 2]
            scaled = [dve.do(lambda e, b=b, t=t, nm=nm: e.scalar_tensor_tensor(
                u[:, b * T + t, :], u[:, b * T + t, :], nm.mv[:, t, 0:1], og[:, :], ALU.subtract, ALU.mult),
                out_rs[b], og_h) for t in range(T)]
            for t in range(T):
                i = b * T + t
                res_ready[i] = dve.do(lambda e, t=t, i=i, nm=nm: e.scalar_tensor_tensor(
                    res[:, i, :], u[:, i, :], nm.rs[:, t:t + 1], res[:, i, :], ALU.mult, ALU.add), scaled[t], res_ready[i])
            nm.read = [res_ready[b * T + T - 1]]
            if final:
                otok = oflag.dma(sp, out[b].rearrange("(t p) d -> p t d", p=P), res[:, b * T:(b + 1) * T, :],
                                 [res_ready[i] for i in range(b * T, (b + 1) * T)])
        if final:
            sp.fence(otok)
        stack.close()

    saved_tokens = []

    def ahead_of(ph):
        return lambda: next(runs[ph + 1]) if ph + 1 < len(runs) else None
    runs = [attention_phase(0, False, True, ahead_of(0)), moe_phase(1, ahead_of(1)),
            small_attention_phase(2, ahead_of(2)),
            attention_phase(3, False, False, ahead_of(3)), moe_phase(4, ahead_of(4)),
            thought_phase(5, False, True, ahead_of(5)), attention_phase(6, True, True, ahead_of(6)),
            thought_phase(7, True, False, ahead_of(7))]
    load(0)
    next(runs[0])
    for b in range(1, B):
        load(b)
    for run in runs:
        for _ in run:
            pass

    with nc.Block() as block:
        block.sync(sp.play)
        block.gpsimd(pool.play)
        block.vector(dve.play)
        block.scalar(act.play)
        block.tensor(pe.play)
    ctx.close()


def _rope_tables():
    f = np.float32
    pos = np.arange(S, dtype=f)[:, None]
    inv0 = f(1.0) / (f(150000.0) ** (np.arange(32, dtype=f) / f(32)))
    a0 = pos * inv0
    a0 = np.concatenate([a0, a0], -1)
    scale1 = f(10000.0) ** (np.arange(0, 128, 2, dtype=f) / f(128))
    a1 = pos / scale1[None, :]
    a1 = np.concatenate([a1, a1], -1)

    def signed(s):
        h = s.shape[1] // 2
        return np.concatenate([-s[:, :h], s[:, h:]], -1)
    return {"rope0_cos": np.cos(a0), "rope0_sin": signed(np.sin(a0)),
            "rope1_cos": np.cos(a1), "rope1_sin": signed(np.sin(a1))}


def kernel(**inputs):
    import concourse.bacc as bacc
    from concourse.bass_utils import run_bass_kernel_spmd

    nc = bacc.Bacc("TRN2", target_bir_lowering=False, num_devices=1)
    arrays, io = {}, {}
    for name, value in {**inputs, **_rope_tables()}.items():
        a = np.ascontiguousarray(value)
        arrays[f"in_{name}"] = a
        io[name] = nc.dram_tensor(f"in_{name}", a.shape, mybir.dt.from_np(a.dtype), kind="ExternalInput").ap()
    out = nc.dram_tensor("out", (B, S, D), mybir.dt.float32, kind="ExternalOutput").ap()
    build(nc, io, out)
    r = run_bass_kernel_spmd(nc, [arrays], core_ids=[0])
    return r.results[0]["out"]
```
